# Optimizing a Trainium2 kernel written in Bass

```python
import numpy as np
import jax
import jax.numpy as jnp

def _softmax(x, axis=-1):
    return jax.nn.softmax(x, axis=axis)

def _gelu(x):
    return jax.nn.gelu(x, approximate=True)

def _silu(x):
    return jax.nn.silu(x)

def _sigmoid(x):
    return jax.nn.sigmoid(x)

def _layernorm(x, axis=-1, eps=1e-05):
    m = jnp.mean(x, axis=axis, keepdims=True)
    v = jnp.var(x, axis=axis, keepdims=True)
    return (x - m) / jnp.sqrt(v + eps)

def _scatter_add(tgt, idx, src, axis=0):
    return tgt.at[idx].add(src)

def _segment_sum(src, seg, n):
    return jax.ops.segment_sum(src, seg, n)
kernel_name = 'mk_perceiver_d1_seqx_r8_88a35f'

def setup_inputs(seed: int=0):
    np.random.seed(seed)
    _w = jnp.asarray

    def _rec_inputs():
        import jax
        import jax.numpy as jnp
        _rk = jax.random.key(seed)
        x = -0.0003929 + 0.9999 * jax.random.normal(jax.random.fold_in(_rk, 1), (16, 64, 256), jnp.float32)
        _lenS = 64 - jax.random.randint(jax.random.fold_in(_rk, 7), (16,), 0, max(1, 64 // 4) + 1, jnp.int32)
        _lenS2 = 128 - jax.random.randint(jax.random.fold_in(_rk, 8), (16,), 0, max(1, 128 // 4) + 1, jnp.int32)
        _ctx_2048P = jax.random.normal(jax.random.fold_in(_rk, 11), (16, 16, 256), jnp.float32)
        _ctx_2048c = jax.random.dirichlet(jax.random.fold_in(_rk, 511), 0.3 * jnp.ones((16,), jnp.float32), (16, 128))
        _ctx_2048t = jnp.einsum('bsk,bkd->bsd', _ctx_2048c, _ctx_2048P)
        _ctx_2048t = _ctx_2048t * jax.lax.rsqrt(jnp.mean(jnp.square(_ctx_2048t)) + 1e-12) * 0.953939
        ctx_2048 = -1.39393e-06 + 0.999914 * (_ctx_2048t + 0.3 * jax.random.normal(jax.random.fold_in(_rk, 611), (16, 128, 256), jnp.float32))
        itok_BxS_0_1023 = jax.random.randint(jax.random.fold_in(_rk, 12), (16, 64), 0, 128, jnp.int32)
        return (x, ctx_2048, itok_BxS_0_1023)
    x, ctx_2048, itok_BxS_0_1023 = _rec_inputs()

    def _L0_xattn_setup():
        import jax, jax.numpy as jnp
        import numpy as np
        B, Lq, Lk = (2, 512, 128)
        Q_DIM, KV_DIM = (256, 256)
        H, HD = (16, 128)
        KVC, QC, R = (64, 96, 64)
        LOOKBACK = 8
        NEG = -1e+30

        def _rope(x, L):
            half = x.shape[-1] // 2
            inv_freq = 1.0 / 10000.0 ** (jnp.arange(half, dtype=jnp.float32) / half)
            ang = jnp.arange(L, dtype=jnp.float32)[:, None] * inv_freq
            cos, sin = (jnp.cos(ang), jnp.sin(ang))
            x1, x2 = (x[..., :half], x[..., half:])
            return jnp.concatenate([x1 * cos - x2 * sin, x1 * sin + x2 * cos], axis=-1)
        key = jax.random.key(seed)
        ks = jax.random.split(key, 11)

        def w(k, shape, fan_in):
            return jax.random.normal(k, shape, jnp.float32) / np.sqrt(fan_in).astype(np.float32)
        return {'q': jax.random.normal(ks[0], (B, Lq, Q_DIM), jnp.float32), 'kv': jax.random.normal(ks[1], (B, Lk, KV_DIM), jnp.float32), 'seg_id': jnp.sort(jax.random.randint(ks[2], (B, Lq), 0, Lk), axis=-1), 'W_kvc': w(ks[3], (KV_DIM, KVC), KV_DIM), 'W_dq': w(ks[4], (Q_DIM, QC), Q_DIM), 'W_uq': w(ks[5], (QC, H * HD), QC), 'W_qr': w(ks[6], (QC, H * R), QC), 'W_uk': w(ks[7], (KVC, H * HD), KVC), 'W_kr': w(ks[8], (KVC, R), KVC), 'W_uv': w(ks[9], (KVC, H * HD), KVC), 'W_o': w(ks[10], (H * HD, Q_DIM), H * HD)}
    _L0_xattn_all = _L0_xattn_setup()
    _L0_xattn_in = {k: v for k, v in _L0_xattn_all.items() if k in ('W_kvc', 'W_dq', 'W_uq', 'W_qr', 'W_uk', 'W_kr', 'W_uv', 'W_o')}
    del _L0_xattn_all

    def _L0_attn_setup():
        import jax, jax.numpy as jnp
        import numpy as np
        HIDDEN = 256
        NUM_HEADS = 16
        HEAD_DIM = HIDDEN // NUM_HEADS
        key = jax.random.key(seed)
        ks = jax.random.split(key, 5)
        B, S, H = (2, 256, HIDDEN)
        qkv_bound = float(np.sqrt(6.0 / (H + 3 * H)))
        out_bound = float(np.sqrt(6.0 / (H + H)))
        return {'x': jax.random.normal(ks[0], (B, S, H), dtype=jnp.float32), 'W_qkv': jax.random.uniform(ks[1], (3 * H, H), minval=-qkv_bound, maxval=qkv_bound, dtype=jnp.float32), 'b_qkv': jnp.zeros((3 * H,), dtype=jnp.float32), 'W_out': jax.random.uniform(ks[2], (H, H), minval=-out_bound, maxval=out_bound, dtype=jnp.float32), 'b_out': jnp.zeros((H,), dtype=jnp.float32)}
    _L0_attn_all = _L0_attn_setup()
    _L0_attn_in = {k: v for k, v in _L0_attn_all.items() if k in ('W_qkv', 'b_qkv', 'W_out', 'b_out')}
    del _L0_attn_all

    def _L0_ffn_setup():
        import jax, jax.numpy as jnp
        import numpy as np
        B, T, D = (2, 128, 256)
        E, F, K = (64, 64, 4)
        S, HS = (2, 64 * 4)
        key = jax.random.key(seed)
        ks = jax.random.split(key, 9)
        s = 0.02
        f32 = jnp.float32
        return {'x': jax.random.normal(ks[0], (B, T, D), f32), 'router_w': jax.random.normal(ks[1], (D, E), f32) * s, 'router_bias': jnp.zeros((E,), f32), 'wg': jax.random.normal(ks[2], (E, D, F), f32) * s, 'wu': jax.random.normal(ks[3], (E, D, F), f32) * s, 'wd': jax.random.normal(ks[4], (E, F, D), f32) * s, 'swg': jax.random.normal(ks[5], (S, D, HS), f32) * s, 'swu': jax.random.normal(ks[6], (S, D, HS), f32) * s, 'swd': jax.random.normal(ks[7], (S, HS, D), f32) * s}
    _L0_ffn_all = _L0_ffn_setup()
    _L0_ffn_in = {k: v for k, v in _L0_ffn_all.items() if k in ('router_w', 'router_bias', 'wg', 'wu', 'wd', 'swg', 'swu', 'swd')}
    del _L0_ffn_all
    return {'x': x, 'ctx_2048': ctx_2048, 'itok_BxS_0_1023': itok_BxS_0_1023, 'L0_xattn_W_kvc': _L0_xattn_in['W_kvc'], 'L0_xattn_W_dq': _L0_xattn_in['W_dq'], 'L0_xattn_W_uq': _L0_xattn_in['W_uq'], 'L0_xattn_W_qr': _L0_xattn_in['W_qr'], 'L0_xattn_W_uk': _L0_xattn_in['W_uk'], 'L0_xattn_W_kr': _L0_xattn_in['W_kr'], 'L0_xattn_W_uv': _L0_xattn_in['W_uv'], 'L0_xattn_W_o': _L0_xattn_in['W_o'], 'L0_attn_W_qkv': _L0_attn_in['W_qkv'], 'L0_attn_b_qkv': _L0_attn_in['b_qkv'], 'L0_attn_W_out': _L0_attn_in['W_out'], 'L0_attn_b_out': _L0_attn_in['b_out'], 'L0_ffn_router_w': _L0_ffn_in['router_w'], 'L0_ffn_router_bias': _L0_ffn_in['router_bias'], 'L0_ffn_wg': _L0_ffn_in['wg'], 'L0_ffn_wu': _L0_ffn_in['wu'], 'L0_ffn_wd': _L0_ffn_in['wd'], 'L0_ffn_swg': _L0_ffn_in['swg'], 'L0_ffn_swu': _L0_ffn_in['swu'], 'L0_ffn_swd': _L0_ffn_in['swd']}

def reference(x, ctx_2048, itok_BxS_0_1023, L0_xattn_W_kvc, L0_xattn_W_dq, L0_xattn_W_uq, L0_xattn_W_qr, L0_xattn_W_uk, L0_xattn_W_kr, L0_xattn_W_uv, L0_xattn_W_o, L0_attn_W_qkv, L0_attn_b_qkv, L0_attn_W_out, L0_attn_b_out, L0_ffn_router_w, L0_ffn_router_bias, L0_ffn_wg, L0_ffn_wu, L0_ffn_wd, L0_ffn_swg, L0_ffn_swu, L0_ffn_swd):
    import jax
    import jax.numpy as jnp

    def _L0_xattn_ref(q, kv, seg_id, W_kvc, W_dq, W_uq, W_qr, W_uk, W_kr, W_uv, W_o):
        import jax, jax.numpy as jnp
        import numpy as np
        B, Lq, Lk = (2, 512, 128)
        Q_DIM, KV_DIM = (256, 256)
        H, HD = (16, 128)
        KVC, QC, R = (64, 96, 64)
        LOOKBACK = 8
        NEG = -1e+30

        def _rope(x, L):
            half = x.shape[-1] // 2
            inv_freq = 1.0 / 10000.0 ** (jnp.arange(half, dtype=jnp.float32) / half)
            ang = jnp.arange(L, dtype=jnp.float32)[:, None] * inv_freq
            cos, sin = (jnp.cos(ang), jnp.sin(ang))
            x1, x2 = (x[..., :half], x[..., half:])
            return jnp.concatenate([x1 * cos - x2 * sin, x1 * sin + x2 * cos], axis=-1)
        b, lq, _ = q.shape
        lk = kv.shape[1]
        kv_c = kv @ W_kvc
        q_c = q @ W_dq
        q_nope = (q_c @ W_uq).reshape(b, lq, H, HD).transpose(0, 2, 1, 3)
        q_rope = (q_c @ W_qr).reshape(b, lq, H, R).transpose(0, 2, 1, 3)
        k_nope = (kv_c @ W_uk).reshape(b, lk, H, HD)
        v = (kv_c @ W_uv).reshape(b, lk, H, HD)
        k_rope = kv_c @ W_kr
        q_rope = _rope(q_rope, lq)
        k_rope = _rope(k_rope, lk)
        scale = 1.0 / np.sqrt(HD + R).astype(np.float32)
        scores = (jnp.einsum('bhqd,bkhd->bhqk', q_nope, k_nope) + jnp.einsum('bhqr,bkr->bhqk', q_rope, k_rope)) * scale
        k_ids = jnp.arange(lk)[None, None, :]
        qs = seg_id[:, :, None]
        good = (k_ids <= qs) & (k_ids >= qs - LOOKBACK)
        scores = jnp.where(good[:, None, :, :], scores, NEG)
        attn = jax.nn.softmax(scores, axis=-1)
        out = jnp.einsum('bhqk,bkhd->bqhd', attn, v).reshape(b, lq, H * HD)
        return out @ W_o

    def _L0_attn_ref(x, W_qkv, b_qkv, W_out, b_out):
        import jax, jax.numpy as jnp
        import numpy as np
        HIDDEN = 256
        NUM_HEADS = 16
        HEAD_DIM = HIDDEN // NUM_HEADS
        B, S, H = x.shape
        qkv = x @ W_qkv.T + b_qkv
        q, k, v = jnp.split(qkv, 3, axis=-1)

        def to_heads(t):
            return t.reshape(B, S, NUM_HEADS, HEAD_DIM).transpose(0, 2, 1, 3)
        q, k, v = (to_heads(q), to_heads(k), to_heads(v))
        scale = HEAD_DIM ** (-0.5)
        scores = jnp.einsum('bnqd,bnkd->bnqk', q, k) * scale
        causal = jnp.triu(jnp.ones((S, S), dtype=bool), k=1)
        scores = jnp.where(causal, -jnp.inf, scores)
        attn = jax.nn.softmax(scores, axis=-1)
        out = jnp.einsum('bnqk,bnkd->bnqd', attn, v)
        out = out.transpose(0, 2, 1, 3).reshape(B, S, H)
        return out @ W_out.T + b_out

    def _L0_ffn_ref(x, router_w, router_bias, wg, wu, wd, swg, swu, swd):
        import jax, jax.numpy as jnp
        import numpy as np
        B, T, D = (2, 128, 256)
        E, F, K = (64, 64, 4)
        S, HS = (2, 64 * 4)
        b, t, d = x.shape
        flat = x.reshape(b * t, d)
        n = flat.shape[0]
        logits = flat @ router_w
        scores = jax.nn.softmax(logits, axis=-1)
        _, topk_idx = jax.lax.top_k(logits + router_bias, K)
        topk_scores = jnp.take_along_axis(scores, topk_idx, axis=-1)
        topk_scores = topk_scores / topk_scores.sum(axis=-1, keepdims=True)
        comb = jnp.zeros((n, E), dtype=flat.dtype).at[jnp.arange(n)[:, None], topk_idx].set(topk_scores)
        g = jax.nn.silu(jnp.einsum('nd,edf->nef', flat, wg))
        u = jnp.einsum('nd,edf->nef', flat, wu)
        routed = jnp.einsum('ne,nef,efd->nd', comb, g * u, wd)
        sg = jax.nn.silu(jnp.einsum('nd,sdh->nsh', flat, swg))
        su = jnp.einsum('nd,sdh->nsh', flat, swu)
        shared = jnp.einsum('nsh,shd->nd', sg * su, swd)
        return (routed + shared).reshape(b, t, d)
    x = x + _L0_xattn_ref(_layernorm(x, axis=-1), ctx_2048, itok_BxS_0_1023, L0_xattn_W_kvc, L0_xattn_W_dq, L0_xattn_W_uq, L0_xattn_W_qr, L0_xattn_W_uk, L0_xattn_W_kr, L0_xattn_W_uv, L0_xattn_W_o)
    x = x + _L0_attn_ref(_layernorm(x, axis=-1), L0_attn_W_qkv, L0_attn_b_qkv, L0_attn_W_out, L0_attn_b_out)
    x = x + _L0_ffn_ref(_layernorm(x, axis=-1), L0_ffn_router_w, L0_ffn_router_bias, L0_ffn_wg, L0_ffn_wu, L0_ffn_wd, L0_ffn_swg, L0_ffn_swu, L0_ffn_swd)
    return x

_drawn_inputs = setup_inputs


def setup_inputs(seed=0):
    import zlib

    import numpy as np

    out = dict(_drawn_inputs(seed))
    spreads = {'L0_attn_b_qkv': (0.0, 0.1), 'L0_attn_b_out': (0.0, 0.1), 'L0_ffn_router_bias': (0.0, 0.8)}
    factors = {'L0_ffn_router_w': 8.0,
     'L0_ffn_wg': 8.0,
     'L0_ffn_wu': 8.0,
     'L0_ffn_wd': 8.0,
     'L0_ffn_swg': 3.034,
     'L0_ffn_swu': 3.001,
     'L0_ffn_swd': 3.001}
    for name, (base, spread) in spreads.items():
        noise = np.random.default_rng([zlib.crc32(name.encode()), seed]).standard_normal(out[name].shape)
        drawn = base * np.exp(spread * noise) if base else spread * noise
        out[name] = jnp.asarray(drawn.astype(out[name].dtype))
    for name, factor in factors.items():
        out[name] = (out[name] * factor).astype(out[name].dtype)
    return out
```

```python
from contextlib import ExitStack

import concourse.bass as bass
from concourse import mybir

ALU = mybir.AluOpType
ACT = mybir.ActivationFunctionType
F32 = mybir.dt.float32
BF16 = mybir.dt.bfloat16
I32 = mybir.dt.int32
U32 = mybir.dt.uint32
AX = mybir.AxisListType

P = 128
NB, LQ, D = 16, 64, 256
LK = 128
N = NB * LQ
NT = N // P
BT = P // LQ
DC = D // P
H, HD = 16, 128
KVC, QC, R = 64, 96, 64
HALF = R // 2
LOOKBACK = 8
XSCALE = float((HD + R) ** -0.5)
HPAIR = H // 2
SD = D // H
ASCALE = float(SD ** -0.5)
NEG = -1e30
EPS = 1e-5
E, F, TOPK = 64, 64, 4
NSH, HS = 2, 256
EG = 512 // F
NG = E // EG
W2_LOADS = 6
ROUTE_STEPS = 4 + 2 * NT + 1 + 2 * TOPK - 1 + 4

ORDER = [("x", 1), ("y", 18), ("x", 2), ("a", 0), ("x", 3), ("x", 4), ("a", 0.5), ("x", 5), ("x", 6),
         ("x", 7), ("a", 1), ("x", 8), ("a", 2), ("a", 3), ("x", 9), ("a", 4), ("x", 10), ("x", 11),
         ("a", 5), ("x", 12), ("x", 12.5), ("a", 6), ("x", 13), ("x", 14), ("a", 7), ("x", 16),
         ("x", 15), ("a", 8), ("x", 17)]


def build(nc, x, ctx, seg, w_kvc, w_dq, w_uq, w_qr, w_uk, w_kr, w_uv, w_o, w_qkv, b_qkv, w_out,
          b_out, router_w, router_b, wg, wu, wd, swg, swu, swd, rope_k, rope_q, out):
    stack = ExitStack()
    with stack:
        def sb(name, shape, dt=F32):
            return stack.enter_context(nc.sbuf_tensor(name, shape, dt))

        def sem(name):
            return stack.enter_context(nc.semaphore(name))

        x_sb = sb("x_sb", [P, NT, D])
        ctx_sb = sb("ctx_sb", [P, BT, D])
        seg_i = sb("seg_i", [P, NT], I32)
        w_kvc_sb = sb("w_kvc_sb", [P, DC, KVC])
        w_dq_sb = sb("w_dq_sb", [P, DC, QC])
        w_qr_sb = sb("w_qr_sb", [QC, H * R])
        w_kr_sb = sb("w_kr_sb", [KVC, R])
        w_kr_rot = sb("w_kr_rot", [KVC, R])
        rope_k_sb = sb("rope_k_sb", [P, 2, BT * LK])
        rope_q_sb = sb("rope_q_sb", [P, 2, R])
        bqk_sb = sb("bqk_sb", [P, 2 * DC])
        bv_sb = sb("bv_sb", [P, D])
        bout_sb = sb("bout_sb", [P, D])
        rw_sb = sb("rw_sb", [P, DC, E])
        rb_sb = sb("rb_sb", [P, E])
        QN = sb("QN", [P, H, KVC + R])
        QN_flat = QN[:, :, :].rearrange("p a b -> p (a b)")
        QT = sb("QT", [P, BT, H, LQ])
        QT_flat = QT[:, :, :, :].rearrange("p a b c -> p (a b c)")
        xpT = sb("xpT", [P, BT, HPAIR, P])
        xpT_flat = xpT[:, :, :, :].rearrange("p a b c -> p (a b c)")
        big = sb("big", [P, 8192 + H * HD])
        flat_g = big[:, 0:8192]
        w_uq_sb = flat_g[0:QC, 0:H * HD]
        w_uk_sb = flat_g[0:KVC, H * HD:2 * H * HD]
        w_uv_sb = big[0:KVC, 8192:8192 + H * HD]
        w_o_sb = flat_g[:, 2 * H * HD:].rearrange("p (h d) -> p h d", h=H)
        w_qkv_nat = QN_flat[:, 0:3 * DC * D].rearrange("p (c d) -> p c d", d=D)
        w_out_nat = QN_flat[:, 1536:1536 + DC * D].rearrange("p (c d) -> p c d", d=D)
        w_out_p = QT_flat[:, 0:DC * D].rearrange("p (c r n) -> p c r n", c=DC, r=2)
        st_uqT = QT_flat[:, 512:512 + H * QC].rearrange("p (h n) -> p h n", h=H)
        st_kuvT = xpT_flat[:, 0:2 * H * KVC].rearrange("p (h k n) -> p h k n", h=H, k=2)
        ident = sb("ident", [P, P])
        ones_f = sb("ones_f", [P, P])
        pick = sb("pick", [P, BT, 2, LQ], BF16)
        causal = sb("causal", [P, BT, LQ], BF16)
        head_of = sb("head_of", [P, P // SD])
        uqk_sb = sb("uqk_sb", [QC, H, KVC])
        uvo_sb = sb("uvo_sb", [P, H // 4, 2, D])
        w_qkvT = sb("w_qkvT", [P, DC, 3 * D])
        w_outT = sb("w_outT", [P, 2, D])
        neg_mask = sb("neg_mask", [P, NT, LK], BF16)
        key_iota = sb("key_iota", [P, LK])
        seg_f = sb("seg_f", [P, NT])
        e_iota = sb("e_iota", [P, E])
        half_neg = sb("half_neg", [P, 1])
        stats = sb("stats", [P, 2, 6])
        held = sb("held", [P, 1])
        mv = sb("mv", [P, 2, 2])
        rstd = sb("rstd", [P, 2, 2])
        xn = sb("xn", [P, D])
        xnT = sb("xnT", [P, DC, P])
        ctxT = sb("ctxT", [P, DC, BT, LK])
        qcT = sb("qcT", [QC, P])
        KK = sb("KK", [P, BT, LK])
        kr_a = sb("kr_a", [P, BT * LK])
        kr_b = sb("kr_b", [P, BT * LK])
        kv_nat = sb("kv_nat", [P, BT, KVC + 1])
        rt_b = sb("rt_b", [P, H, R])
        x_max = sb("x_max", [P, BT, HPAIR])
        x_rec = sb("x_rec", [P, BT, HPAIR])
        xp = sb("xp", [P, BT, HPAIR, LK])
        ON = sb("ON", [P, BT, HPAIR, KVC])
        OT = sb("OT", [P, H // 4, 2, BT, LQ])
        held_p = sb("held_p", [P, NT])
        an = sb("an", [P, D])
        anT = sb("anT", [P, DC, P])
        qT = sb("qT", [P, DC, P])
        kT = sb("kT", [P, DC, P])
        v_nat = sb("v_nat", [P, HPAIR, 2 * SD + 1])
        qbd = sb("qbd", [P, BT, DC, P // SD, LQ])
        a_max = sb("a_max", [P, BT, HPAIR])
        a_rec = sb("a_rec", [P, BT, HPAIR])
        ap = sb("ap", [P, HPAIR, BT, LQ])
        apT = sb("apT", [P, HPAIR, P])
        aON = sb("aON", [P, BT, HPAIR, SD])
        aOT = sb("aOT", [P, 2, BT, LQ])
        xT = sb("xT", [P, DC, NT, P])
        logit = sb("logit", [P, NT, E])
        biased = sb("biased", [P, NT, E])
        comb = sb("comb", [P, NT, E])
        chosen = sb("chosen", [P, NT, E])
        is_j = sb("is_j", [P, NT, E])
        top_v = sb("top_v", [P, NT, 8])
        top_i = sb("top_i", [P, NT, 8], U32)
        top_f = sb("top_f", [P, NT, 8])
        row_s = sb("row_s", [P, 3, NT])
        silu = sb("silu", [P, 2, 512])
        hid = sb("hid", [P, 2, 512])
        hidT = sb("hidT", [P, 2, 512])
        comb_g = comb[:, :, :].rearrange("p t (r e) -> p t r e", e=EG)
        GW = 512 * DC
        gbuf = [big[:, 3 * GW * k:3 * GW * (k + 1)] for k in range(2)]
        ps = stack.enter_context(nc.psum_tensor("ps", [P, 8, 512], F32))

        def bank(b):
            return ps[:, b, :]

        ld_r = sem("ld_r")
        ld_g = [sem("ld_g0"), sem("ld_g1")]
        route, route_ex = sem("route"), sem("route_ex")
        ld_x, ld_ctx, ld_w1, ld_w2, ld_small, ld_ffn, ld_wd, st_out = (sem(n) for n in (
            "ld_x", "ld_ctx", "ld_w1", "ld_w2", "ld_small", "ld_ffn", "ld_wd", "st_out"))
        zeroed, consts, masks, mask_step = (sem(n) for n in ("zeroed", "consts", "masks", "mask_step"))
        su_pe, su_ev, sorted_out = sem("su_pe"), sem("su_ev"), sem("sorted_out")
        names = """x_stat x_aggr x_veps x_rstd x_norm x_nT_pe x_nT x_ctxT_pe x_ctxT x_kvT_pe x_kvT
            x_qcT_pe x_qcT x_kr_pe x_kra x_krb x_kr x_kvn_pe x_kvn x_q_pe x_q x_qr_pe x_cos0 x_cos1
            x_sin0 x_sin1 x_qn0 x_qn1 x_qt_pe0 x_qt_pe1 x_qt_pe2 x_qt_pe3 x_qt0 x_qt1 x_qt2 x_qt3
            x_s0_pe x_s1_pe x_mx0 x_mx1 x_sub0 x_sub1 x_exp0 x_exp1
            x_pl0_pe x_ph0_pe x_pl1_pe x_ph1_pe x_pl0 x_ph0 x_pl1 x_ph1
            x_o0_pe x_o1_pe x_rec0 x_rec1 x_on0 x_on1 x_ot0_pe x_ot1_pe x_ot0 x_ot1 x_y_pe x_res
            a_stat a_aggr a_veps a_rstd a_norm a_nT_pe a_nT a_qk_pe a_q a_k a_qbd a_v_pe a_v
            a_s_pe a_mx a_sub a_exp a_pl_pe a_ph_pe a_pl a_ph a_o_pe a_rec a_on a_ot_pe a_ot
            a_y_pe a_res a_resb
            r_stat r_aggr r_veps r_rstd r_norm r_T_pe r_T r_l_pe""".split()
        names += ["f_gu_pe", "f_silu", "f_hid", "f_comb", "f_hT_pe", "f_hT", "f_y_pe", "f_acc"]
        S = {n: sem(n) for n in names}

        def done(eng, name, t):
            if isinstance(t, int) and t < 0:
                return
            eng.wait_ge(S[name], t + 1)

        xr = x.rearrange("b q d -> (b q) d").rearrange("(t p) d -> p t d", p=P)
        outr = out.rearrange("b q d -> (b q) d").rearrange("(t p) d -> p t d", p=P)
        ctxr = ctx.rearrange("(t b) k d -> t k b d", b=BT)
        segr = seg.rearrange("b q -> (b q)").rearrange("(t p) -> p t", p=P)

        setup_groups = []

        def setup_group(after, work, dst, src):
            setup_groups.append((after, work, dst, src))
            return len(setup_groups)

        for g in range(4):
            bk = bank(len(setup_groups) % 8)
            n_uq = setup_group(0, [("t", bk[:, j * QC:(j + 1) * QC], w_uq_sb[:, (4 * g + j) * HD:(4 * g + j + 1) * HD], None)
                                   for j in range(4)],
                               st_uqT[:, 4 * g:4 * g + 4, :], bk[:, 0:4 * QC].rearrange("p (h n) -> p h n", h=4))
            bk = bank(len(setup_groups) % 8)
            n_kuv = setup_group(0, [("t", bk[:, (2 * j + i) * KVC:(2 * j + i + 1) * KVC],
                                     w[:, (4 * g + j) * HD:(4 * g + j + 1) * HD], None)
                                    for j in range(4) for i, w in enumerate((w_uk_sb, w_uv_sb))],
                                st_kuvT[:, 4 * g:4 * g + 4, :, :], bk.rearrange("p (h k n) -> p h k n", h=4, k=2))
            if g == 0:
                for c in range(DC):
                    for o0, o1 in ((0, 4), (4, 6)):
                        bk = bank(len(setup_groups) % 8)
                        setup_group(0, [("t", bk[:, (o - o0) * P:(o - o0 + 1) * P], w_qkv_nat[:, o, c * P:(c + 1) * P], None)
                                        for o in range(o0, o1)],
                                    w_qkvT[:, c, o0 * P:o1 * P], bk[:, 0:(o1 - o0) * P])
                bk = bank(len(setup_groups) % 8)
                setup_group(0, [("t", bk[:, (r * DC + c) * P:(r * DC + c + 1) * P], w_out_p[:, c, r, :], None)
                                for r in range(2) for c in range(DC)],
                            w_outT[:, :, :], bk.rearrange("p (r o) -> p r o", r=2))
            bk = bank(len(setup_groups) % 8)
            setup_group(n_kuv, [("m", bk[0:QC, j * KVC:(j + 1) * KVC], st_uqT[:, 4 * g + j, :], st_kuvT[:, 4 * g + j, 0, :])
                                for j in range(4)],
                        uqk_sb[:, 4 * g:4 * g + 4, :], bk[0:QC, 0:4 * KVC].rearrange("p (h n) -> p h n", h=4))
            bk = bank(len(setup_groups) % 8)
            setup_group(n_kuv, [("m", bk[(j // 2) * KVC:(j // 2 + 1) * KVC, (j % 2) * D:(j % 2 + 1) * D],
                                 st_kuvT[:, 4 * g + j, 1, :], w_o_sb[:, 4 * g + j, :]) for j in range(4)],
                        uvo_sb[:, g, :, :], bk.rearrange("p (r d) -> p r d", r=2))

        block = stack.enter_context(nc.Block())

        def interleave(steps, t_x, t_a):
            for kind, what in ORDER:
                t = t_x if kind == "x" else t_a
                if t is not None and (kind, what) in steps:
                    steps[(kind, what)](t)

        def run_tiles(eng, steps):
            interleave(steps, 0, None)
            interleave(steps, 1, 0)
            with eng.Fori(2, NT) as t:
                interleave(steps, t, t - 1)
            interleave(steps, None, NT - 1)

        def gates(k):
            b = gbuf[k]
            return b[:, 0:GW], b[:, GW:2 * GW], b[:, 2 * GW:3 * GW].rearrange("p (n d) -> p n d", d=D)

        def load_shared(sp):
            gate, up, down = gates(0)
            for dst, src in ((gate, swg), (up, swu)):
                sp.dma_start(dst.rearrange("p (s n) -> p s n", s=NSH),
                             src.rearrange("s (p c) h -> p s (c h)", c=DC)).then_inc(ld_g[0], 16)
            sp.dma_start(down, swd.rearrange("s (n p) d -> p (s n) d", p=P)).then_inc(ld_g[0], 16)

        def load_group(sp, k, r):
            gate, up, down = gates(k)
            for dst, src in ((gate, wg), (up, wu)):
                src = src.rearrange("(r e) (p c) f -> r p e (c f)", e=EG, c=DC)
                sp.dma_start(dst.rearrange("p (e n) -> p e n", e=EG), src[r]).then_inc(ld_g[k], 16)
            src = wd.rearrange("(r n j) f d -> r (j f) n d", n=EG // 2, j=2)
            sp.dma_start(down, src[r]).then_inc(ld_g[k], 16)

        def run_units(eng, step):
            for tile in range(NT):
                step(tile, 0, tile)
            with eng.Fori(0, NG // 2) as i:
                for k in range(2):
                    for tile in range(NT):
                        step(NT * (2 * i + 1 + k) + tile, (2 * i + 1 + k, (1 + k) % 2), tile)

        @block.sync
        def _(sp):
            sp.dma_start(w_uq_sb, w_uq).then_inc(ld_w1, 16)
            sp.dma_start(w_uk_sb, w_uk).then_inc(ld_w1, 16)
            sp.dma_start(w_uv_sb, w_uv).then_inc(ld_w1, 16)
            sp.dma_start(w_o_sb, w_o.rearrange("(h p) d -> p h d", p=HD)).then_inc(ld_w1, 16)
            sp.dma_start(x_sb[:, :, :], xr).then_inc(ld_x, 16)
            sp.dma_start(rope_k_sb[KVC:P, :, :], rope_k).then_inc(ld_small, 16)
            sp.dma_start(rope_q_sb[:, :, :], rope_q).then_inc(ld_small, 16)
            sp.dma_start(bqk_sb[:, :], b_qkv[0:2 * D].rearrange("(c p) -> p c", p=P), allow_slow_non_contiguous=True).then_inc(ld_small, 16)
            sp.dma_start(bv_sb[:, :], b_qkv[2 * D:3 * D].rearrange("(o d) -> o d", o=1).to_broadcast([P, D])).then_inc(ld_small, 16)
            sp.dma_start(bout_sb[:, :], b_out.rearrange("(o d) -> o d", o=1).to_broadcast([P, D])).then_inc(ld_small, 16)
            sp.dma_start(rb_sb[:, :], router_b.rearrange("(o e) -> o e", o=1).to_broadcast([P, E])).then_inc(ld_r, 16)
            sp.dma_start(rw_sb[:, :, :], router_w.rearrange("(p c) e -> p c e", c=DC)).then_inc(ld_r, 16)
            sp.dma_start(ctx_sb[:, :, :], ctxr[0]).then_inc(ld_ctx, 16)
            with sp.Fori(1, NT) as t:
                done(sp, "x_ctxT_pe", t - 1)
                sp.dma_start(ctx_sb[:, :, :], ctxr[t]).then_inc(ld_ctx, 16)
            sp.wait_ge(su_ev, len(setup_groups))
            load_shared(sp)
            load_group(sp, 1, 0)
            with sp.Fori(0, NG // 2 - 1) as i:
                for k in range(2):
                    done(sp, "f_y_pe", NT * (2 * i + k) + NT - 1)
                    load_group(sp, k, 2 * i + k + 1)
            done(sp, "f_y_pe", NT * (NG - 2) + NT - 1)
            load_group(sp, 0, NG - 1)
            done(sp, "f_acc", NT * (NG + 1) - 1)
            sp.dma_start(outr, x_sb[:, :, :]).then_inc(st_out, 16)
            sp.wait_ge(st_out, 16)

        @block.gpsimd
        def _(pool):
            g = nc.gpsimd
            g.memset(ident[:, :], 0.0).then_inc(zeroed, 1)
            g.memset(ones_f[:, :], 1.0).then_inc(zeroed, 1)
            g.memset(pick[:, :, :, :], 0.0).then_inc(zeroed, 1)
            g.memset(causal[:, :, :], 0.0).then_inc(zeroed, 1)
            g.memset(half_neg[:, :], -0.5).then_inc(zeroed, 1)
            g.memset(kv_nat[:, :, KVC:KVC + 1], 1.0).then_inc(consts, 1)
            g.memset(v_nat[:, :, 2 * SD:2 * SD + 1], 1.0).then_inc(consts, 1)
            g.iota(key_iota[:, :], pattern=[[1, LK]], base=0, channel_multiplier=0,
                   allow_small_or_imprecise_dtypes=True).then_inc(consts, 1)
            g.iota(e_iota[:, :], pattern=[[1, E]], base=0, channel_multiplier=0,
                   allow_small_or_imprecise_dtypes=True).then_inc(consts, 1)
            pool.wait_ge(zeroed, 5)
            g.affine_select(out=ident[:, :], in_=ident[:, :], compare_op=ALU.not_equal, fill=1.0,
                            base=0, pattern=[[-1, P]], channel_multiplier=1).then_inc(consts, 1)
            for b in range(BT):
                g.affine_select(out=pick[:, b, :, :], in_=pick[:, b, :, :], compare_op=ALU.not_equal,
                                fill=1.0, base=-LQ * b, pattern=[[0, 2], [-1, LQ]],
                                channel_multiplier=1).then_inc(consts, 1)
            g.affine_select(out=causal[:, :, :], in_=causal[:, :, :], compare_op=ALU.is_ge,
                            fill=NEG, base=0, pattern=[[-LQ, BT], [-1, LQ]],
                            channel_multiplier=1).then_inc(consts, 1)
            g.affine_select(out=head_of[:, :], in_=ones_f[:, 0:P // SD], compare_op=ALU.is_ge,
                            fill=0.0, base=0, pattern=[[-SD, P // SD]],
                            channel_multiplier=1).then_inc(mask_step, 1)
            pool.wait_ge(mask_step, 1)
            g.affine_select(out=head_of[:, :], in_=head_of[:, :], compare_op=ALU.is_ge,
                            fill=0.0, base=SD - 1, pattern=[[SD, P // SD]],
                            channel_multiplier=-1).then_inc(consts, 1)

            def x_rstd(t):
                done(pool, "x_veps", t)
                g.tensor_tensor(rstd[:, 0, 1:2], rstd[:, 0, 0:1], half_neg[:, :], ALU.pow).then_inc(S["x_rstd"], 1)

            def x_qn(t):
                done(pool, "x_sin0", t)
                hh = H // 2
                g.tensor_tensor(QN[:, 0:hh, KVC:], QN[:, 0:hh, KVC:], rt_b[:, 0:hh, :], ALU.add).then_inc(S["x_qn0"], 1)

            def a_rstd(t):
                done(pool, "a_veps", t)
                g.tensor_tensor(rstd[:, 1, 1:2], rstd[:, 1, 0:1], half_neg[:, :], ALU.pow).then_inc(S["a_rstd"], 1)

            def a_qbd(t):
                done(pool, "a_q", t)
                done(pool, "a_s_pe", t - 1)
                for b in range(BT):
                    for c in range(DC):
                        last = g.tensor_tensor(
                            qbd[:, b, c, :, :],
                            qT[:, c, b * LQ:(b + 1) * LQ].unsqueeze(1).to_broadcast([P, P // SD, LQ]),
                            head_of[:, :].unsqueeze(2).to_broadcast([P, P // SD, LQ]), ALU.mult)
                        last.then_inc(S["a_qbd"], 1)

            def a_resb(t):
                done(pool, "x_res", t)
                done(pool, "a_stat", t)
                done(pool, "a_norm", t)
                if isinstance(t, int) and t == 0:
                    pool.wait_ge(ld_small, 96)
                g.tensor_tensor(x_sb[:, t, :], x_sb[:, t, :], bout_sb[:, :], ALU.add).then_inc(S["a_resb"], 1)

            run_tiles(pool, {("x", 1): x_rstd, ("x", 8): x_qn,
                             ("a", 0): a_rstd, ("a", 2): a_qbd, ("a", 3): a_resb})

            for t in range(NT):
                done(pool, "r_veps", t)
                g.tensor_tensor(rstd[:, 0, 1:2], rstd[:, 0, 0:1], half_neg[:, :], ALU.pow).then_inc(S["r_rstd"], 1)

            def weigh(u, group, tile):
                done(pool, "f_hid", u)
                if isinstance(group, int):
                    g.memset(held_p[:, tile:tile + 1], 0.0).then_inc(S["f_comb"], 1)
                    return
                done(pool, "f_hT_pe", u - 2)
                if tile == 0:
                    pool.wait_ge(route, ROUTE_STEPS)
                h = hid[:, tile % 2, :].rearrange("p (e f) -> p e f", e=EG)
                r, _ = group
                g.tensor_tensor(h, h, comb_g[:, tile, r - 1, :].unsqueeze(2).to_broadcast([P, EG, F]),
                                ALU.mult).then_inc(S["f_comb"], 1)
            run_units(pool, weigh)

        @block.vector
        def _(dve):
            v = nc.vector

            dve.wait_ge(ld_small, 96)
            dve.wait_ge(consts, 9)
            v.tensor_copy(seg_f[:, :], seg_i[:, :]).then_inc(masks, 1)
            dve.wait_ge(masks, 1)
            dist = xp[:, 0, :, :].rearrange("p h k -> p (h k)").rearrange("p (t k) -> p t k", t=NT)
            dist2 = rt_b[:, :, :].rearrange("p h r -> p (h r)").rearrange("p (t k) -> p t k", t=NT)
            v.tensor_tensor(dist, key_iota[:, :].unsqueeze(1).to_broadcast([P, NT, LK]),
                            seg_f[:, :].unsqueeze(2).to_broadcast([P, NT, LK]), ALU.subtract).then_inc(masks, 1)
            dve.wait_ge(masks, 2)
            v.tensor_scalar(dist2, dist, 0.0, NEG, ALU.is_gt, ALU.mult).then_inc(masks, 1)
            v.tensor_scalar(dist, dist, float(-LOOKBACK), NEG, ALU.is_lt, ALU.mult).then_inc(masks, 1)
            dve.wait_ge(masks, 4)
            v.tensor_tensor(neg_mask[:, :, :], dist, dist2, ALU.add).then_inc(masks, 1)
            dve.wait_ge(masks, 5)
            dve.wait_ge(ld_w2, 16 * W2_LOADS)
            v.tensor_scalar(w_kr_rot[:, 0:HALF], w_kr_sb[:, HALF:R], -1.0, None, ALU.mult).then_inc(masks, 1)
            v.tensor_copy(w_kr_rot[:, HALF:R], w_kr_sb[:, 0:HALF]).then_inc(masks, 1)

            def su_copy(dst, src):
                v.tensor_copy(dst, src).then_inc(su_ev, 1)
            for n, (_, _, dst, src) in enumerate(setup_groups):
                dve.wait_ge(su_pe, n + 1)
                su_copy(dst, src)

            def norm_stats(t, k, pre, before):
                done(dve, before, t) if before else dve.wait_ge(ld_x, 16)
                v.memset(held[:, :], 0.0)
                v.bn_stats(stats[:, k, :], x_sb[:, t, :]).then_inc(S[pre + "_stat"], 1)
                done(dve, pre + "_stat", t)
                v.memset(held[:, :], 0.0)
                v.bn_aggr(mv[:, k, :], stats[:, k, :]).then_inc(S[pre + "_aggr"], 1)
                done(dve, pre + "_aggr", t)
                v.tensor_scalar(rstd[:, k, 0:1], mv[:, k, 1:2], EPS, None, ALU.add).then_inc(S[pre + "_veps"], 1)

            def norm_apply(t, k, pre, dst, reader):
                done(dve, pre + "_rstd", t)
                done(dve, reader, t - 1)
                v.tensor_scalar(dst[:, :], x_sb[:, t, :], mv[:, k, 0:1], rstd[:, k, 1:2],
                                ALU.subtract, ALU.mult).then_inc(S[pre + "_norm"], 1)

            def x_norm(t):
                norm_stats(t, 0, "x", None)
                norm_apply(t, 0, "x", xn, "x_nT_pe")

            def x_nT(t):
                done(dve, "x_nT_pe", t)
                done(dve, "x_qcT_pe", t - 1)
                v.tensor_copy(xnT[:, :, :], bank(1)[:, 0:DC * P].rearrange("p (c n) -> p c n", c=DC)).then_inc(S["x_nT"], 1)

            def x_qcT(t):
                done(dve, "x_qcT_pe", t)
                done(dve, "x_qr_pe", t - 1)
                v.tensor_copy(qcT[:, :], bank(3)[0:QC, 0:P]).then_inc(S["x_qcT"], 1)

            def x_kr(t):
                done(dve, "x_kr_pe", t)
                v.tensor_tensor(kr_a[KVC:P, :], bank(0)[KVC:P, 0:BT * LK], rope_k_sb[KVC:P, 0, :], ALU.mult).then_inc(S["x_kra"], 1)
                v.tensor_tensor(kr_b[KVC:P, :], bank(0)[KVC:P, BT * LK:2 * BT * LK], rope_k_sb[KVC:P, 1, :], ALU.mult).then_inc(S["x_krb"], 1)
                done(dve, "x_krb", t)
                done(dve, "x_s1_pe", t - 1)
                v.tensor_tensor(KK[KVC:P, :, :], kr_a[KVC:P, :].rearrange("p (b k) -> p b k", b=BT),
                                kr_b[KVC:P, :].rearrange("p (b k) -> p b k", b=BT), ALU.add).then_inc(S["x_kr"], 1)

            def x_rope(t):
                done(dve, "x_qr_pe", t)
                done(dve, "x_qt_pe3", t - 1)
                hh = H // 2
                for n, b in enumerate((4, 0)):
                    src = bank(b).rearrange("p (h r) -> p h r", h=hh)
                    hs = slice(hh * n, hh * n + hh)
                    cos = rope_q_sb[:, 0, :].unsqueeze(1).to_broadcast([P, hh, R])
                    v.tensor_tensor(QN[:, hs, KVC:], src, cos, ALU.mult).then_inc(S[f"x_cos{n}"], 1)
                    done(dve, f"x_qn{n}", t - 1)
                    for lo, hi in ((0, HALF), (HALF, 0)):
                        sin = rope_q_sb[:, 1, lo:lo + HALF].unsqueeze(1).to_broadcast([P, hh, HALF])
                        last = v.tensor_tensor(rt_b[:, hs, lo:lo + HALF], src[:, :, hi:hi + HALF], sin, ALU.mult)
                    last.then_inc(S[f"x_sin{n}"], 1)
                done(dve, "x_sin1", t)
                v.tensor_tensor(QN[:, hh:, KVC:], QN[:, hh:, KVC:], rt_b[:, hh:, :], ALU.add).then_inc(S["x_qn1"], 1)

            def x_soft(t, b):
                s = ps[:, 2 * b:2 * b + 2, :].rearrange("p a (h k) -> p (a h) k", k=LK)
                done(dve, f"x_s{b}_pe", t)
                v.tensor_reduce(x_max[:, b, :], s, AX.X, ALU.max).then_inc(S[f"x_mx{b}"], 1)
                done(dve, f"x_mx{b}", t)
                done(dve, f"x_ph{b}_pe", t - 1)
                v.tensor_tensor(xp[:, b, :, :], s, x_max[:, b, :].unsqueeze(2).to_broadcast([P, HPAIR, LK]),
                                ALU.subtract).then_inc(S[f"x_sub{b}"], 1)

            def x_ph(t, b):
                done(dve, f"x_ph{b}_pe", t)
                done(dve, f"x_o{b}_pe", t - 1)
                v.tensor_copy(xpT[:, b, 4:8, :], bank((0, 2)[b]).rearrange("p (h n) -> p h n", h=4)).then_inc(S[f"x_ph{b}"], 1)

            def x_on(t, b):
                banks = ((1, 4), (3, 0))[b]
                done(dve, f"x_o{b}_pe", t)
                for n, k in enumerate(banks):
                    o = bank(k)[:, 0:4 * (KVC + 1)].rearrange("p (h c) -> p h c", h=4)
                    v.reciprocal(x_rec[:, b, 4 * n:4 * n + 4], o[:, :, KVC]).then_inc(S[f"x_rec{b}"], 1)
                dve.wait_ge(S[f"x_rec{b}"], 2 * t + 2)
                done(dve, f"x_ot{b}_pe", t - 1)
                for n, k in enumerate(banks):
                    o = bank(k)[:, 0:4 * (KVC + 1)].rearrange("p (h c) -> p h c", h=4)
                    last = v.tensor_tensor(ON[:, b, 4 * n:4 * n + 4, :], o[:, :, 0:KVC],
                                           x_rec[:, b, 4 * n:4 * n + 4].unsqueeze(2).to_broadcast([P, 4, KVC]), ALU.mult)
                last.then_inc(S[f"x_on{b}"], 1)

            def x_res(t):
                done(dve, "x_y_pe", t)
                done(dve, "x_norm", t)
                v.tensor_tensor(x_sb[:, t, :], x_sb[:, t, :], bank(4)[:, 0:D], ALU.add).then_inc(S["x_res"], 1)

            def a_stats(t):
                norm_stats(t, 1, "a", "x_res")

            def a_norm(t):
                norm_apply(t, 1, "a", an, "a_nT_pe")

            def a_nT(t):
                done(dve, "a_nT_pe", t)
                done(dve, "a_v_pe", t - 1)
                v.tensor_copy(anT[:, :, :], bank(5)[:, 0:DC * P].rearrange("p (c n) -> p c n", c=DC)).then_inc(S["a_nT"], 1)

            def a_v(t):
                done(dve, "a_v_pe", t)
                done(dve, "a_o_pe", t - 1)
                v.tensor_tensor(v_nat[:, :, 0:2 * SD], bank(7)[:, 0:D].rearrange("p (h d) -> p h d", h=HPAIR),
                                bv_sb[:, :].rearrange("p (h d) -> p h d", h=HPAIR), ALU.add).then_inc(S["a_v"], 1)

            def a_soft(t):
                s = ps[:, 5:7, :].rearrange("p b (h k) -> p b h k", k=LQ)
                done(dve, "a_s_pe", t)
                v.tensor_reduce(a_max[:, :, :], s, AX.X, ALU.max).then_inc(S["a_mx"], 1)
                done(dve, "a_mx", t)
                done(dve, "a_ph_pe", t - 1)
                for b in range(BT):
                    last = v.tensor_tensor(ap[:, :, b, :], s[:, b, :, :],
                                           a_max[:, b, :].unsqueeze(2).to_broadcast([P, HPAIR, LQ]), ALU.subtract)
                last.then_inc(S["a_sub"], 1)

            def a_on(t):
                w = 2 * SD + 1
                o = ps[:, 6:8, 0:HPAIR * w].rearrange("p b (h d) -> p b h d", h=HPAIR)
                done(dve, "a_o_pe", t)
                v.reciprocal(a_rec[:, :, :], o[:, :, :, 2 * SD]).then_inc(S["a_rec"], 1)
                done(dve, "a_rec", t)
                done(dve, "a_ot_pe", t - 1)
                for par in range(2):
                    rows = slice(LQ * par, LQ * par + LQ)
                    last = v.tensor_tensor(
                        aON[rows, :, :, :], o[rows, :, :, SD * par:SD * par + SD],
                        a_rec[rows, :, :].unsqueeze(3).to_broadcast([LQ, BT, HPAIR, SD]), ALU.mult)
                last.then_inc(S["a_on"], 1)

            def a_res(t):
                done(dve, "a_y_pe", t)
                done(dve, "a_resb", t)
                v.tensor_tensor(x_sb[:, t, :], x_sb[:, t, :], bank(6)[:, 0:D], ALU.add).then_inc(S["a_res"], 1)

            run_tiles(dve, {
                ("x", 1): x_norm, ("x", 2): x_nT, ("a", 0): a_stats, ("x", 4): x_qcT, ("a", 0.5): a_norm, ("a", 1): a_nT,
                ("x", 6): x_kr, ("a", 3): a_v, ("x", 8): x_rope, ("a", 4): a_soft,
                ("x", 10): lambda t: x_soft(t, 0), ("x", 11): lambda t: x_soft(t, 1),
                ("x", 12): lambda t: x_ph(t, 0), ("x", 14): lambda t: x_ph(t, 1),
                ("x", 13): lambda t: x_on(t, 0), ("a", 6): a_on,
                ("x", 15): lambda t: x_on(t, 1), ("a", 8): a_res, ("y", 18): x_res})

            for t in range(NT):
                norm_stats(t, 0, "r", "a_res")
                norm_apply(t, 0, "r", xn, "r_T_pe")
            dve.wait_ge(S["r_l_pe"], NT)
            dve.wait_ge(ld_r, 32)
            steps = [0]

            def link(ins):
                steps[0] += 1
                ins.then_inc(route, 1)
                dve.wait_ge(route, steps[0])

            def over_e(a):
                return a.unsqueeze(2).to_broadcast([P, NT, E])

            link(v.tensor_copy(logit[:, :, :], bank(1).rearrange("p (t e) -> p t e", t=NT)))
            link(v.tensor_tensor(biased[:, :, :], logit[:, :, :],
                                 rb_sb[:, :].unsqueeze(1).to_broadcast([P, NT, E]), ALU.add))
            link(v.tensor_reduce(row_s[:, 0, :], logit[:, :, :], AX.X, ALU.max))
            link(v.tensor_tensor(logit[:, :, :], logit[:, :, :], over_e(row_s[:, 0, :]), ALU.subtract))
            for t in range(NT):
                link(v.max(top_v[:, t, :], biased[:, t, :]))
                link(v.max_index(top_i[:, t, :], top_v[:, t, :], biased[:, t, :]))
            link(v.tensor_copy(top_f[:, :, :], top_i[:, :, :]))
            for j in range(TOPK):
                dst = chosen if j == 0 else is_j
                link(v.tensor_tensor(dst[:, :, :], e_iota[:, :].unsqueeze(1).to_broadcast([P, NT, E]),
                                     over_e(top_f[:, :, j]), ALU.is_equal))
                if j > 0:
                    link(v.tensor_tensor(chosen[:, :, :], chosen[:, :, :], is_j[:, :, :], ALU.add))
            dve.wait_ge(route_ex, 1)
            link(v.tensor_tensor(comb[:, :, :], chosen[:, :, :], logit[:, :, :], ALU.mult))
            link(v.tensor_reduce(row_s[:, 1, :], comb[:, :, :], AX.X, ALU.add))
            link(v.reciprocal(row_s[:, 2, :], row_s[:, 1, :]))
            link(v.tensor_tensor(comb[:, :, :], comb[:, :, :], over_e(row_s[:, 2, :]), ALU.mult))
            assert steps[0] == ROUTE_STEPS, steps

            def expert(u, group, tile):
                k = tile % 2
                done(dve, "f_silu", u)
                done(dve, "f_hT_pe", u - 2)
                v.tensor_tensor(hid[:, k, :], silu[:, k, :], bank(2 + k), ALU.mult).then_inc(S["f_hid"], 1)
                if isinstance(u, int) and u < 2:
                    return
                add_result(u - 2, (tile - 2) % NT)

            def add_result(u, tile):
                done(dve, "f_y_pe", u)
                done(dve, "f_acc", u - 1)
                v.tensor_tensor(x_sb[:, tile, :], x_sb[:, tile, :], bank(6 + tile % 2)[:, 0:D],
                                ALU.add).then_inc(S["f_acc"], 1)
            run_units(dve, expert)
            last_u = NT * (NG + 1)
            for u in (last_u - 2, last_u - 1):
                add_result(u, u % NT)

        @block.scalar
        def _(act):
            s = nc.scalar
            act.dma_start(seg_i[:, :], segr, allow_slow_non_contiguous=True).then_inc(ld_small, 16)
            for dst, src in (
                    (w_kvc_sb[:, :, :], w_kvc.rearrange("(c p) n -> p c n", p=P)),
                    (w_dq_sb[:, :, :], w_dq.rearrange("(c p) n -> p c n", p=P)),
                    (w_qr_sb[:, :], w_qr), (w_kr_sb[:, :], w_kr),
                    (w_qkv_nat, w_qkv.rearrange("(c p) d -> p c d", p=P)),
                    (w_out_nat, w_out.rearrange("(c p) d -> p c d", p=P))):
                act.dma_start(dst, src).then_inc(ld_w2, 16)

            act.wait_ge(ld_w2, 16 * W2_LOADS)
            for c in range(DC):
                s.copy(w_out_p[:, c, :, :].rearrange("p r (a d) -> p r a d", a=HPAIR),
                       w_out_nat[:, c, :].rearrange("p (a r d) -> p r a d", a=HPAIR, r=2)).then_inc(sorted_out, 1)

            def x_ctxT(t):
                done(act, "x_ctxT_pe", t)
                done(act, "x_kvT_pe", t - 1)
                s.copy(ctxT[:, :, :, :], bank(0).rearrange("p (c b k) -> p c b k", c=DC, b=BT)).then_inc(S["x_ctxT"], 1)

            def x_kvT(t):
                done(act, "x_kvT_pe", t)
                done(act, "x_s1_pe", t - 1)
                s.copy(KK[0:KVC, :, :], bank(2)[0:KVC, 0:BT * LK].rearrange("p (b k) -> p b k", b=BT)).then_inc(S["x_kvT"], 1)

            def x_kvn(t):
                done(act, "x_kvn_pe", t)
                done(act, "x_o1_pe", t - 1)
                if isinstance(t, int) and t == 0:
                    act.wait_ge(consts, 9)
                s.copy(kv_nat[:, :, 0:KVC], bank(1)[:, 0:BT * KVC].rearrange("p (b c) -> p b c", b=BT)).then_inc(S["x_kvn"], 1)

            def x_q(t):
                done(act, "x_q_pe", t)
                done(act, "x_qt_pe3", t - 1)
                s.copy(QN[:, :, 0:KVC], ps[:, 2:4, :].rearrange("p a (h c) -> p (a h) c", c=KVC)).then_inc(S["x_q"], 1)

            def x_qt(t):
                for g in range(4):
                    done(act, f"x_qt_pe{g}", t)
                    if g == 0:
                        done(act, "x_s1_pe", t - 1)
                    s.copy(QT[:, :, 4 * g:4 * g + 4, :],
                           bank(1 + g).rearrange("p (h b q) -> p b h q", h=4, b=BT)).then_inc(S[f"x_qt{g}"], 1)

            def x_exp(t, b):
                done(act, f"x_sub{b}", t)
                s.activation(xp[:, b, :, :], xp[:, b, :, :], ACT.Exp, scale=XSCALE).then_inc(S[f"x_exp{b}"], 1)

            def x_pl(t, b):
                done(act, f"x_pl{b}_pe", t)
                done(act, f"x_o{b}_pe", t - 1)
                s.copy(xpT[:, b, 0:4, :], bank((4, 0)[b]).rearrange("p (h n) -> p h n", h=4)).then_inc(S[f"x_pl{b}"], 1)

            def x_ot(t, b):
                done(act, f"x_ot{b}_pe", t)
                done(act, "x_y_pe", t - 1)
                s.copy(OT[:, :, :, b, :], bank((1, 2)[b]).rearrange("p (k r q) -> p k r q", k=H // 4, r=2)).then_inc(S[f"x_ot{b}"], 1)

            def a_qk(t):
                done(act, "a_qk_pe", t)
                if not isinstance(t, int) or t > 0:
                    act.wait_ge(S["a_qbd"], 4 * t)
                q = bank(6).rearrange("p (c n) -> p c n", c=2 * DC)
                for c in range(DC):
                    last = s.activation(qT[:, c, :], q[:, c, :], ACT.Identity, bias=bqk_sb[:, c:c + 1])
                last.then_inc(S["a_q"], 1)
                done(act, "a_s_pe", t - 1)
                for c in range(DC):
                    last = s.activation(kT[:, c, :], q[:, DC + c, :], ACT.Identity, bias=bqk_sb[:, DC + c:DC + c + 1])
                last.then_inc(S["a_k"], 1)

            def a_exp(t):
                done(act, "a_sub", t)
                s.activation(ap[:, :, :, :], ap[:, :, :, :], ACT.Exp, scale=ASCALE).then_inc(S["a_exp"], 1)

            def a_pl(t):
                done(act, "a_pl_pe", t)
                done(act, "a_o_pe", t - 1)
                s.copy(apT[:, 0:4, :], bank(7).rearrange("p (h n) -> p h n", h=4)).then_inc(S["a_pl"], 1)
                done(act, "a_ph_pe", t)
                s.copy(apT[:, 4:8, :], bank(5).rearrange("p (h n) -> p h n", h=4)).then_inc(S["a_ph"], 1)

            def a_ot(t):
                done(act, "a_ot_pe", t)
                done(act, "a_y_pe", t - 1)
                s.copy(aOT[:, :, :, :], bank(5)[:, 0:2 * P].rearrange("p (b r q) -> p r b q", b=BT, r=2)).then_inc(S["a_ot"], 1)

            act.wait_ge(ld_small, 96)
            run_tiles(act, {
                ("x", 1): x_ctxT, ("x", 3): x_kvT, ("a", 2): a_qk, ("x", 5): x_kvn, ("x", 7): x_q,
                ("x", 9): x_qt, ("a", 4): a_exp, ("x", 10): lambda t: x_exp(t, 0),
                ("x", 12.5): lambda t: x_exp(t, 1), ("a", 5): a_pl,
                ("x", 12): lambda t: x_pl(t, 0), ("x", 14): lambda t: x_pl(t, 1),
                ("a", 7): a_ot, ("x", 16): lambda t: x_ot(t, 0), ("x", 17): lambda t: x_ot(t, 1)})

            for t in range(NT):
                done(act, "r_T_pe", t)
                s.copy(xT[:, :, t, :], bank(0)[:, 0:DC * P].rearrange("p (c n) -> p c n", c=DC)).then_inc(S["r_T"], 1)
            act.wait_ge(route, 4)
            s.activation(logit[:, :, :], logit[:, :, :], ACT.Exp).then_inc(route_ex, 1)

            def expert(u, group, tile):
                k = tile % 2
                done(act, "f_gu_pe", u)
                done(act, "f_hid", u - 2)
                s.activation(silu[:, k, :], bank(k), ACT.Silu).then_inc(S["f_silu"], 1)
                if isinstance(u, int) and u < 1:
                    return
                turn(u - 1, 1 - k)

            def turn(u, k):
                done(act, "f_hT_pe", u)
                done(act, "f_y_pe", u - 2)
                s.copy(hidT[:, k, :], bank(4 + k)).then_inc(S["f_hT"], 1)
            run_units(act, expert)
            turn(NT * (NG + 1) - 1, 1)

        @block.tensor
        def _(pe):
            m = nc.tensor
            pe.wait_ge(consts, 9)
            pe.wait_ge(ld_w1, 64)
            pe.wait_ge(ld_w2, 16 * W2_LOADS)
            pe.wait_ge(masks, 7)
            pe.wait_ge(sorted_out, DC)

            def tr(dst, src):
                return m.transpose(dst, src, ident[0:src.shape[0], 0:src.shape[0]])

            for n, (after, work, _, _) in enumerate(setup_groups):
                if max(after, n - 7) > 0:
                    pe.wait_ge(su_ev, max(after, n - 7))
                for kind, dst, a, b in work:
                    last = tr(dst, a) if kind == "t" else m.matmul(dst, a, b, start=True, stop=True)
                last.then_inc(su_pe, 1)
            pe.wait_ge(su_ev, len(setup_groups))

            def x_ctxT(t):
                pe.wait_ge(ld_ctx, 16 * t + 16)
                done(pe, "x_on1", t - 1)
                for c in range(DC):
                    for b in range(BT):
                        last = tr(bank(0)[:, (c * BT + b) * P:(c * BT + b + 1) * P], ctx_sb[:, b, c * P:(c + 1) * P])
                last.then_inc(S["x_ctxT_pe"], 1)

            def x_nT(t):
                done(pe, "x_norm", t)
                done(pe, "x_ot0", t - 1)
                for c in range(DC):
                    last = tr(bank(1)[:, c * P:(c + 1) * P], xn[:, c * P:(c + 1) * P])
                last.then_inc(S["x_nT_pe"], 1)

            def x_kvT(t):
                done(pe, "x_ctxT", t)
                done(pe, "x_ot1", t - 1)
                for c in range(DC):
                    last = m.matmul(bank(2)[0:KVC, 0:BT * LK], w_kvc_sb[:, c, :], ctxT[:, c, :, :],
                                    start=(c == 0), stop=(c == DC - 1))
                last.then_inc(S["x_kvT_pe"], 1)

            def x_qcT(t):
                done(pe, "x_nT", t)
                done(pe, "x_on1", t - 1)
                for c in range(DC):
                    last = m.matmul(bank(3)[0:QC, 0:P], w_dq_sb[:, c, :], xnT[:, c, :],
                                    start=(c == 0), stop=(c == DC - 1))
                last.then_inc(S["x_qcT_pe"], 1)

            def x_kr(t):
                m.matmul(bank(0)[KVC:P, 0:BT * LK], w_kr_sb[:, :], KK[0:KVC, :, :], start=True, stop=True)
                m.matmul(bank(0)[KVC:P, BT * LK:2 * BT * LK], w_kr_rot[:, :], KK[0:KVC, :, :],
                         start=True, stop=True).then_inc(S["x_kr_pe"], 1)

            def x_kvn(t):
                done(pe, "x_kvT", t)
                for b in range(BT):
                    last = m.matmul(bank(1)[:, b * KVC:(b + 1) * KVC], KK[0:KVC, b, :], ident[0:KVC, 0:KVC],
                                    start=True, stop=True)
                last.then_inc(S["x_kvn_pe"], 1)

            def x_q(t):
                done(pe, "x_qcT", t)
                for n in range(2):
                    last = m.matmul(bank(2 + n), qcT[:, :], uqk_sb[:, 8 * n:8 * n + 8, :], start=True, stop=True)
                last.then_inc(S["x_q_pe"], 1)

            def x_qr(t):
                done(pe, "x_krb", t)
                done(pe, "x_res", t - 1)
                for n, k in enumerate((4, 0)):
                    last = m.matmul(bank(k), qcT[:, :], w_qr_sb[:, 512 * n:512 * n + 512], start=True, stop=True)
                last.then_inc(S["x_qr_pe"], 1)

            def x_qt(t):
                done(pe, "x_q", t)
                done(pe, "x_kvn", t)
                for g in range(4):
                    if g % 2 == 0:
                        done(pe, f"x_qn{g // 2}", t)
                    for h in range(4):
                        last = tr(bank(1 + g)[:, h * P:(h + 1) * P], QN[:, 4 * g + h, :])
                    last.then_inc(S[f"x_qt_pe{g}"], 1)

            def x_s(t, b):
                if b == 0:
                    done(pe, "x_kr", t)
                for a in range(2):
                    if b == 0:
                        done(pe, f"x_qt{2 * a}", t)
                        done(pe, f"x_qt{2 * a + 1}", t)
                    for h in range(4):
                        p = 4 * a + h
                        m.matmul(bank(2 * b + a)[:, h * LK:(h + 1) * LK],
                                 QT[:, b, 2 * p:2 * p + 2, :], KK[:, b, :], start=(h == 0), stop=False,
                                 skip_group_check=True)
                    last = m.matmul(bank(2 * b + a), pick[:, b, :, :],
                                    neg_mask[:, t, :].unsqueeze(1).to_broadcast([P, 4, LK]),
                                    start=False, stop=True, skip_group_check=True)
                last.then_inc(S[f"x_s{b}_pe"], 1)

            def x_p(t, b):
                done(pe, f"x_exp{b}", t)
                if b == 1:
                    done(pe, "x_ph0", t)
                lo, hi = ((4, 0), (0, 2))[b]
                for name, k, p0 in ((f"x_pl{b}_pe", lo, 0), (f"x_ph{b}_pe", hi, 4)):
                    for h in range(4):
                        last = tr(bank(k)[:, h * P:(h + 1) * P], xp[:, b, p0 + h, :])
                    last.then_inc(S[name], 1)

            def x_o(t, b):
                done(pe, f"x_pl{b}", t)
                done(pe, f"x_ph{b}", t)
                w = KVC + 1
                for n, k in enumerate(((1, 4), (3, 0))[b]):
                    for h in range(4):
                        last = m.matmul(bank(k)[:, h * w:(h + 1) * w], xpT[:, b, 4 * n + h, :], kv_nat[:, b, :],
                                        start=True, stop=True)
                last.then_inc(S[f"x_o{b}_pe"], 1)

            def x_ot(t, b):
                done(pe, f"x_on{b}", t)
                for k in range(H // 4):
                    last = tr(bank((1, 2)[b])[:, k * P:(k + 1) * P], ON[:, b, 2 * k:2 * k + 2, :])
                last.then_inc(S[f"x_ot{b}_pe"], 1)

            def x_y(t):
                done(pe, "x_ot0", t)
                done(pe, "x_ot1", t)
                for n in range(H // 2):
                    k, par = n // 2, n % 2
                    last = m.matmul(bank(4)[:, 0:D], OT[:, k, par, :, :], uvo_sb[:, k, par, :],
                                    start=(n == 0), stop=(n == H // 2 - 1))
                last.then_inc(S["x_y_pe"], 1)

            def a_nT(t):
                done(pe, "a_norm", t)
                done(pe, "a_ot", t - 1)
                for c in range(DC):
                    last = tr(bank(5)[:, c * P:(c + 1) * P], an[:, c * P:(c + 1) * P])
                last.then_inc(S["a_nT_pe"], 1)

            def a_qk(t):
                done(pe, "a_nT", t)
                done(pe, "a_res", t - 1)
                for n in range(2 * DC):
                    for c in range(DC):
                        last = m.matmul(bank(6)[:, n * P:(n + 1) * P], w_qkvT[:, c, n * P:(n + 1) * P],
                                        anT[:, c, :], start=(c == 0), stop=(c == DC - 1))
                last.then_inc(S["a_qk_pe"], 1)

            def a_v(t):
                done(pe, "a_on", t - 1)
                for c in range(DC):
                    last = m.matmul(bank(7)[:, 0:D], anT[:, c, :], w_qkvT[:, c, 2 * D:3 * D],
                                    start=(c == 0), stop=(c == DC - 1))
                last.then_inc(S["a_v_pe"], 1)

            def a_s(t):
                pe.wait_ge(S["a_qbd"], 4 * t + 4)
                done(pe, "a_k", t)
                for b in range(BT):
                    for p in range(HPAIR):
                        c, h = divmod(2 * p, P // SD)
                        m.matmul(bank(5 + b)[:, p * LQ:(p + 1) * LQ], qbd[:, b, c, h:h + 2, :],
                                 kT[:, c, b * LQ:(b + 1) * LQ], start=(p == 0), stop=False,
                                 skip_group_check=True)
                    last = m.matmul(bank(5 + b), pick[:, b, :, :],
                                    causal[:, b, :].unsqueeze(1).to_broadcast([P, HPAIR, LQ]),
                                    start=False, stop=True, skip_group_check=True)
                last.then_inc(S["a_s_pe"], 1)

            def a_p(t):
                done(pe, "a_exp", t)
                done(pe, "a_v", t)
                for name, k, p0 in (("a_pl_pe", 7, 0), ("a_ph_pe", 5, 4)):
                    for h in range(4):
                        last = tr(bank(k)[:, h * P:(h + 1) * P], ap[:, p0 + h, :, :])
                    last.then_inc(S[name], 1)

            def a_o(t):
                done(pe, "a_pl", t)
                done(pe, "a_ph", t)
                w = 2 * SD + 1
                for b in range(BT):
                    rows = slice(LQ * b, LQ * b + LQ)
                    for p in range(HPAIR):
                        last = m.matmul(bank(6 + b)[:, p * w:(p + 1) * w], apT[rows, p, :], v_nat[rows, p, :],
                                        start=True, stop=True)
                last.then_inc(S["a_o_pe"], 1)

            def a_ot(t):
                done(pe, "a_on", t)
                for b in range(BT):
                    last = tr(bank(5)[:, b * P:(b + 1) * P], aON[:, b, :, :])
                last.then_inc(S["a_ot_pe"], 1)

            def a_y(t):
                done(pe, "a_ot", t)
                for par in range(2):
                    last = m.matmul(bank(6)[:, 0:D], aOT[:, par, :, :], w_outT[:, par, :],
                                    start=(par == 0), stop=(par == 1))
                last.then_inc(S["a_y_pe"], 1)

            run_tiles(pe, {
                ("x", 1): x_ctxT, ("x", 2): x_nT, ("a", 1): a_nT, ("x", 3): x_kvT, ("x", 4): x_qcT,
                ("a", 2): a_qk, ("x", 5): x_kvn, ("x", 6): x_kr, ("x", 7): x_q, ("a", 3): a_v,
                ("x", 8): x_qr, ("a", 4): a_s, ("x", 9): x_qt, ("x", 10): lambda t: x_s(t, 0),
                ("a", 5): a_p, ("x", 11): lambda t: x_s(t, 1), ("a", 6): a_o,
                ("x", 12): lambda t: x_p(t, 0), ("a", 7): a_ot, ("x", 13): lambda t: x_o(t, 0),
                ("a", 8): a_y, ("x", 14): lambda t: x_p(t, 1), ("x", 15): lambda t: x_o(t, 1),
                ("x", 16): lambda t: x_ot(t, 0), ("x", 17): lambda t: x_ot(t, 1), ("y", 18): x_y})

            pe.wait_ge(ld_r, 32)
            for t in range(NT):
                done(pe, "r_norm", t)
                done(pe, "r_T", t - 1)
                odd_even = xn[:, :].rearrange("p (n c) -> p c n", c=DC)
                for c in range(DC):
                    last = tr(bank(0)[:, c * P:(c + 1) * P], odd_even[:, c, :])
                last.then_inc(S["r_T_pe"], 1)
                done(pe, "r_T", t)
                for c in range(DC):
                    last = m.matmul(bank(1)[:, t * E:(t + 1) * E], xT[:, c, t, :], rw_sb[:, c, :],
                                    start=(c == 0), stop=(c == DC - 1))
                last.then_inc(S["r_l_pe"], 1)

            pe.wait_ge(route, 1)

            def up_products(u, group, tile):
                k = tile % 2
                buf = 0 if isinstance(group, int) else group[1]
                if tile == 0:
                    if isinstance(group, int):
                        pe.wait_ge(ld_g[0], 48)
                    else:
                        pe.wait_ge(ld_g[buf], 24 * (group[0] - buf) + 48)
                done(pe, "f_silu", u - 2)
                done(pe, "f_hid", u - 2)
                gate, up, _ = gates(buf)
                for w, b in ((gate, k), (up, 2 + k)):
                    w = w.rearrange("p (s c n) -> p c s n", s=NSH if isinstance(group, int) else EG, c=DC)
                    for c in range(DC):
                        last = m.matmul(bank(b), xT[:, c, tile, :], w[:, c, :, :], start=(c == 0), stop=(c == DC - 1))
                last.then_inc(S["f_gu_pe"], 1)

            def down_products(u, buf, tile):
                k = tile % 2
                done(pe, "f_hT", u)
                done(pe, "f_acc", u - 2)
                _, _, down = gates(buf)
                for n in range(4):
                    last = m.matmul(bank(6 + k)[:, 0:D], hidT[:, k, n * P:(n + 1) * P], down[:, n, :],
                                    start=(n == 0), stop=(n == 3))
                last.then_inc(S["f_y_pe"], 1)

            def turn_hidden(u, tile):
                k = tile % 2
                done(pe, "f_comb", u)
                done(pe, "f_hT", u - 2)
                for n in range(4):
                    last = tr(bank(4 + k)[:, n * P:(n + 1) * P], hid[:, k, n * P:(n + 1) * P])
                last.then_inc(S["f_hT_pe"], 1)

            def expert(u, group, tile):
                up_products(u, group, tile)
                buf = 0 if isinstance(group, int) else group[1]
                if not (isinstance(u, int) and u < 2):
                    down_products(u - 2, buf if tile >= 2 else 1 - buf, (tile - 2) % NT)
                if not (isinstance(u, int) and u < 1):
                    turn_hidden(u - 1, (tile - 1) % NT)
            run_units(pe, expert)
            last_u = NT * (NG + 1)
            down_products(last_u - 2, 0, NT - 2)
            turn_hidden(last_u - 1, NT - 1)
            down_products(last_u - 1, 0, NT - 1)


def rope_tables():
    import numpy as np
    inv = (1.0 / np.float32(10000.0) ** (np.arange(HALF, dtype=np.float32) / np.float32(HALF))).astype(np.float32)
    ang = np.arange(LK, dtype=np.float32)[:, None] * inv
    cos = np.concatenate([np.cos(ang)] * 2, axis=1).astype(np.float32)
    sin = np.concatenate([np.sin(ang)] * 2, axis=1).astype(np.float32)
    keys = np.stack([np.tile(cos.T, (1, BT)), np.tile(sin.T, (1, BT))], axis=1)
    signed = np.concatenate([-sin[:, :HALF], sin[:, HALF:]], axis=1)
    latents = np.stack([np.tile(cos[:LQ], (BT, 1)), np.tile(signed[:LQ], (BT, 1))], axis=1)
    return np.ascontiguousarray(keys), np.ascontiguousarray(latents)


_INS = ["x", "ctx_2048", "itok_BxS_0_1023", "L0_xattn_W_kvc", "L0_xattn_W_dq", "L0_xattn_W_uq",
        "L0_xattn_W_qr", "L0_xattn_W_uk", "L0_xattn_W_kr", "L0_xattn_W_uv", "L0_xattn_W_o",
        "L0_attn_W_qkv", "L0_attn_b_qkv", "L0_attn_W_out", "L0_attn_b_out", "L0_ffn_router_w",
        "L0_ffn_router_bias", "L0_ffn_wg", "L0_ffn_wu", "L0_ffn_wd", "L0_ffn_swg", "L0_ffn_swu",
        "L0_ffn_swd"]


def kernel(**inputs):
    import numpy as _np
    import concourse.bacc as _bacc
    from concourse import mybir as _mybir
    from concourse.bass_utils import run_bass_kernel_spmd as _run

    nc = _bacc.Bacc("TRN2", target_bir_lowering=False, num_devices=1)
    arrays, args = {}, []
    tables = dict(zip(("rope_keys", "rope_latents"), rope_tables()))
    for name in _INS + list(tables):
        a = _np.ascontiguousarray(inputs[name] if name in inputs else tables[name])
        arrays[f"in_{name}_dram"] = a
        args.append(nc.dram_tensor(f"in_{name}_dram", a.shape, _mybir.dt.from_np(a.dtype), kind="ExternalInput").ap())
    out = nc.dram_tensor("out_0_dram", (NB, LQ, D), _mybir.dt.float32, kind="ExternalOutput").ap()
    build(nc, *args, out)
    r = _run(nc, [arrays], core_ids=[0])
    return r.results[0]["out_0_dram"]
```

```python
from contextlib import ExitStack

import concourse.bass as bass
from concourse import mybir

ALU = mybir.AluOpType
ACT = mybir.ActivationFunctionType
F32 = mybir.dt.float32
BF16 = mybir.dt.bfloat16
I32 = mybir.dt.int32
U32 = mybir.dt.uint32
AX = mybir.AxisListType

P = 128
NB, LQ, D = 16, 64, 256
LK = 128
N = NB * LQ
NT = N // P
BT = P // LQ
DC = D // P
H, HD = 16, 128
KVC, QC, R = 64, 96, 64
HALF = R // 2
LOOKBACK = 8
XSCALE = float((HD + R) ** -0.5)
HPAIR = H // 2
SD = D // H
ASCALE = float(SD ** -0.5)
NEG = -1e30
EPS = 1e-5
E, F, TOPK = 64, 64, 4
NSH, HS = 2, 256
CAP = P
SLOTS = N * TOPK
NBLK = (SLOTS + E * (CAP - 1)) // CAP
QB = 4
QBUF = 4
NQ = -(-NBLK // (QB * QBUF)) * QBUF
NBLK = NQ * QB
WROW = 2 * DC * F + D // 2
GB = 4
CHOSEN_STEPS = 4 + 2 * NT + 1 + TOPK + 4
EID_STEPS = CHOSEN_STEPS + 5 + 2 * (E.bit_length() - 1) + 5
RANKS_AT, EID_AT = 1, 3
LATE = 8
LEAD = 2

ORDER = [("x", 1), ("y", 18), ("x", 2), ("a", 0), ("x", 3), ("x", 4), ("a", 0.5), ("x", 5), ("x", 6),
         ("x", 7), ("a", 1), ("x", 8), ("a", 2), ("s", 0), ("a", 3), ("x", 9), ("s", 1), ("x", 10),
         ("s", 2), ("x", 11), ("a", 4), ("x", 12), ("s", 3), ("a", 4.5), ("x", 12.5), ("x", 14),
         ("x", 13), ("a", 4.7), ("a", 5), ("x", 16), ("x", 15), ("a", 6), ("x", 17), ("a", 7), ("a", 8)]


def build(nc, x, ctx, seg, w_kvc, w_dq, w_uqT, w_qr, w_ukuvT, w_kr, w_o, w_qkv_T, b_qk, b_v,
          w_out_T, b_out, router_w, router_b, w_exp, swg, swu, swd, rope_k, rope_q, out, xs, ys):
    stack = ExitStack()
    with stack:
        def sb(name, shape, dt=F32):
            return stack.enter_context(nc.sbuf_tensor(name, shape, dt))

        def sem(name):
            return stack.enter_context(nc.semaphore(name))

        x_sb = sb("x_sb", [P, NT, D])
        ctx_sb = sb("ctx_sb", [P, BT, D])
        seg_i = sb("seg_i", [P, NT], I32)
        w_kvc_sb = sb("w_kvc_sb", [P, DC, KVC])
        w_dq_sb = sb("w_dq_sb", [P, DC, QC])
        w_qr_sb = sb("w_qr_sb", [QC, H * R])
        w_kr_sb = sb("w_kr_sb", [KVC, R])
        w_kr_rot = sb("w_kr_rot", [KVC, R])
        rope_k_sb = sb("rope_k_sb", [P, 2, BT * LK])
        rope_q_sb = sb("rope_q_sb", [P, 2, R])
        bqk_sb = sb("bqk_sb", [P, 2 * DC])
        bv_sb = sb("bv_sb", [P, D])
        bout_sb = sb("bout_sb", [P, D])
        rw_sb = sb("rw_sb", [P, DC, E])
        rb_sb = sb("rb_sb", [P, E])
        QN = sb("QN", [P, H, KVC + R])
        QN_flat = QN[:, :, :].rearrange("p a b -> p (a b)")
        QT = sb("QT", [P, BT, H, LQ])
        QT_flat = QT[:, :, :, :].rearrange("p a b c -> p (a b c)")
        xpT = sb("xpT", [P, BT, HPAIR, P])
        xpT_flat = xpT[:, :, :, :].rearrange("p a b c -> p (a b c)")
        big = sb("big", [P, 8192 + H * HD])
        flat_g = big[:, 0:8192]
        w_o_sb = flat_g[:, 2 * H * HD:].rearrange("p (h d) -> p h d", h=H)
        st_uqT = flat_g[:, 0:H * QC].rearrange("p (h n) -> p h n", h=H)
        st_kuvT = flat_g[:, H * HD:2 * H * HD].rearrange("p (k h n) -> p k h n", h=H, k=2)
        ident = sb("ident", [P, P])
        ones_f = sb("ones_f", [P, P])
        pick = sb("pick", [P, BT, 2, LQ], BF16)
        causal = sb("causal", [P, BT, LQ], BF16)
        head_of = sb("head_of", [P, P // SD])
        uqk_sb = sb("uqk_sb", [QC, H, KVC])
        uvo_sb = sb("uvo_sb", [P, H // 4, 2, D])
        w_qkvT = sb("w_qkvT", [P, DC, 3 * D])
        w_outT = sb("w_outT", [P, 2, D])
        neg_mask = sb("neg_mask", [P, NT, LK], BF16)
        key_iota = sb("key_iota", [P, LK])
        seg_f = sb("seg_f", [P, NT])
        e_iota = sb("e_iota", [P, E])
        half_neg = sb("half_neg", [P, 1])
        stats = sb("stats", [P, 2, 6])
        held = sb("held", [P, 1])
        mv = sb("mv", [P, 2, 2])
        rstd = sb("rstd", [P, 2, 2])
        xn = sb("xn", [P, D])
        xnT = sb("xnT", [P, DC, P])
        ctxT = sb("ctxT", [P, DC, BT, LK])
        qcT = sb("qcT", [QC, P])
        KK = sb("KK", [P, BT, LK])
        kr_a = sb("kr_a", [P, BT * LK])
        kr_b = sb("kr_b", [P, BT * LK])
        kv_nat = sb("kv_nat", [P, BT, KVC + 1])
        rt_b = sb("rt_b", [P, H, R])
        x_max = sb("x_max", [P, BT, HPAIR])
        x_rec = sb("x_rec", [P, BT, HPAIR])
        xp = sb("xp", [P, BT, HPAIR, LK])
        ON = sb("ON", [P, BT, HPAIR, KVC])
        OT = sb("OT", [P, H // 4, 2, BT, LQ])
        held_p = sb("held_p", [P, NT])
        an = sb("an", [P, D])
        anT = sb("anT", [P, DC, P])
        qT = sb("qT", [P, DC, P])
        kT = sb("kT", [P, DC, P])
        v_nat = sb("v_nat", [P, HPAIR, 2 * SD + 1])
        qbd = sb("qbd", [P, BT, DC, P // SD, LQ])
        a_max = sb("a_max", [P, BT, HPAIR])
        a_rec = sb("a_rec", [P, BT, HPAIR])
        ap = sb("ap", [P, HPAIR, BT, LQ])
        apT = sb("apT", [P, HPAIR, P])
        aON = sb("aON", [P, BT, HPAIR, SD])
        aOT = sb("aOT", [P, 2, BT, LQ])
        xT = sb("xT", [P, DC, NT, P])
        logit = sb("logit", [P, NT, E])
        biased = sb("biased", [P, NT, E])
        comb = sb("comb", [P, NT, E])
        chosen = sb("chosen", [P, NT, E])
        picked = sb("picked", [P, NT, E])
        slot_of = sb("slot_of", [P, NT, E])
        top_v = sb("top_v", [P, NT, 8])
        top_i = sb("top_i", [P, NT, 8], U32)
        top_f = sb("top_f", [P, NT, 8])
        row_s = sb("row_s", [P, 3, NT])
        silu = sb("silu", [P, 2, 512])
        hid = sb("hid", [P, 2, 512])
        hidT = sb("hidT", [P, 2, 512])
        GW = 512 * DC
        shared = big[:, 0:3 * GW]
        part_iota = sb("part_iota", [P, 1])
        tri = sb("tri", [P, P], BF16)
        ones_b = sb("ones_b", [P, P], BF16)
        slot_f = sb("slot_f", [P, TOPK, NT])
        slot_u = sb("slot_u", [P, TOPK, NT], U32)
        gate_j = sb("gate_j", [P, TOPK, NT])
        cnt_i = sb("cnt_i", [P, 2, E], I32)
        cnt_f = sb("cnt_f", [P, 3, E])
        eid_col = sb("eid_col", [P, 1])
        eid_i = sb("eid_i", [1, P], I32)
        uqk_flat = w_qkvT[:, :, :].rearrange("p c n -> p (c n)")
        w_blk = big[:, 3 * GW:3 * GW + QBUF * QB * WROW].rearrange("p (k j n) -> p k j n", k=QBUF, j=QB)
        spare = uqk_flat
        sil_q = spare[:, 0:QB * F].rearrange("p (j f) -> p j f", j=QB)
        hid_q = spare[:, 256:256 + 2 * QB * F].rearrange("p (j r f) -> p j r f", j=QB, r=2)
        hT_q = spare[:, 768:768 + QB * P]
        chosen_b = sb("chosen_b", [P, NT, E], BF16)
        ZW = 2048
        zeros = big[:, 3 * GW:3 * GW + ZW]
        x_blk = [QT_flat[:, 1024:2048], xpT_flat[:, 0:1024], xpT_flat[:, 1024:2048],
                 ON[:, :, :, :].rearrange("p a b c -> p (a b c)")]
        y_blk = [QN_flat[:, 0:1024], QN_flat[:, 1024:2048], QT_flat[:, 0:1024],
                 OT[:, :, :, :, :].rearrange("p a b c d -> p (a b c d)")]
        xT_q = rt_b[:, :, :].rearrange("p h r -> p (h r)")
        x3 = xp[:, :, :, :].rearrange("p a b c -> p (a b c)").rearrange("p (t d) -> p t d", t=NT)
        is_all = qbd[:, :, :, :, :].rearrange("p a b c d -> p (a b c d)").rearrange(
            "p (j t e) -> p j t e", j=TOPK, t=NT)
        y_got = uvo_sb[:, :, :, :].rearrange("p a b c -> p (a b c)")[:, 0:GB * D].rearrange("p (k d) -> p k d", k=GB)
        ps = stack.enter_context(nc.psum_tensor("ps", [P, 8, 512], F32))

        def bank(b):
            return ps[:, b, :]

        ld_r = sem("ld_r")
        ld_shared, zero_done, scattered = (sem(n) for n in ("ld_shared", "zero_done", "scattered"))
        route, route_ex, rank_pe, eid_pe, slots_ready, eid_ready = (sem(n) for n in (
            "route", "route_ex", "rank_pe", "eid_pe", "slots_ready", "eid_ready"))
        ld_tok = [sem(f"ld_tok{k}") for k in range(QBUF)]
        ld_exp = [sem(f"ld_exp{k}") for k in range(QBUF)]
        st_y = [sem(f"st_y{k}") for k in range(QBUF)]
        got = [sem(f"got{k}") for k in range(GB)]
        ld_x, ld_ctx, ld_w1, ld_w2, ld_small, ld_late, st_out = (sem(n) for n in (
            "ld_x", "ld_ctx", "ld_w1", "ld_w2", "ld_small", "ld_late", "st_out"))
        zeroed, consts, masks, mask_step = (sem(n) for n in ("zeroed", "consts", "masks", "mask_step"))
        su_pe, su_ev = sem("su_pe"), sem("su_ev")
        names = """x_stat x_aggr x_veps x_rstd x_norm x_nT_pe x_nT x_ctxT_pe x_ctxT x_kvT_pe x_kvT
            x_qcT_pe x_qcT x_kr_pe x_krb x_kr x_kvn_pe x_kvn x_q_pe x_q x_qr_pe x_sin0 x_sin1 x_qn0 x_qn1 x_qt_pe0 x_qt_pe1 x_qt_pe2 x_qt_pe3 x_qt0 x_qt1 x_qt2 x_qt3
            x_s0_pe x_s1_pe x_mx0 x_mx1 x_sub0 x_sub1 x_exp0 x_exp1
            x_pl0_pe x_ph0_pe x_pl1_pe x_ph1_pe x_pl0 x_ph0 x_pl1 x_ph1
            x_o0_pe x_o1_pe x_rec0 x_rec1 x_on0 x_on1 x_ot0_pe x_ot1_pe x_ot0 x_ot1 x_y_pe x_res
            a_stat a_aggr a_veps a_rstd a_norm a_nT_pe a_nT a_qk_pe a_q a_k a_qbd a_v_pe a_v
            a_s_pe a_mx a_sub a_exp a_pl_pe a_ph_pe a_pl a_ph a_o_pe a_rec a_on a_ot_pe a_ot
            a_y_pe a_res a_resb
            r_stat r_aggr r_veps r_rstd r_norm r_T_pe r_T r_l_pe""".split()
        names += ["f_gu_pe", "f_silu", "f_hid", "f_hT_pe", "f_hT", "f_y_pe", "f_acc", "q_xT_pe", "q_xT",
                  "q_up_pe", "q_silu", "q_hid", "q_hT_pe", "q_hT", "q_down_pe", "q_y", "combined"]
        S = {n: sem(n) for n in names}

        def done(eng, name, t):
            if isinstance(t, int) and t < 0:
                return
            eng.wait_ge(S[name], t + 1)

        ZEROS = NBLK * CAP * D // P // ZW

        def g_not_first(g):
            return not isinstance(g, int) or g >= QBUF

        xr = x.rearrange("b q d -> (b q) d").rearrange("(t p) d -> p t d", p=P)
        outr = out.rearrange("b q d -> (b q) d").rearrange("(t p) d -> p t d", p=P)
        ctxr = ctx.rearrange("(t b) k d -> t k b d", b=BT)
        

        def form_uqk(g):
            bk = bank(4 + g)
            return ([(bk[0:QC, j * KVC:(j + 1) * KVC], st_uqT[:, 4 * g + j, :], st_kuvT[:, 0, 4 * g + j, :])
                     for j in range(4)],
                    uqk_sb[:, 4 * g:4 * g + 4, :], bk[0:QC, 0:4 * KVC].rearrange("p (h n) -> p h n", h=4))

        def form_uvo(g):
            bk = bank(5 + g % 3)
            return ([(bk[(j // 2) * KVC:(j // 2 + 1) * KVC, (j % 2) * D:(j % 2 + 1) * D],
                      st_kuvT[:, 1, 4 * g + j, :], w_o_sb[:, 4 * g + j, :]) for j in range(4)],
                    uvo_sb[:, g, :, :], bk.rearrange("p (r d) -> p r d", r=2))
        SETUP = 8

        block = stack.enter_context(nc.Block())

        def interleave(steps, t_x, t_a):
            for kind, what in ORDER:
                if kind == "s" and t_a is None and kind in steps:
                    steps[kind](what)
                t = t_x if kind == "x" else None if kind == "s" else t_a
                if t is not None and (kind, what) in steps:
                    steps[(kind, what)](t)

        def run_tiles(eng, steps):
            interleave(steps, 0, None)
            interleave(steps, 1, 0)
            with eng.Fori(2, NT) as t:
                interleave(steps, t, t - 1)
            interleave(steps, None, NT - 1)

        def halves(buf):
            return buf[:, 0:GW], buf[:, GW:2 * GW], buf[:, 2 * GW:3 * GW].rearrange("p (n d) -> p n d", d=D)

        def run_quads(eng, step):
            for g in range(QBUF):
                step(g, g, 0)
            with eng.Fori(1, NQ // QBUF - 1) as i:
                for k in range(QBUF):
                    step(QBUF * i + k, k, i)
            for g in range(NQ - QBUF, NQ):
                step(g, g % QBUF, g // QBUF)

        def shared_hidden(eng, ops, u):
            k = u % 2
            done(eng, "f_silu", u)
            done(eng, "f_hT_pe", u - 2)
            done(eng, "f_hid", u - 1)
            ops.tensor_tensor(hid[:, k, :], silu[:, k, :], bank(2 + k), ALU.mult).then_inc(S["f_hid"], 1)

        def shared_result(eng, ops, u):
            done(eng, "f_y_pe", u)
            done(eng, "f_acc", u - 1)
            ops.tensor_tensor(x_sb[:, u, :], x_sb[:, u, :], bank(6)[:, 0:D],
                              ALU.add).then_inc(S["f_acc"], 1)

        @block.sync
        def _(sp):
            sp.dma_start(ctx_sb[:, :, :], ctxr[0]).then_inc(ld_ctx, 16)
            sp.dma_start(st_uqT, w_uqT).then_inc(ld_w1, 16)
            sp.dma_start(st_kuvT[:, 0, :, :], w_ukuvT[:, 0, :, :]).then_inc(ld_w1, 16)
            sp.dma_start(w_qr_sb[:, :], w_qr).then_inc(ld_w1, 16)
            sp.dma_start(st_kuvT[:, 1, :, :], w_ukuvT[:, 1, :, :]).then_inc(ld_late, 16)
            sp.dma_start(w_o_sb, w_o.rearrange("(h p) d -> p h d", p=HD)).then_inc(ld_late, 16)
            sp.dma_start(w_qkvT[:, :, :], w_qkv_T).then_inc(ld_late, 16)
            sp.dma_start(w_outT[:, :, :], w_out_T).then_inc(ld_late, 16)
            sp.dma_start(bqk_sb[:, :], b_qk).then_inc(ld_late, 16)
            sp.dma_start(bv_sb[:, :], b_v.rearrange("(o d) -> o d", o=1).to_broadcast([P, D])).then_inc(ld_late, 16)
            sp.dma_start(bout_sb[:, :], b_out.rearrange("(o d) -> o d", o=1).to_broadcast([P, D])).then_inc(ld_late, 16)
            sp.dma_start(x_sb[:, 1:, :], xr[:, 1:, :]).then_inc(ld_late, 16)
            sp.dma_start(rb_sb[:, :], router_b.rearrange("(o e) -> o e", o=1).to_broadcast([P, E])).then_inc(ld_r, 16)
            sp.dma_start(rw_sb[:, :, :], router_w.rearrange("(p c) e -> p c e", c=DC)).then_inc(ld_r, 16)
            with sp.Fori(1, NT) as t:
                done(sp, "x_ctxT_pe", t - 1)
                sp.dma_start(ctx_sb[:, :, :], ctxr[t]).then_inc(ld_ctx, 16)
            sp.wait_ge(su_ev, SETUP)
            gate, up, down = halves(shared)
            for dst, src in ((gate, swg), (up, swu)):
                sp.dma_start(dst.rearrange("p (s n) -> p s n", s=NSH),
                             src.rearrange("s (p c) h -> p s (c h)", c=DC)).then_inc(ld_shared, 16)
            sp.dma_start(down, swd.rearrange("s (n p) d -> p (s n) d", p=P)).then_inc(ld_shared, 16)
            sp.wait_ge(su_ev, SETUP + 1)
            xs_flat = xs.rearrange("(p r) d -> p (r d)", p=P)
            for n in range(ZEROS):
                sp.dma_start(xs_flat[:, n * ZW:(n + 1) * ZW], zeros).then_inc(zero_done, 16)

            picks = [sp.alloc_register(f"expert{j}") for j in range(QB)]

            def load_tokens(g, k):
                if g_not_first(g):
                    done(sp, "q_xT_pe", g - QBUF)
                sp.dma_start(x_blk[k].rearrange("p (j d) -> p j d", j=QB),
                             xs.rearrange("(g j p) d -> g p j d", j=QB, p=P)[g]).then_inc(ld_tok[k], 16)

            def load_quad(g, k, _):
                if g_not_first(g):
                    done(sp, "q_down_pe", g - QBUF)
                sp.load(picks, eid_i[0:1, bass.ds(QB * g, QB)])
                for j in range(QB):
                    e = sp.snap(picks[j], min_val=0, max_val=E - 1)
                    sp.dma_start(w_blk[:, k, j, :], w_exp[bass.ds(e, 1), :, :].rearrange("o p n -> p (o n)")).then_inc(ld_exp[k], 16)
                if not (isinstance(g, int) and g == NQ - 1):
                    if isinstance(g, int) and g == 0:
                        sp.wait_ge(scattered, 16 * TOPK * NT)
                        load_tokens(0, 0)
                    load_tokens(g + 1, (k + 1) % QBUF)
            sp.wait_ge(zero_done, 16 * ZEROS)
            sp.wait_ge(eid_ready, 1)
            run_quads(sp, load_quad)
            for t in range(NT):
                done(sp, "combined", TOPK * t + TOPK - 1)
                sp.dma_start(outr[:, t, :], x_sb[:, t, :]).then_inc(st_out, 16)
            sp.wait_ge(st_out, 16 * NT)

        @block.gpsimd
        def _(pool):
            g = nc.gpsimd
            g.memset(ident[:, :], 0.0).then_inc(zeroed, 1)
            g.memset(ones_f[:, :], 1.0).then_inc(zeroed, 1)
            g.memset(pick[:, :, :, :], 0.0).then_inc(zeroed, 1)
            g.memset(causal[:, :, :], 0.0).then_inc(zeroed, 1)
            g.memset(half_neg[:, :], -0.5).then_inc(zeroed, 1)
            g.memset(kv_nat[:, :, KVC:KVC + 1], 1.0).then_inc(consts, 1)
            g.memset(v_nat[:, :, 2 * SD:2 * SD + 1], 1.0).then_inc(consts, 1)
            g.iota(key_iota[:, :], pattern=[[1, LK]], base=0, channel_multiplier=0,
                   allow_small_or_imprecise_dtypes=True).then_inc(consts, 1)
            g.iota(e_iota[:, :], pattern=[[1, E]], base=0, channel_multiplier=0,
                   allow_small_or_imprecise_dtypes=True).then_inc(consts, 1)
            g.memset(ones_b[:, :], 1.0).then_inc(zeroed, 1)
            g.iota(part_iota[:, :], pattern=[[0, 1]], base=0, channel_multiplier=1,
                   allow_small_or_imprecise_dtypes=True).then_inc(consts, 1)
            pool.wait_ge(zeroed, 6)
            g.affine_select(out=tri[:, :], in_=ones_b[:, :], compare_op=ALU.is_ge, fill=0.0,
                            base=-1, pattern=[[1, P]], channel_multiplier=-1).then_inc(consts, 1)
            g.affine_select(out=ident[:, :], in_=ident[:, :], compare_op=ALU.not_equal, fill=1.0,
                            base=0, pattern=[[-1, P]], channel_multiplier=1).then_inc(consts, 1)
            for b in range(BT):
                g.affine_select(out=pick[:, b, :, :], in_=pick[:, b, :, :], compare_op=ALU.not_equal,
                                fill=1.0, base=-LQ * b, pattern=[[0, 2], [-1, LQ]],
                                channel_multiplier=1).then_inc(consts, 1)
            g.affine_select(out=causal[:, :, :], in_=causal[:, :, :], compare_op=ALU.is_ge,
                            fill=NEG, base=0, pattern=[[-LQ, BT], [-1, LQ]],
                            channel_multiplier=1).then_inc(consts, 1)
            g.affine_select(out=head_of[:, :], in_=ones_f[:, 0:P // SD], compare_op=ALU.is_ge,
                            fill=0.0, base=0, pattern=[[-SD, P // SD]],
                            channel_multiplier=1).then_inc(mask_step, 1)
            pool.wait_ge(mask_step, 1)
            g.affine_select(out=head_of[:, :], in_=head_of[:, :], compare_op=ALU.is_ge,
                            fill=0.0, base=SD - 1, pattern=[[SD, P // SD]],
                            channel_multiplier=-1).then_inc(consts, 1)

            def x_rstd(t):
                done(pool, "x_veps", t)
                g.tensor_tensor(rstd[:, 0, 1:2], rstd[:, 0, 0:1], half_neg[:, :], ALU.pow).then_inc(S["x_rstd"], 1)

            def x_qn(t):
                done(pool, "x_sin0", t)
                hh = H // 2
                g.tensor_tensor(QN[:, 0:hh, KVC:], QN[:, 0:hh, KVC:], rt_b[:, 0:hh, :], ALU.add).then_inc(S["x_qn0"], 1)

            def a_rstd(t):
                done(pool, "a_veps", t)
                g.tensor_tensor(rstd[:, 1, 1:2], rstd[:, 1, 0:1], half_neg[:, :], ALU.pow).then_inc(S["a_rstd"], 1)

            def a_qbd(t):
                done(pool, "a_q", t)
                done(pool, "a_s_pe", t - 1)
                for b in range(BT):
                    for c in range(DC):
                        last = g.tensor_tensor(
                            qbd[:, b, c, :, :],
                            qT[:, c, b * LQ:(b + 1) * LQ].unsqueeze(1).to_broadcast([P, P // SD, LQ]),
                            head_of[:, :].unsqueeze(2).to_broadcast([P, P // SD, LQ]), ALU.mult)
                        last.then_inc(S["a_qbd"], 1)

            def a_resb(t):
                done(pool, "x_res", t)
                done(pool, "a_stat", t)
                done(pool, "a_norm", t)
                if isinstance(t, int) and t == 0:
                    pool.wait_ge(ld_late, 16 * LATE)
                g.tensor_tensor(x_sb[:, t, :], x_sb[:, t, :], bout_sb[:, :], ALU.add).then_inc(S["a_resb"], 1)

            run_tiles(pool, {("x", 1): x_rstd, ("x", 8): x_qn,
                             ("a", 0): a_rstd, ("a", 2): a_qbd, ("a", 3): a_resb})

            for t in range(NT):
                done(pool, "r_veps", t)
                g.tensor_tensor(rstd[:, 0, 1:2], rstd[:, 0, 0:1], half_neg[:, :], ALU.pow).then_inc(S["r_rstd"], 1)

            pool.wait_ge(zero_done, 16 * ZEROS)
            pool.wait_ge(slots_ready, 1)
            for t in range(NT):
                for j in range(TOPK):
                    g.indirect_dma_start(
                        out=xs, out_offset=bass.IndirectOffsetOnAxis(ap=slot_u[:, j, t:t + 1], axis=0),
                        in_=x3[:, t, :], in_offset=None).then_inc(scattered, 16)

            def store_quad(gq, k, _):
                done(pool, "q_y", gq)
                pool.dma_start(ys.rearrange("(g j p) d -> g p j d", j=QB, p=P)[gq],
                               y_blk[k].rearrange("p (j d) -> p j d", j=QB)).then_inc(st_y[k], 16)
            run_quads(pool, store_quad)

            for k in range(QBUF):
                pool.wait_ge(st_y[k], 16 * (NQ // QBUF))
            for n in range(TOPK * NT):
                t, j = divmod(n, TOPK)
                done(pool, "combined", n - GB)
                g.indirect_dma_start(
                    out=y_got[:, n % GB, :], out_offset=None, in_=ys,
                    in_offset=bass.IndirectOffsetOnAxis(ap=slot_u[:, j, t:t + 1], axis=0)).then_inc(got[n % GB], 16)

        @block.vector
        def _(dve):
            v = nc.vector

            def turned_key_weights():
                dve.wait_ge(ld_w2, 48)
                v.tensor_scalar(w_kr_rot[:, 0:HALF], w_kr_sb[:, HALF:R], -1.0, None, ALU.mult).then_inc(masks, 1)
                v.tensor_copy(w_kr_rot[:, HALF:R], w_kr_sb[:, 0:HALF]).then_inc(masks, 1)

            def band_masks():
                dve.wait_ge(ld_small, 48)
                dve.wait_ge(consts, 11)
                v.tensor_copy(seg_f[:, :], seg_i[:, :]).then_inc(masks, 1)
                dve.wait_ge(masks, 3)
                dist = xp[:, 0, :, :].rearrange("p h k -> p (h k)").rearrange("p (t k) -> p t k", t=NT)
                dist2 = rt_b[:, :, :].rearrange("p h r -> p (h r)").rearrange("p (t k) -> p t k", t=NT)
                v.tensor_tensor(dist, key_iota[:, :].unsqueeze(1).to_broadcast([P, NT, LK]),
                                seg_f[:, :].unsqueeze(2).to_broadcast([P, NT, LK]), ALU.subtract).then_inc(masks, 1)
                dve.wait_ge(masks, 4)
                v.tensor_scalar(dist2, dist, 0.0, NEG, ALU.is_gt, ALU.mult).then_inc(masks, 1)
                v.tensor_scalar(dist, dist, float(-LOOKBACK), NEG, ALU.is_lt, ALU.mult).then_inc(masks, 1)
                dve.wait_ge(masks, 6)
                v.tensor_tensor(neg_mask[:, :, :], dist, dist2, ALU.add).then_inc(masks, 1)
                dve.wait_ge(masks, 7)

            def keep(n, formed):
                _, dst, src = formed
                dve.wait_ge(su_pe, n + 1)
                v.tensor_copy(dst, src).then_inc(su_ev, 1)

            def s_uvo(g):
                keep(4 + g, form_uvo(g))
                if g == 3:
                    v.memset(zeros, 0.0).then_inc(su_ev, 1)

            def norm_stats(t, k, pre, before):
                if before:
                    done(dve, before, t)
                elif isinstance(t, int):
                    dve.wait_ge(*((ld_x, 16) if t == 0 else (ld_late, 16 * LATE)))
                v.memset(held[:, :], 0.0)
                v.bn_stats(stats[:, k, :], x_sb[:, t, :]).then_inc(S[pre + "_stat"], 1)
                done(dve, pre + "_stat", t)
                v.memset(held[:, :], 0.0)
                v.bn_aggr(mv[:, k, :], stats[:, k, :]).then_inc(S[pre + "_aggr"], 1)
                done(dve, pre + "_aggr", t)
                v.tensor_scalar(rstd[:, k, 0:1], mv[:, k, 1:2], EPS, None, ALU.add).then_inc(S[pre + "_veps"], 1)

            def norm_apply(t, k, pre, dst, reader):
                done(dve, pre + "_rstd", t)
                done(dve, reader, t - 1)
                v.tensor_scalar(dst[:, :], x_sb[:, t, :], mv[:, k, 0:1], rstd[:, k, 1:2],
                                ALU.subtract, ALU.mult).then_inc(S[pre + "_norm"], 1)

            def x_norm(t):
                norm_stats(t, 0, "x", None)
                norm_apply(t, 0, "x", xn, "x_nT_pe")
                if isinstance(t, int) and t == 0:
                    turned_key_weights()

            def x_nT(t):
                done(dve, "x_nT_pe", t)
                done(dve, "x_qcT_pe", t - 1)
                v.tensor_copy(xnT[:, :, :], bank(1)[:, 0:DC * P].rearrange("p (c n) -> p c n", c=DC)).then_inc(S["x_nT"], 1)

            def x_qcT(t):
                done(dve, "x_qcT_pe", t)
                done(dve, "x_qr_pe", t - 1)
                v.tensor_copy(qcT[:, :], bank(3)[0:QC, 0:P]).then_inc(S["x_qcT"], 1)

            def x_kr(t):
                done(dve, "x_kr_pe", t)
                if isinstance(t, int) and t == 0:
                    dve.wait_ge(ld_small, 48)
                v.tensor_tensor(kr_a[KVC:P, :], bank(0)[KVC:P, 0:BT * LK], rope_k_sb[KVC:P, 0, :], ALU.mult)
                v.tensor_tensor(kr_b[KVC:P, :], bank(0)[KVC:P, BT * LK:2 * BT * LK], rope_k_sb[KVC:P, 1, :], ALU.mult).then_inc(S["x_krb"], 1)
                done(dve, "x_krb", t)
                done(dve, "x_s1_pe", t - 1)
                v.tensor_tensor(KK[KVC:P, :, :], kr_a[KVC:P, :].rearrange("p (b k) -> p b k", b=BT),
                                kr_b[KVC:P, :].rearrange("p (b k) -> p b k", b=BT), ALU.add).then_inc(S["x_kr"], 1)
                if isinstance(t, int) and t == 0:
                    for g in range(4):
                        keep(g, form_uqk(g))
                    band_masks()

            def x_rope(t):
                done(dve, "x_qr_pe", t)
                done(dve, "x_qt_pe3", t - 1)
                hh = H // 2
                for n, b in enumerate((4, 0)):
                    src = bank(b).rearrange("p (h r) -> p h r", h=hh)
                    hs = slice(hh * n, hh * n + hh)
                    cos = rope_q_sb[:, 0, :].unsqueeze(1).to_broadcast([P, hh, R])
                    v.tensor_tensor(QN[:, hs, KVC:], src, cos, ALU.mult)
                    done(dve, f"x_qn{n}", t - 1)
                    for lo, hi in ((0, HALF), (HALF, 0)):
                        sin = rope_q_sb[:, 1, lo:lo + HALF].unsqueeze(1).to_broadcast([P, hh, HALF])
                        last = v.tensor_tensor(rt_b[:, hs, lo:lo + HALF], src[:, :, hi:hi + HALF], sin, ALU.mult)
                    last.then_inc(S[f"x_sin{n}"], 1)
                done(dve, "x_sin1", t)
                v.tensor_tensor(QN[:, hh:, KVC:], QN[:, hh:, KVC:], rt_b[:, hh:, :], ALU.add).then_inc(S["x_qn1"], 1)

            def x_soft(t, b):
                s = ps[:, 2 * b:2 * b + 2, :].rearrange("p a (h k) -> p (a h) k", k=LK)
                done(dve, f"x_s{b}_pe", t)
                v.tensor_reduce(x_max[:, b, :], s, AX.X, ALU.max).then_inc(S[f"x_mx{b}"], 1)
                done(dve, f"x_mx{b}", t)
                done(dve, f"x_ph{b}_pe", t - 1)
                v.tensor_tensor(xp[:, b, :, :], s, x_max[:, b, :].unsqueeze(2).to_broadcast([P, HPAIR, LK]),
                                ALU.subtract).then_inc(S[f"x_sub{b}"], 1)

            def x_ph(t, b):
                done(dve, f"x_ph{b}_pe", t)
                done(dve, f"x_o{b}_pe", t - 1)
                v.tensor_copy(xpT[:, b, 4:8, :], bank((0, 2)[b]).rearrange("p (h n) -> p h n", h=4)).then_inc(S[f"x_ph{b}"], 1)

            def x_on(t, b):
                banks = ((1, 4), (3, 0))[b]
                done(dve, f"x_o{b}_pe", t)
                for n, k in enumerate(banks):
                    o = bank(k)[:, 0:4 * (KVC + 1)].rearrange("p (h c) -> p h c", h=4)
                    v.reciprocal(x_rec[:, b, 4 * n:4 * n + 4], o[:, :, KVC]).then_inc(S[f"x_rec{b}"], 1)
                dve.wait_ge(S[f"x_rec{b}"], 2 * t + 2)
                done(dve, f"x_ot{b}_pe", t - 1)
                for n, k in enumerate(banks):
                    o = bank(k)[:, 0:4 * (KVC + 1)].rearrange("p (h c) -> p h c", h=4)
                    last = v.tensor_tensor(ON[:, b, 4 * n:4 * n + 4, :], o[:, :, 0:KVC],
                                           x_rec[:, b, 4 * n:4 * n + 4].unsqueeze(2).to_broadcast([P, 4, KVC]), ALU.mult)
                last.then_inc(S[f"x_on{b}"], 1)

            def x_res(t):
                done(dve, "x_y_pe", t)
                done(dve, "x_norm", t)
                v.tensor_tensor(x_sb[:, t, :], x_sb[:, t, :], bank(4)[:, 0:D], ALU.add).then_inc(S["x_res"], 1)

            def a_stats(t):
                norm_stats(t, 1, "a", "x_res")

            def a_norm(t):
                norm_apply(t, 1, "a", an, "a_nT_pe")

            def a_nT(t):
                done(dve, "a_nT_pe", t)
                done(dve, "a_v_pe", t - 1)
                v.tensor_copy(anT[:, :, :], bank(5)[:, 0:DC * P].rearrange("p (c n) -> p c n", c=DC)).then_inc(S["a_nT"], 1)

            def a_v(t):
                done(dve, "a_v_pe", t)
                done(dve, "a_o_pe", t - 1)
                v.tensor_tensor(v_nat[:, :, 0:2 * SD], bank(7)[:, 0:D].rearrange("p (h d) -> p h d", h=HPAIR),
                                bv_sb[:, :].rearrange("p (h d) -> p h d", h=HPAIR), ALU.add).then_inc(S["a_v"], 1)

            def a_soft(t):
                s = ps[:, 5:7, :].rearrange("p b (h k) -> p b h k", k=LQ)
                done(dve, "a_s_pe", t)
                v.tensor_reduce(a_max[:, :, :], s, AX.X, ALU.max).then_inc(S["a_mx"], 1)
                done(dve, "a_mx", t)
                done(dve, "a_ph_pe", t - 1)
                for b in range(BT):
                    last = v.tensor_tensor(ap[:, :, b, :], s[:, b, :, :],
                                           a_max[:, b, :].unsqueeze(2).to_broadcast([P, HPAIR, LQ]), ALU.subtract)
                last.then_inc(S["a_sub"], 1)

            def a_on(t):
                w = 2 * SD + 1
                o = ps[:, 6:8, 0:HPAIR * w].rearrange("p b (h d) -> p b h d", h=HPAIR)
                done(dve, "a_o_pe", t)
                v.reciprocal(a_rec[:, :, :], o[:, :, :, 2 * SD]).then_inc(S["a_rec"], 1)
                done(dve, "a_rec", t)
                done(dve, "a_ot_pe", t - 1)
                for par in range(2):
                    rows = slice(LQ * par, LQ * par + LQ)
                    last = v.tensor_tensor(
                        aON[rows, :, :, :], o[rows, :, :, SD * par:SD * par + SD],
                        a_rec[rows, :, :].unsqueeze(3).to_broadcast([LQ, BT, HPAIR, SD]), ALU.mult)
                last.then_inc(S["a_on"], 1)

            def a_res(t):
                done(dve, "a_y_pe", t)
                done(dve, "a_resb", t)
                v.tensor_tensor(x_sb[:, t, :], x_sb[:, t, :], bank(6)[:, 0:D], ALU.add).then_inc(S["a_res"], 1)

            run_tiles(dve, {
                "s": s_uvo,
                ("x", 1): x_norm, ("x", 2): x_nT, ("a", 0): a_stats, ("x", 4): x_qcT, ("a", 0.5): a_norm, ("a", 1): a_nT,
                ("x", 6): x_kr, ("a", 3): a_v, ("x", 8): x_rope, ("a", 4.5): a_soft,
                ("x", 10): lambda t: x_soft(t, 0), ("x", 11): lambda t: x_soft(t, 1),
                ("x", 12): lambda t: x_ph(t, 0), ("x", 14): lambda t: x_ph(t, 1),
                ("x", 13): lambda t: x_on(t, 0), ("a", 6): a_on,
                ("x", 15): lambda t: x_on(t, 1), ("a", 8): a_res, ("y", 18): x_res})

            for t in range(NT):
                norm_stats(t, 0, "r", "a_res")
                done(dve, "r_rstd", t)
                v.tensor_scalar(x3[:, t, :], x_sb[:, t, :], mv[:, 0, 0:1], rstd[:, 0, 1:2],
                                ALU.subtract, ALU.mult).then_inc(S["r_norm"], 1)
            dve.wait_ge(S["r_l_pe"], NT)
            dve.wait_ge(ld_r, 32)
            steps = [0]

            def link(ins):
                steps[0] += 1
                ins.then_inc(route, 1)
                dve.wait_ge(route, steps[0])

            def over_e(a):
                return a.unsqueeze(2).to_broadcast([P, NT, E])

            link(v.tensor_copy(logit[:, :, :], bank(1).rearrange("p (t e) -> p t e", t=NT)))
            link(v.tensor_tensor(biased[:, :, :], logit[:, :, :],
                                 rb_sb[:, :].unsqueeze(1).to_broadcast([P, NT, E]), ALU.add))
            link(v.tensor_reduce(row_s[:, 0, :], logit[:, :, :], AX.X, ALU.max))
            link(v.tensor_tensor(logit[:, :, :], logit[:, :, :], over_e(row_s[:, 0, :]), ALU.subtract))
            for t in range(NT):
                link(v.max(top_v[:, t, :], biased[:, t, :]))
                link(v.max_index(top_i[:, t, :], top_v[:, t, :], biased[:, t, :]))
            link(v.tensor_copy(top_f[:, :, :], top_i[:, :, :]))
            for j in range(TOPK):
                link(v.tensor_tensor(is_all[:, j, :, :], e_iota[:, :].unsqueeze(1).to_broadcast([P, NT, E]),
                                     over_e(top_f[:, :, j]), ALU.is_equal))
            link(v.tensor_tensor(chosen[:, :, :], is_all[:, 0, :, :], is_all[:, 1, :, :], ALU.add))
            link(v.tensor_tensor(picked[:, :, :], is_all[:, 2, :, :], is_all[:, 3, :, :], ALU.add))
            link(v.tensor_tensor(chosen[:, :, :], chosen[:, :, :], picked[:, :, :], ALU.add))
            link(v.tensor_copy(chosen_b[:, :, :], chosen[:, :, :]))
            assert steps[0] == CHOSEN_STEPS, steps

            for u in range(LEAD):
                shared_hidden(dve, v, u)

            dve.wait_ge(rank_pe, 1)
            link(v.tensor_copy(cnt_i[:, 0, :], bank(5)[:, 0:E]))
            link(v.tensor_scalar(cnt_i[:, 1, :], cnt_i[:, 0, :], CAP - 1, None, ALU.add))
            link(v.tensor_scalar(cnt_i[:, 0, :], cnt_i[:, 1, :], CAP.bit_length() - 1, None, ALU.logical_shift_right))
            link(v.tensor_copy(cnt_f[:, 2, :], cnt_i[:, 0, :]))
            link(v.tensor_copy(cnt_f[:, 0, :], cnt_i[:, 0, :]))
            src, step = 0, 1
            while step < E:
                dst = 1 - src
                v.tensor_copy(cnt_f[:, dst, 0:step], cnt_f[:, src, 0:step]).then_inc(route, 1)
                steps[0] += 1
                link(v.tensor_tensor(cnt_f[:, dst, step:], cnt_f[:, src, step:], cnt_f[:, src, 0:E - step], ALU.add))
                src, step = dst, 2 * step
            ends = cnt_f[:, src, :]
            firsts = cnt_f[:, 1 - src, :]
            link(v.tensor_tensor(firsts, ends, cnt_f[:, 2, :], ALU.subtract))
            link(v.tensor_scalar(cnt_f[:, 2, :], ends, part_iota[:, 0:1], None, ALU.is_le))
            link(v.tensor_reduce(eid_col[:, :], cnt_f[:, 2, :], AX.X, ALU.add))
            link(v.tensor_scalar(eid_col[:, :], eid_col[:, :], float(E - 1), None, ALU.min))
            link(v.tensor_scalar(firsts, firsts, float(CAP), None, ALU.mult))
            assert steps[0] == EID_STEPS, steps
            link(v.tensor_tensor(slot_of[:, :, :], bank(7).rearrange("p (t e) -> p t e", t=NT),
                                 firsts.unsqueeze(1).to_broadcast([P, NT, E]), ALU.add))
            for j in range(TOPK):
                link(v.tensor_tensor(picked[:, :, :], is_all[:, j, :, :], slot_of[:, :, :], ALU.mult))
                link(v.tensor_reduce(slot_f[:, j, :], picked[:, :, :], AX.X, ALU.add))
            v.tensor_copy(slot_u[:, :, :], slot_f[:, :, :]).then_inc(slots_ready, 1)
            dve.wait_ge(eid_pe, 1)
            v.tensor_copy(eid_i[:, :], bank(5)[0:1, 0:P]).then_inc(eid_ready, 1)

            for u in range(LEAD, NT):
                shared_hidden(dve, v, u)
                shared_result(dve, v, u - 2)
            shared_result(dve, v, NT - 2)
            shared_result(dve, v, NT - 1)

            dve.wait_ge(route_ex, 1)
            link(v.tensor_tensor(comb[:, :, :], chosen[:, :, :], logit[:, :, :], ALU.mult))
            link(v.tensor_reduce(row_s[:, 1, :], comb[:, :, :], AX.X, ALU.add))
            link(v.reciprocal(row_s[:, 2, :], row_s[:, 1, :]))
            link(v.tensor_tensor(comb[:, :, :], comb[:, :, :], over_e(row_s[:, 2, :]), ALU.mult))
            for j in range(TOPK):
                link(v.tensor_tensor(picked[:, :, :], is_all[:, j, :, :], comb[:, :, :], ALU.mult))
                link(v.tensor_reduce(gate_j[:, j, :], picked[:, :, :], AX.X, ALU.add))

            def quad(g, k, i):
                done(dve, "q_silu", g)
                done(dve, "q_hT_pe", g - 1)
                up = bank(2).rearrange("p (j w f) -> p j w f", j=QB, w=2)[:, :, 1, :]
                v.tensor_tensor(hid_q, sil_q.unsqueeze(2).to_broadcast([P, QB, 2, F]),
                                up.unsqueeze(2).to_broadcast([P, QB, 2, F]), ALU.mult).then_inc(S["q_hid"], 1)
                if not (isinstance(g, int) and g < 1):
                    y_copy(g - 1, (k - 1) % QBUF, i if k else i - 1)
                done(dve, "q_hT_pe", g)
                done(dve, "q_down_pe", g - 1)
                v.tensor_copy(hT_q, bank(3)).then_inc(S["q_hT"], 1)

            def y_copy(g, k, i):
                done(dve, "q_down_pe", g)
                if g_not_first(g):
                    dve.wait_ge(st_y[k], 16 * i)
                v.tensor_copy(y_blk[k].rearrange("p (j h n) -> p h j n", j=QB, h=2),
                              ps[:, 4:6, :].rearrange("p h (j n) -> p h j n", j=QB)).then_inc(S["q_y"], 1)
            run_quads(dve, quad)
            y_copy(NQ - 1, QBUF - 1, NQ // QBUF - 1)

            for n in range(TOPK * NT):
                t, j = divmod(n, TOPK)
                dve.wait_ge(got[n % GB], 16 * (n // GB + 1))
                done(dve, "combined", n - 1)
                v.scalar_tensor_tensor(x_sb[:, t, :], y_got[:, n % GB, :], gate_j[:, j, t:t + 1], x_sb[:, t, :],
                                       ALU.mult, ALU.add).then_inc(S["combined"], 1)

        @block.scalar
        def _(act):
            s = nc.scalar
            for dst, src, s_ld in (
                    (x_sb[:, 0, :], xr[:, 0, :], ld_x),
                    (w_kvc_sb[:, :, :], w_kvc.rearrange("(c p) n -> p c n", p=P), ld_w2),
                    (w_dq_sb[:, :, :], w_dq.rearrange("(c p) n -> p c n", p=P), ld_w2),
                    (w_kr_sb[:, :], w_kr, ld_w2), (rope_k_sb[KVC:P, :, :], rope_k, ld_small),
                    (seg_i[:, :], seg, ld_small), (rope_q_sb[:, :, :], rope_q, ld_small)):
                act.dma_start(dst, src).then_inc(s_ld, 16)

            def x_ctxT(t):
                done(act, "x_ctxT_pe", t)
                done(act, "x_kvT_pe", t - 1)
                s.copy(ctxT[:, :, :, :], bank(0).rearrange("p (c b k) -> p c b k", c=DC, b=BT)).then_inc(S["x_ctxT"], 1)

            def x_kvT(t):
                done(act, "x_kvT_pe", t)
                done(act, "x_s1_pe", t - 1)
                s.copy(KK[0:KVC, :, :], bank(2)[0:KVC, 0:BT * LK].rearrange("p (b k) -> p b k", b=BT)).then_inc(S["x_kvT"], 1)

            def x_kvn(t):
                done(act, "x_kvn_pe", t)
                done(act, "x_o1_pe", t - 1)
                if isinstance(t, int) and t == 0:
                    act.wait_ge(consts, 11)
                s.copy(kv_nat[:, :, 0:KVC], bank(1)[:, 0:BT * KVC].rearrange("p (b c) -> p b c", b=BT)).then_inc(S["x_kvn"], 1)

            def x_q(t):
                done(act, "x_q_pe", t)
                done(act, "x_qt_pe3", t - 1)
                s.copy(QN[:, :, 0:KVC], ps[:, 2:4, :].rearrange("p a (h c) -> p (a h) c", c=KVC)).then_inc(S["x_q"], 1)

            def x_qt(t):
                for g in range(4):
                    done(act, f"x_qt_pe{g}", t)
                    if g == 0:
                        done(act, "x_s1_pe", t - 1)
                    s.copy(QT[:, :, 4 * g:4 * g + 4, :],
                           bank(1 + g).rearrange("p (h b q) -> p b h q", h=4, b=BT)).then_inc(S[f"x_qt{g}"], 1)

            def x_exp(t, b):
                done(act, f"x_sub{b}", t)
                s.activation(xp[:, b, :, :], xp[:, b, :, :], ACT.Exp, scale=XSCALE).then_inc(S[f"x_exp{b}"], 1)

            def x_pl(t, b):
                done(act, f"x_pl{b}_pe", t)
                done(act, f"x_o{b}_pe", t - 1)
                s.copy(xpT[:, b, 0:4, :], bank((4, 0)[b]).rearrange("p (h n) -> p h n", h=4)).then_inc(S[f"x_pl{b}"], 1)

            def x_ot(t, b):
                done(act, f"x_ot{b}_pe", t)
                done(act, "x_y_pe", t - 1)
                s.copy(OT[:, :, :, b, :], bank((1, 2)[b]).rearrange("p (k r q) -> p k r q", k=H // 4, r=2)).then_inc(S[f"x_ot{b}"], 1)

            def a_qk(t):
                done(act, "a_qk_pe", t)
                if not isinstance(t, int) or t > 0:
                    act.wait_ge(S["a_qbd"], 4 * t)
                q = bank(6).rearrange("p (c n) -> p c n", c=2 * DC)
                for c in range(DC):
                    last = s.activation(qT[:, c, :], q[:, c, :], ACT.Identity, bias=bqk_sb[:, c:c + 1])
                last.then_inc(S["a_q"], 1)
                done(act, "a_s_pe", t - 1)
                for c in range(DC):
                    last = s.activation(kT[:, c, :], q[:, DC + c, :], ACT.Identity, bias=bqk_sb[:, DC + c:DC + c + 1])
                last.then_inc(S["a_k"], 1)

            def a_exp(t):
                done(act, "a_sub", t)
                s.activation(ap[:, :, :, :], ap[:, :, :, :], ACT.Exp, scale=ASCALE).then_inc(S["a_exp"], 1)

            def a_pl(t):
                done(act, "a_pl_pe", t)
                done(act, "a_o_pe", t - 1)
                s.copy(apT[:, 0:4, :], bank(7).rearrange("p (h n) -> p h n", h=4)).then_inc(S["a_pl"], 1)
                done(act, "a_ph_pe", t)
                s.copy(apT[:, 4:8, :], bank(5).rearrange("p (h n) -> p h n", h=4)).then_inc(S["a_ph"], 1)

            def a_ot(t):
                done(act, "a_ot_pe", t)
                done(act, "a_y_pe", t - 1)
                s.copy(aOT[:, :, :, :], bank(5)[:, 0:2 * P].rearrange("p (b r q) -> p r b q", b=BT, r=2)).then_inc(S["a_ot"], 1)

            run_tiles(act, {
                ("x", 1): x_ctxT, ("x", 3): x_kvT, ("a", 2): a_qk, ("x", 5): x_kvn, ("x", 7): x_q,
                ("x", 9): x_qt, ("a", 4.7): a_exp, ("x", 10): lambda t: x_exp(t, 0),
                ("x", 12.5): lambda t: x_exp(t, 1), ("a", 5): a_pl,
                ("x", 12): lambda t: x_pl(t, 0), ("x", 14): lambda t: x_pl(t, 1),
                ("a", 7): a_ot, ("x", 16): lambda t: x_ot(t, 0), ("x", 17): lambda t: x_ot(t, 1)})

            for t in range(NT):
                done(act, "r_T_pe", t)
                s.copy(xT[:, :, t, :], bank(0)[:, 0:DC * P].rearrange("p (c n) -> p c n", c=DC)).then_inc(S["r_T"], 1)
            act.wait_ge(route, 4)
            s.activation(logit[:, :, :], logit[:, :, :], ACT.Exp).then_inc(route_ex, 1)

            def turned(u):
                done(act, "f_hT_pe", u)
                done(act, "f_y_pe", u - 2)
                s.copy(hidT[:, u % 2, :], bank(4)).then_inc(S["f_hT"], 1)
            for u in range(NT):
                done(act, "f_gu_pe", u)
                done(act, "f_hid", u - 2)
                s.activation(silu[:, u % 2, :], bank(u % 2), ACT.Silu).then_inc(S["f_silu"], 1)
                if u > 0:
                    turned(u - 1)
            turned(NT - 1)

            def xT_copy(g):
                done(act, "q_xT_pe", g)
                done(act, "q_up_pe", g - 1)
                s.copy(xT_q.rearrange("p (a n) -> p a n", a=2), ps[:, 0:2, :]).then_inc(S["q_xT"], 1)

            def quad(g, k, i):
                done(act, "q_up_pe", g)
                done(act, "q_hid", g - 1)
                gate = bank(2).rearrange("p (j w f) -> p j w f", j=QB, w=2)[:, :, 0, :]
                s.activation(sil_q, gate, ACT.Silu).then_inc(S["q_silu"], 1)
                if not (isinstance(g, int) and g == NQ - 1):
                    xT_copy(g + 1)
            xT_copy(0)
            run_quads(act, quad)

        @block.tensor
        def _(pe):
            m = nc.tensor
            pe.wait_ge(consts, 11)
            def tr(dst, src):
                return m.transpose(dst, src, ident[0:src.shape[0], 0:src.shape[0]])

            def form(formed):
                for dst, a, b in formed[0]:
                    last = m.matmul(dst, a, b, start=True, stop=True)
                last.then_inc(su_pe, 1)

            def s_uvo(g):
                if g == 0:
                    pe.wait_ge(ld_late, 16 * LATE)
                    pe.wait_ge(su_ev, 4)
                if g == 3:
                    pe.wait_ge(su_ev, 5)
                form(form_uvo(g))

            def x_ctxT(t):
                pe.wait_ge(ld_ctx, 16 * t + 16)
                done(pe, "x_on1", t - 1)
                for c in range(DC):
                    for b in range(BT):
                        last = tr(bank(0)[:, (c * BT + b) * P:(c * BT + b + 1) * P], ctx_sb[:, b, c * P:(c + 1) * P])
                last.then_inc(S["x_ctxT_pe"], 1)

            def x_nT(t):
                done(pe, "x_norm", t)
                done(pe, "x_ot0", t - 1)
                for c in range(DC):
                    last = tr(bank(1)[:, c * P:(c + 1) * P], xn[:, c * P:(c + 1) * P])
                last.then_inc(S["x_nT_pe"], 1)

            def x_kvT(t):
                done(pe, "x_ctxT", t)
                if isinstance(t, int) and t == 0:
                    pe.wait_ge(ld_w2, 48)
                    pe.wait_ge(masks, 2)
                done(pe, "x_ot1", t - 1)
                for c in range(DC):
                    last = m.matmul(bank(2)[0:KVC, 0:BT * LK], w_kvc_sb[:, c, :], ctxT[:, c, :, :],
                                    start=(c == 0), stop=(c == DC - 1))
                last.then_inc(S["x_kvT_pe"], 1)

            def x_qcT(t):
                done(pe, "x_nT", t)
                done(pe, "x_on1", t - 1)
                for c in range(DC):
                    last = m.matmul(bank(3)[0:QC, 0:P], w_dq_sb[:, c, :], xnT[:, c, :],
                                    start=(c == 0), stop=(c == DC - 1))
                last.then_inc(S["x_qcT_pe"], 1)

            def x_kr(t):
                m.matmul(bank(0)[KVC:P, 0:BT * LK], w_kr_sb[:, :], KK[0:KVC, :, :], start=True, stop=True)
                m.matmul(bank(0)[KVC:P, BT * LK:2 * BT * LK], w_kr_rot[:, :], KK[0:KVC, :, :],
                         start=True, stop=True).then_inc(S["x_kr_pe"], 1)

            def x_kvn(t):
                done(pe, "x_kvT", t)
                for b in range(BT):
                    last = m.matmul(bank(1)[:, b * KVC:(b + 1) * KVC], KK[0:KVC, b, :], ident[0:KVC, 0:KVC],
                                    start=True, stop=True)
                last.then_inc(S["x_kvn_pe"], 1)

            def x_q(t):
                done(pe, "x_qcT", t)
                if isinstance(t, int) and t == 0:
                    pe.wait_ge(ld_w1, 48)
                    for g in range(4):
                        form(form_uqk(g))
                    pe.wait_ge(su_ev, 4)
                for n in range(2):
                    last = m.matmul(bank(2 + n), qcT[:, :], uqk_sb[:, 8 * n:8 * n + 8, :], start=True, stop=True)
                last.then_inc(S["x_q_pe"], 1)

            def x_qr(t):
                done(pe, "x_krb", t)
                done(pe, "x_res", t - 1)
                for n, k in enumerate((4, 0)):
                    last = m.matmul(bank(k), qcT[:, :], w_qr_sb[:, 512 * n:512 * n + 512], start=True, stop=True)
                last.then_inc(S["x_qr_pe"], 1)

            def x_qt(t):
                done(pe, "x_q", t)
                done(pe, "x_kvn", t)
                for g in range(4):
                    if g % 2 == 0:
                        done(pe, f"x_qn{g // 2}", t)
                    for h in range(4):
                        last = tr(bank(1 + g)[:, h * P:(h + 1) * P], QN[:, 4 * g + h, :])
                    last.then_inc(S[f"x_qt_pe{g}"], 1)

            def x_s(t, b):
                if b == 0:
                    done(pe, "x_kr", t)
                    if isinstance(t, int) and t == 0:
                        pe.wait_ge(masks, 7)
                for a in range(2):
                    if b == 0:
                        done(pe, f"x_qt{2 * a}", t)
                        done(pe, f"x_qt{2 * a + 1}", t)
                    for h in range(4):
                        p = 4 * a + h
                        m.matmul(bank(2 * b + a)[:, h * LK:(h + 1) * LK],
                                 QT[:, b, 2 * p:2 * p + 2, :], KK[:, b, :], start=(h == 0), stop=False,
                                 skip_group_check=True)
                    last = m.matmul(bank(2 * b + a), pick[:, b, :, :],
                                    neg_mask[:, t, :].unsqueeze(1).to_broadcast([P, 4, LK]),
                                    start=False, stop=True, skip_group_check=True)
                last.then_inc(S[f"x_s{b}_pe"], 1)

            def x_p(t, b):
                done(pe, f"x_exp{b}", t)
                if b == 1:
                    done(pe, "x_ph0", t)
                lo, hi = ((4, 0), (0, 2))[b]
                for name, k, p0 in ((f"x_pl{b}_pe", lo, 0), (f"x_ph{b}_pe", hi, 4)):
                    for h in range(4):
                        last = tr(bank(k)[:, h * P:(h + 1) * P], xp[:, b, p0 + h, :])
                    last.then_inc(S[name], 1)

            def x_o(t, b):
                done(pe, f"x_pl{b}", t)
                done(pe, f"x_ph{b}", t)
                w = KVC + 1
                for n, k in enumerate(((1, 4), (3, 0))[b]):
                    for h in range(4):
                        last = m.matmul(bank(k)[:, h * w:(h + 1) * w], xpT[:, b, 4 * n + h, :], kv_nat[:, b, :],
                                        start=True, stop=True)
                last.then_inc(S[f"x_o{b}_pe"], 1)

            def x_ot(t, b):
                done(pe, f"x_on{b}", t)
                for k in range(H // 4):
                    last = tr(bank((1, 2)[b])[:, k * P:(k + 1) * P], ON[:, b, 2 * k:2 * k + 2, :])
                last.then_inc(S[f"x_ot{b}_pe"], 1)

            def x_y(t):
                done(pe, "x_ot0", t)
                done(pe, "x_ot1", t)
                if isinstance(t, int) and t == 0:
                    pe.wait_ge(su_ev, SETUP)
                for n in range(H // 2):
                    k, par = n // 2, n % 2
                    last = m.matmul(bank(4)[:, 0:D], OT[:, k, par, :, :], uvo_sb[:, k, par, :],
                                    start=(n == 0), stop=(n == H // 2 - 1))
                last.then_inc(S["x_y_pe"], 1)

            def a_nT(t):
                done(pe, "a_norm", t)
                done(pe, "a_ot", t - 1)
                for c in range(DC):
                    last = tr(bank(5)[:, c * P:(c + 1) * P], an[:, c * P:(c + 1) * P])
                last.then_inc(S["a_nT_pe"], 1)

            def a_qk(t):
                done(pe, "a_nT", t)
                done(pe, "a_res", t - 1)
                for n in range(2 * DC):
                    for c in range(DC):
                        last = m.matmul(bank(6)[:, n * P:(n + 1) * P], w_qkvT[:, c, n * P:(n + 1) * P],
                                        anT[:, c, :], start=(c == 0), stop=(c == DC - 1))
                last.then_inc(S["a_qk_pe"], 1)

            def a_v(t):
                done(pe, "a_on", t - 1)
                for c in range(DC):
                    last = m.matmul(bank(7)[:, 0:D], anT[:, c, :], w_qkvT[:, c, 2 * D:3 * D],
                                    start=(c == 0), stop=(c == DC - 1))
                last.then_inc(S["a_v_pe"], 1)

            def a_s(t):
                pe.wait_ge(S["a_qbd"], 4 * t + 4)
                done(pe, "a_k", t)
                for b in range(BT):
                    for p in range(HPAIR):
                        c, h = divmod(2 * p, P // SD)
                        m.matmul(bank(5 + b)[:, p * LQ:(p + 1) * LQ], qbd[:, b, c, h:h + 2, :],
                                 kT[:, c, b * LQ:(b + 1) * LQ], start=(p == 0), stop=False,
                                 skip_group_check=True)
                    last = m.matmul(bank(5 + b), pick[:, b, :, :],
                                    causal[:, b, :].unsqueeze(1).to_broadcast([P, HPAIR, LQ]),
                                    start=False, stop=True, skip_group_check=True)
                last.then_inc(S["a_s_pe"], 1)

            def a_p(t):
                done(pe, "a_exp", t)
                done(pe, "a_v", t)
                for name, k, p0 in (("a_pl_pe", 7, 0), ("a_ph_pe", 5, 4)):
                    for h in range(4):
                        last = tr(bank(k)[:, h * P:(h + 1) * P], ap[:, p0 + h, :, :])
                    last.then_inc(S[name], 1)

            def a_o(t):
                done(pe, "a_pl", t)
                done(pe, "a_ph", t)
                w = 2 * SD + 1
                for b in range(BT):
                    rows = slice(LQ * b, LQ * b + LQ)
                    for p in range(HPAIR):
                        last = m.matmul(bank(6 + b)[:, p * w:(p + 1) * w], apT[rows, p, :], v_nat[rows, p, :],
                                        start=True, stop=True)
                last.then_inc(S["a_o_pe"], 1)

            def a_ot(t):
                done(pe, "a_on", t)
                for b in range(BT):
                    last = tr(bank(5)[:, b * P:(b + 1) * P], aON[:, b, :, :])
                last.then_inc(S["a_ot_pe"], 1)

            def a_y(t):
                done(pe, "a_ot", t)
                for par in range(2):
                    last = m.matmul(bank(6)[:, 0:D], aOT[:, par, :, :], w_outT[:, par, :],
                                    start=(par == 0), stop=(par == 1))
                last.then_inc(S["a_y_pe"], 1)

            run_tiles(pe, {
                "s": s_uvo,
                ("x", 1): x_ctxT, ("x", 2): x_nT, ("a", 1): a_nT, ("x", 3): x_kvT, ("x", 4): x_qcT,
                ("a", 2): a_qk, ("x", 5): x_kvn, ("x", 6): x_kr, ("x", 7): x_q, ("a", 3): a_v,
                ("x", 8): x_qr, ("a", 4): a_s, ("x", 9): x_qt, ("x", 10): lambda t: x_s(t, 0),
                ("a", 5): a_p, ("x", 11): lambda t: x_s(t, 1), ("a", 6): a_o,
                ("x", 12): lambda t: x_p(t, 0), ("a", 7): a_ot, ("x", 13): lambda t: x_o(t, 0),
                ("a", 8): a_y, ("x", 14): lambda t: x_p(t, 1), ("x", 15): lambda t: x_o(t, 1),
                ("x", 16): lambda t: x_ot(t, 0), ("x", 17): lambda t: x_ot(t, 1), ("y", 18): x_y})

            pe.wait_ge(ld_r, 32)
            for t in range(NT):
                done(pe, "r_norm", t)
                done(pe, "r_T", t - 1)
                odd_even = x3[:, t, :].rearrange("p (n c) -> p c n", c=DC)
                for c in range(DC):
                    last = tr(bank(0)[:, c * P:(c + 1) * P], odd_even[:, c, :])
                last.then_inc(S["r_T_pe"], 1)
                done(pe, "r_T", t)
                for c in range(DC):
                    last = m.matmul(bank(1)[:, t * E:(t + 1) * E], xT[:, c, t, :], rw_sb[:, c, :],
                                    start=(c == 0), stop=(c == DC - 1))
                last.then_inc(S["r_l_pe"], 1)

            pe.wait_ge(route, 1)
            pe.wait_ge(ld_shared, 48)

            def up_products(u):
                k = u % 2
                done(pe, "f_silu", u - 2)
                done(pe, "f_hid", u - 2)
                gate, up, _ = halves(shared)
                for w, b in ((gate, k), (up, 2 + k)):
                    w = w.rearrange("p (s c n) -> p c s n", s=NSH, c=DC)
                    for c in range(DC):
                        last = m.matmul(bank(b), xT[:, c, u, :], w[:, c, :, :], start=(c == 0), stop=(c == DC - 1))
                last.then_inc(S["f_gu_pe"], 1)

            def down_products(u):
                k = u % 2
                done(pe, "f_hT", u)
                done(pe, "f_acc", u - 1)
                _, _, down = halves(shared)
                for n in range(4):
                    last = m.matmul(bank(6)[:, 0:D], hidT[:, k, n * P:(n + 1) * P], down[:, n, :],
                                    start=(n == 0), stop=(n == 3))
                last.then_inc(S["f_y_pe"], 1)

            def turn_hidden(u):
                done(pe, "f_hid", u)
                done(pe, "f_hT", u - 1)
                for n in range(4):
                    last = tr(bank(4)[:, n * P:(n + 1) * P], hid[:, u % 2, n * P:(n + 1) * P])
                last.then_inc(S["f_hT_pe"], 1)

            def ranks():
                pe.wait_ge(route, CHOSEN_STEPS)
                m.matmul(bank(7), tri[:, :], chosen_b[:, :, :], start=True, stop=False, skip_group_check=True)
                for t in range(NT - 1):
                    later = NT - 1 - t
                    m.matmul(bank(7)[:, (t + 1) * E:], ones_b[:, :],
                             chosen_b[:, t, :].unsqueeze(1).to_broadcast([P, later, E]),
                             start=False, stop=(t == NT - 2), skip_group_check=True)
                for t in range(NT):
                    last = m.matmul(bank(5)[:, 0:E], ones_b[:, :], chosen_b[:, t, :],
                                    start=(t == 0), stop=(t == NT - 1))
                last.then_inc(rank_pe, 1)

            for u in range(NT):
                up_products(u)
                if u == RANKS_AT:
                    ranks()
                if u == EID_AT:
                    pe.wait_ge(route, EID_STEPS)
                    m.matmul(bank(5)[0:1, 0:P], eid_col[:, :], ident[:, :], start=True, stop=True).then_inc(eid_pe, 1)
                if u >= 2:
                    down_products(u - 2)
                if u >= 1:
                    turn_hidden(u - 1)
            down_products(NT - 2)
            turn_hidden(NT - 1)
            down_products(NT - 1)

            def turn_tokens(g, k, i):
                pe.wait_ge(ld_tok[k], 16 * (i + 1))
                done(pe, "q_xT", g - 1)
                for j in range(QB):
                    tokens = x_blk[k][:, j * D:(j + 1) * D].rearrange("p (n c) -> p c n", c=DC)
                    for c in range(DC):
                        n = DC * j + c
                        last = tr(bank(n // 4)[:, (n % 4) * P:(n % 4 + 1) * P], tokens[:, c, :])
                last.then_inc(S["q_xT_pe"], 1)

            def up_blocks(g, k, i):
                pe.wait_ge(ld_exp[k], 16 * QB * (i + 1))
                done(pe, "q_xT", g)
                done(pe, "q_hid", g - 1)
                for j in range(QB):
                    for c in range(DC):
                        last = m.matmul(bank(2)[:, j * P:(j + 1) * P], xT_q[:, (DC * j + c) * P:(DC * j + c + 1) * P],
                                        w_blk[:, k, j, c * P:(c + 1) * P], start=(c == 0), stop=(c == DC - 1))
                last.then_inc(S["q_up_pe"], 1)

            def down_blocks(g, k):
                done(pe, "q_hT", g)
                done(pe, "q_y", g - 1)
                for j in range(QB):
                    for h in range(2):
                        rows = slice(F * h, F * h + F)
                        last = m.matmul(bank(4 + h)[:, j * P:(j + 1) * P],
                                        hT_q[rows, j * P:(j + 1) * P], w_blk[rows, k, j, 2 * DC * F:],
                                        start=True, stop=True)
                last.then_inc(S["q_down_pe"], 1)

            def turn_block_hidden(g):
                done(pe, "q_hid", g)
                done(pe, "q_hT", g - 1)
                for j in range(QB):
                    last = tr(bank(3)[:, j * P:(j + 1) * P], hid_q[:, j, :, :])
                last.then_inc(S["q_hT_pe"], 1)

            def quad(g, k, i):
                up_blocks(g, k, i)
                if not (isinstance(g, int) and g == NQ - 1):
                    turn_tokens(g + 1, (k + 1) % QBUF, i if k < QBUF - 1 else i + 1)
                if not (isinstance(g, int) and g < 1):
                    down_blocks(g - 1, (k - 1) % QBUF)
                turn_block_hidden(g)
            done(pe, "f_hid", NT - 1)
            done(pe, "f_silu", NT - 1)
            pe.wait_ge(eid_ready, 1)
            turn_tokens(0, 0, 0)
            run_quads(pe, quad)
            down_blocks(NQ - 1, QBUF - 1)


def rope_tables():
    import numpy as np
    inv = (1.0 / np.float32(10000.0) ** (np.arange(HALF, dtype=np.float32) / np.float32(HALF))).astype(np.float32)
    ang = np.arange(LK, dtype=np.float32)[:, None] * inv
    cos = np.concatenate([np.cos(ang)] * 2, axis=1).astype(np.float32)
    sin = np.concatenate([np.sin(ang)] * 2, axis=1).astype(np.float32)
    keys = np.stack([np.tile(cos.T, (1, BT)), np.tile(sin.T, (1, BT))], axis=1)
    signed = np.concatenate([-sin[:, :HALF], sin[:, HALF:]], axis=1)
    latents = np.stack([np.tile(cos[:LQ], (BT, 1)), np.tile(signed[:LQ], (BT, 1))], axis=1)
    return np.ascontiguousarray(keys), np.ascontiguousarray(latents)


def expert_rows(wg, wu, wd):
    import numpy as np
    ins = np.concatenate([wg.reshape(E, P, DC, F), wu.reshape(E, P, DC, F)], axis=3).reshape(E, P, 2 * DC * F)
    down = wd.reshape(E, F, 2, D // 2).transpose(0, 2, 1, 3).reshape(E, P, D // 2)
    return np.ascontiguousarray(np.concatenate([ins, down], axis=2))


def laid_out(inputs):
    import numpy as np
    a = {n.replace("L0_", ""): np.asarray(v) for n, v in inputs.items()}
    turned = lambda w, width: w.reshape(width, H, HD).transpose(2, 1, 0)
    b_qkv = a["attn_b_qkv"]
    rope_keys, rope_latents = rope_tables()
    return {
        "x": a["x"], "ctx": a["ctx_2048"], "seg": a["itok_BxS_0_1023"].reshape(NT, P).T,
        "w_kvc": a["xattn_W_kvc"], "w_dq": a["xattn_W_dq"], "w_uqT": turned(a["xattn_W_uq"], QC),
        "w_qr": a["xattn_W_qr"],
        "w_ukuvT": np.stack([turned(a["xattn_W_uk"], KVC), turned(a["xattn_W_uv"], KVC)], axis=1),
        "w_kr": a["xattn_W_kr"], "w_o": a["xattn_W_o"],
        "w_qkv_T": a["attn_W_qkv"].T.reshape(DC, P, 3 * D).transpose(1, 0, 2),
        "b_qk": b_qkv[:2 * D].reshape(2 * DC, P).T, "b_v": b_qkv[2 * D:],
        "w_out_T": a["attn_W_out"].T.reshape(HPAIR, 2, SD, D).transpose(0, 2, 1, 3).reshape(P, 2, D),
        "b_out": a["attn_b_out"], "router_w": a["ffn_router_w"], "router_b": a["ffn_router_bias"],
        "experts": expert_rows(a["ffn_wg"], a["ffn_wu"], a["ffn_wd"]),
        "swg": a["ffn_swg"], "swu": a["ffn_swu"], "swd": a["ffn_swd"],
        "rope_keys": rope_keys, "rope_latents": rope_latents}


def kernel(**inputs):
    import numpy as _np
    import concourse.bacc as _bacc
    from concourse import mybir as _mybir
    from concourse.bass_utils import run_bass_kernel_spmd as _run

    nc = _bacc.Bacc("TRN2", target_bir_lowering=False, num_devices=1)
    arrays, args = {}, []
    for name, a in laid_out(inputs).items():
        a = _np.ascontiguousarray(a)
        arrays[f"in_{name}_dram"] = a
        args.append(nc.dram_tensor(f"in_{name}_dram", a.shape, _mybir.dt.from_np(a.dtype), kind="ExternalInput").ap())
    out = nc.dram_tensor("out_0_dram", (NB, LQ, D), _mybir.dt.float32, kind="ExternalOutput").ap()
    rows = [nc.dram_tensor(name, (NBLK * CAP, D), _mybir.dt.float32, kind="Internal").ap()
            for name in ("expert_tokens", "expert_results")]
    build(nc, *args, out, *rows)
    r = _run(nc, [arrays], core_ids=[0])
    return r.results[0]["out_0_dram"]
```

```python
from contextlib import ExitStack

import concourse.bass as bass
from concourse import mybir

ALU = mybir.AluOpType
ACT = mybir.ActivationFunctionType
F32 = mybir.dt.float32
BF16 = mybir.dt.bfloat16
I32 = mybir.dt.int32
U32 = mybir.dt.uint32
AX = mybir.AxisListType

P = 128
NB, LQ, D = 16, 64, 256
LK = 128
N = NB * LQ
NT = N // P
BT = P // LQ
DC = D // P
H, HD = 16, 128
KVC, QC, R = 64, 96, 64
HALF = R // 2
LOOKBACK = 8
XSCALE = float((HD + R) ** -0.5)
HPAIR = H // 2
SD = D // H
ASCALE = float(SD ** -0.5)
NEG = -1e30
EPS = 1e-5
E, F, TOPK = 64, 64, 4
NSH, HS = 2, 256
CAP = P
SLOTS = N * TOPK
NBLK = (SLOTS + E * (CAP - 1)) // CAP
QB = 4
QBUF = 4
NQ = -(-NBLK // (QB * QBUF)) * QBUF
NBLK = NQ * QB
WROW = 2 * DC * F + D // 2
GB = 4
SUB_STEPS = 2
GATE_STEPS = SUB_STEPS + 4 + 2 * TOPK
LATE = 8


ORDER = [("x", 1), ("y", 18), ("b", 1), ("x", 2), ("a", 0), ("x", 3), ("b", 2), ("x", 4), ("a", 0.5),
         ("x", 5), ("x", 6), ("x", 6.5), ("x", 7), ("x", 7.5), ("a", 1), ("b", 3), ("x", 8), ("a", 2), ("s", 0),
         ("x", 9), ("a", 3), ("x", 9.5), ("s", 1), ("b", 4), ("x", 10), ("s", 2), ("x", 11), ("b", 5),
         ("b", 6), ("a", 4), ("a", 4.5), ("x", 12.5), ("x", 12), ("s", 3), ("a", 4.6), ("x", 14),
         ("x", 13), ("a", 4.7), ("a", 5), ("b", 6.5), ("x", 16), ("b", 7), ("b", 7.5),
         ("x", 15), ("b", 9), ("a", 6), ("x", 17)]
LAST_ORDER = [("y", 18), ("a", 0), ("b", 1), ("b", 2), ("a", 0.5), ("a", 1), ("b", 3), ("a", 2), ("a", 3),
              ("e", 0), ("f", 0), ("b", 4), ("b", 5), ("b", 6), ("a", 4), ("e", 1), ("a", 4.5),
              ("a", 4.6), ("a", 4.7), ("f", 1), ("a", 5), ("b", 6.5), ("b", 7), ("b", 7.5), ("a", 6),
              ("b", 9)]
E_ROUND = 2
E_EID = 3
E_PRE = 4
PICKS = 12
WAVES = 12


def build(nc, x, ctx, seg, w_kvc, w_dq, w_uqT, w_qr, w_ukuvT, w_kr, w_o, w_qkv_T, b_qk, b_v,
          w_out_T, b_out, router_w, router_b, w_exp, swg, swu, swd, rope_k, rope_q, out, xs, ys):
    stack = ExitStack()
    with stack:
        def sb(name, shape, dt=F32):
            return stack.enter_context(nc.sbuf_tensor(name, shape, dt))

        def sem(name):
            return stack.enter_context(nc.semaphore(name))

        x_sb = sb("x_sb", [P, NT, D])
        ctx_sb = sb("ctx_sb", [P, BT, D])
        seg_i = sb("seg_i", [P, NT], I32)
        w_kvc_sb = sb("w_kvc_sb", [P, DC, KVC])
        w_dq_sb = sb("w_dq_sb", [P, DC, QC])
        w_qr_sb = sb("w_qr_sb", [QC, H * R])
        w_kr_sb = sb("w_kr_sb", [KVC, R])
        w_kr_rot = sb("w_kr_rot", [KVC, R])
        rope_k_sb = sb("rope_k_sb", [P, 2, BT * LK])
        rope_q_sb = sb("rope_q_sb", [P, 2, R])
        bqk_sb = sb("bqk_sb", [P, 2 * DC])
        bv_sb = sb("bv_sb", [P, D])
        bout_sb = sb("bout_sb", [P, D])
        rw_sb = sb("rw_sb", [P, DC, E])
        rb_sb = sb("rb_sb", [P, E])
        QN = sb("QN", [P, H, KVC + R])
        QN_flat = QN[:, :, :].rearrange("p a b -> p (a b)")
        QT = sb("QT", [P, BT, H, LQ])
        QT_flat = QT[:, :, :, :].rearrange("p a b c -> p (a b c)")
        xpT = sb("xpT", [P, BT, HPAIR, P])
        xpT_flat = xpT[:, :, :, :].rearrange("p a b c -> p (a b c)")
        big = sb("big", [P, 10240])
        st_uqT = big[:, 0:H * QC].rearrange("p (h n) -> p h n", h=H)
        st_kuvT = big[:, 2048:2048 + 2 * H * KVC].rearrange("p (k h n) -> p k h n", h=H, k=2)
        w_o_sb = big[:, 4096:4096 + H * D].rearrange("p (h d) -> p h d", h=H)
        ident = sb("ident", [P, P])
        ones_f = sb("ones_f", [P, P])
        pick = sb("pick", [P, BT, 2, LQ], BF16)
        causal = sb("causal", [P, BT, LQ], BF16)
        head_of = sb("head_of", [P, P // SD])
        uqk_sb = sb("uqk_sb", [QC, H, KVC])
        uvo_sb = sb("uvo_sb", [P, H // 4, 2, D])
        w_qkvT = sb("w_qkvT", [P, DC, 3 * D])
        w_outT = sb("w_outT", [P, 2, D])
        neg_mask = sb("neg_mask", [P, NT, LK], BF16)
        key_iota = sb("key_iota", [P, LK])
        seg_f = sb("seg_f", [P, NT])
        e_iota = sb("e_iota", [P, E])
        half_neg = sb("half_neg", [P, 1])
        stats = sb("stats", [P, 3, 6])
        held = sb("held", [P, 1])
        mv = sb("mv", [P, 3, 2])
        rstd = sb("rstd", [P, 3, 2])
        x_stats = sb("x_stats", [P, NT, 6])
        x_mv = sb("x_mv", [P, NT, 2])
        x_rs = sb("x_rs", [P, NT, 2])
        rn = sb("rn", [P, D])
        rnT = sb("rnT", [P, DC, P])
        xn = sb("xn", [P, D])
        xnT = sb("xnT", [P, DC, P])
        ctxT = sb("ctxT", [P, DC, BT, LK])
        qcT = sb("qcT", [QC, P])
        KK = sb("KK", [P, BT, LK])
        kr_a = sb("kr_a", [P, BT * LK])
        kr_b = sb("kr_b", [P, BT * LK])
        kv_nat = sb("kv_nat", [P, BT, KVC + 1])
        rt_b = sb("rt_b", [P, H, R])
        x_max = sb("x_max", [P, BT, HPAIR])
        x_rec = sb("x_rec", [P, BT, HPAIR])
        xp = sb("xp", [P, BT, HPAIR, LK])
        ON = sb("ON", [P, BT, HPAIR, KVC])
        OT = sb("OT", [P, H // 4, 2, BT, LQ])
        held_p = sb("held_p", [P, 2])
        an = sb("an", [P, D])
        anT = sb("anT", [P, DC, P])
        qT = sb("qT", [P, DC, P])
        kT = sb("kT", [P, DC, P])
        v_nat = sb("v_nat", [P, HPAIR, BT, 2 * SD + 1])
        qbd = sb("qbd", [P, BT, DC, P // SD, LQ])
        a_max = sb("a_max", [P, BT, HPAIR])
        a_rec = sb("a_rec", [P, BT, HPAIR])
        ap = sb("ap", [P, HPAIR, BT, LQ])
        apT = sb("apT", [P, HPAIR, P])
        aON = sb("aON", [P, BT, HPAIR, SD])
        aOT = sb("aOT", [P, 2, BT, LQ])
        xT = sb("xT", [P, DC, NT, P])
        logit = sb("logit", [P, NT, E])
        biased = sb("biased", [P, E])
        comb = sb("comb", [P, NT, E])
        chosen = sb("chosen", [P, NT, E])
        picked = sb("picked", [P, NT, E])
        top_v = sb("top_v", [P, 8])
        top_i = sb("top_i", [P, 8], U32)
        top_f = sb("top_f", [P, 8])
        row_s = sb("row_s", [P, 3, NT])
        silu = sb("silu", [P, 2, 512])
        hid = sb("hid", [P, 2, 512])
        hidT = sb("hidT", [P, 2, 512])
        GW = 512 * DC
        shared = big[:, 0:3 * GW]
        tri = sb("tri", [P, P], BF16)
        ones_b = sb("ones_b", [P, P], BF16)
        slot_f = sb("slot_f", [P, TOPK])
        slot_u = sb("slot_u", [P, NT, TOPK], U32)
        gate_j = sb("gate_j", [P, TOPK, NT])
        slot_now = sb("slot_now", [P, TOPK], U32)
        taken = sb("taken", [P, 3 * E + 2])
        tokens_of, room_of, last_of = (taken[:, E * n:E * n + E] for n in range(3))
        blocks_all = taken[:, 3 * E:3 * E + 1]
        eid_col = taken[:, 3 * E + 1:3 * E + 2]
        wk = sb("wk", [P, 11, E])
        sum_1 = sb("sum_1", [P, 1])
        chosen_now = sb("chosen_now", [P, E], BF16)
        block_1 = sb("block_1", [P, 1])
        e_scaled = sb("e_scaled", [P, E])
        eid_i = sb("eid_i", [1, P], I32)
        w_blk = big[:, 3 * GW:3 * GW + QBUF * QB * WROW].rearrange("p (k j n) -> p k j n", k=QBUF, j=QB)
        spare = w_qkvT[:, :, :].rearrange("p c n -> p (c n)")
        sil_q = spare[:, 0:QB * F].rearrange("p (j f) -> p j f", j=QB)
        hid_q = spare[:, 256:256 + 2 * QB * F].rearrange("p (j r f) -> p j r f", j=QB, r=2)
        hT_q = spare[:, 768:768 + QB * P]
        ZW = 2048
        zeros = big[:, 3 * GW:3 * GW + ZW]
        x_blk = [QT_flat[:, 1024:2048], xpT_flat[:, 0:1024], xpT_flat[:, 1024:2048],
                 ON[:, :, :, :].rearrange("p a b c -> p (a b c)")]
        y_blk = [QN_flat[:, 0:1024], QN_flat[:, 1024:2048], QT_flat[:, 0:1024],
                 OT[:, :, :, :, :].rearrange("p a b c d -> p (a b c d)")]
        xT_q = rt_b[:, :, :].rearrange("p h r -> p (h r)")
        is_all = big[:, 8192:8192 + NT * TOPK * E].rearrange("p (t j e) -> p t j e", j=TOPK, t=NT)
        y_got = uvo_sb[:, :, :, :].rearrange("p a b c -> p (a b c)")[:, 0:GB * D].rearrange("p (k d) -> p k d", k=GB)
        ps = stack.enter_context(nc.psum_tensor("ps", [P, 8, 512], F32))

        def bank(b):
            return ps[:, b, :]

        ld_r = sem("ld_r")
        ld_shared, zero_done, scattered = (sem(n) for n in ("ld_shared", "zero_done", "scattered"))
        route, route_ex, eid_pe, eid_ready = (sem(n) for n in (
            "route", "route_ex", "eid_pe", "eid_ready"))
        ld_tok = [sem(f"ld_tok{k}") for k in range(QBUF)]
        ld_exp = [sem(f"ld_exp{k}") for k in range(QBUF)]
        st_y = [sem(f"st_y{k}") for k in range(QBUF)]
        got = [sem(f"got{k}") for k in range(GB)]
        ld_x, ld_ctx, ld_w1, ld_w2, ld_small, ld_late, st_out = (sem(n) for n in (
            "ld_x", "ld_ctx", "ld_w1", "ld_w2", "ld_small", "ld_late", "st_out"))
        zeroed, consts, masks, mask_step = (sem(n) for n in ("zeroed", "consts", "masks", "mask_step"))
        su_pe, su_ev = sem("su_pe"), sem("su_ev")
        names = """x_stat x_aggr x_veps x_rstd x_norm x_nT_pe x_nT x_ctxT_pe x_ctxT x_kvT_pe x_kvT
            x_qcT_pe x_qcT x_kr_pe x_krb x_kr x_kvn_pe x_kvn x_q_pe x_q x_qr0_pe x_qr1_pe x_sin0 x_sin1 x_qn0 x_qn1 x_qt_pe0 x_qt_pe1 x_qt_pe2 x_qt_pe3 x_qt0 x_qt1 x_qt2 x_qt3
            x_s0_pe x_s1_pe x_mx0 x_mx1 x_sub0 x_sub1 x_exp0 x_exp1
            x_pl0_pe x_ph0_pe x_pl1_pe x_ph1_pe x_pl0 x_ph0 x_pl1 x_ph1
            x_o0_pe x_o1_pe x_rec0 x_rec1 x_on0 x_on1 x_ot0_pe x_ot1_pe x_ot0 x_ot1 x_y_pe x_res
            a_stat a_aggr a_veps a_rstd a_norm a_nT_pe a_nT a_qk_pe a_q a_k a_qbd a_v_pe a_v
            a_s_pe a_mx a_sub a_exp a_pl_pe a_ph_pe a_pl a_ph a_o_pe a_rec a_on a_ot_pe a_ot
            a_y_pe a_res a_resb
            r_pick r_slot r_rank_pe r_rstd r_T_pe r_T r_l_pe""".split()
        names += ["f_gu_pe", "f_silu", "f_hid", "f_hT_pe", "f_hT", "f_y_pe", "f_acc", "q_xT_pe", "q_xT",
                  "q_up_pe", "q_silu", "q_hid", "q_hT_pe", "q_hT", "q_down_pe", "q_y", "combined"]
        S = {n: sem(n) for n in names}

        def done(eng, name, t):
            if isinstance(t, int) and t < 0:
                return
            eng.wait_ge(S[name], t + 1)

        ZEROS = NBLK * CAP * D // P // ZW

        def g_not_first(g):
            return not isinstance(g, int) or g >= QBUF

        xr = x.rearrange("b q d -> (b q) d").rearrange("(t p) d -> p t d", p=P)
        outr = out.rearrange("b q d -> (b q) d").rearrange("(t p) d -> p t d", p=P)
        ctxr = ctx.rearrange("(t b) k d -> t k b d", b=BT)
        

        def form_uqk(g):
            bk = bank(5 + g % 3)
            return ([(bk[0:QC, j * KVC:(j + 1) * KVC], st_uqT[:, 4 * g + j, :], st_kuvT[:, 0, 4 * g + j, :])
                     for j in range(4)],
                    uqk_sb[:, 4 * g:4 * g + 4, :], bk[0:QC, 0:4 * KVC].rearrange("p (h n) -> p h n", h=4))

        def form_uvo(g):
            bk = bank(5 + g % 3)
            return ([(bk[(j // 2) * KVC:(j // 2 + 1) * KVC, (j % 2) * D:(j % 2 + 1) * D],
                      st_kuvT[:, 1, 4 * g + j, :], w_o_sb[:, 4 * g + j, :]) for j in range(4)],
                    uvo_sb[:, g, :, :], bk.rearrange("p (r d) -> p r d", r=2))
        SETUP = 8

        block = stack.enter_context(nc.Block())

        def interleave(steps, t_x, t_a, t_b):
            tiles = {"x": t_x, "y": t_a, "a": t_a, "b": t_b}
            for kind, what in (LAST_ORDER if t_x is None else ORDER):
                if kind in ("e", "f"):
                    if t_a is not None and kind in steps:
                        steps[kind](what)
                elif kind == "s":
                    if t_a is None and kind in steps and t_x == 0:
                        steps[kind](what)
                elif tiles[kind] is not None and (kind, what) in steps:
                    steps[(kind, what)](tiles[kind])

        def run_tiles(eng, steps):
            interleave(steps, 0, None, None)
            interleave(steps, 1, 0, None)
            interleave(steps, 2, 1, 0)
            with eng.Fori(3, NT) as t:
                interleave(steps, t, t - 1, t - 2)
            interleave(steps, None, NT - 1, NT - 2)
            interleave(steps, None, None, NT - 1)

        def is_last(t):
            return isinstance(t, int) and t == NT - 1

        def normed(t):
            return xn[:, :] if is_last(t) else rn[:, :]

        def halves(buf):
            return buf[:, 0:GW], buf[:, GW:2 * GW], buf[:, 2 * GW:3 * GW].rearrange("p (n d) -> p n d", d=D)

        def run_quads(eng, step):
            for g in range(QBUF):
                step(g, g, 0)
            with eng.Fori(1, NQ // QBUF - 1) as i:
                for k in range(QBUF):
                    step(QBUF * i + k, k, i)
            for g in range(NQ - QBUF, NQ):
                step(g, g % QBUF, g // QBUF)

        def shared_hidden(eng, ops, u):
            k = u % 2
            done(eng, "f_silu", u)
            done(eng, "f_hT_pe", u - 2)
            done(eng, "f_hid", u - 1)
            ops.tensor_tensor(hid[:, k, :], silu[:, k, :], bank(2), ALU.mult).then_inc(S["f_hid"], 1)

        def shared_result(eng, ops, u):
            done(eng, "f_y_pe", u)
            done(eng, "f_acc", u - 1)
            ops.tensor_tensor(x_sb[:, u, :], x_sb[:, u, :], bank(3)[:, 0:D],
                              ALU.add).then_inc(S["f_acc"], 1)

        @block.sync
        def _(sp):
            sp.dma_start(ctx_sb[:, :, :], ctxr[0]).then_inc(ld_ctx, 16)
            sp.dma_start(st_uqT, w_uqT).then_inc(ld_w1, 16)
            sp.dma_start(st_kuvT[:, 0, :, :], w_ukuvT[:, 0, :, :]).then_inc(ld_w1, 16)
            sp.dma_start(w_qr_sb[:, :], w_qr).then_inc(ld_w1, 16)
            sp.dma_start(st_kuvT[:, 1, :, :], w_ukuvT[:, 1, :, :]).then_inc(ld_late, 16)
            sp.dma_start(w_o_sb, w_o.rearrange("(h p) d -> p h d", p=HD)).then_inc(ld_late, 16)
            sp.dma_start(w_qkvT[:, :, :], w_qkv_T).then_inc(ld_late, 16)
            sp.dma_start(w_outT[:, :, :], w_out_T).then_inc(ld_late, 16)
            sp.dma_start(bqk_sb[:, :], b_qk).then_inc(ld_late, 16)
            sp.dma_start(bv_sb[:, :], b_v.rearrange("(o d) -> o d", o=1).to_broadcast([P, D])).then_inc(ld_late, 16)
            sp.dma_start(bout_sb[:, :], b_out.rearrange("(o d) -> o d", o=1).to_broadcast([P, D])).then_inc(ld_late, 16)
            sp.dma_start(x_sb[:, 1:, :], xr[:, 1:, :]).then_inc(ld_late, 16)
            sp.dma_start(rb_sb[:, :], router_b.rearrange("(o e) -> o e", o=1).to_broadcast([P, E])).then_inc(ld_r, 16)
            sp.dma_start(rw_sb[:, :, :], router_w.rearrange("(p c) e -> p c e", c=DC)).then_inc(ld_r, 16)
            def load_ctx(t):
                done(sp, "x_ctxT_pe", t - 1)
                sp.dma_start(ctx_sb[:, :, :], ctxr[t]).then_inc(ld_ctx, 16)
            load_ctx(1)
            sp.wait_ge(su_ev, SETUP + 1)
            xs_flat = xs.rearrange("(p r) d -> p (r d)", p=P)
            for n in range(ZEROS):
                sp.dma_start(xs_flat[:, n * ZW:(n + 1) * ZW], zeros).then_inc(zero_done, 16)
                if n == ZEROS // 2:
                    load_ctx(2)
            gate, up, down = halves(shared)
            for dst, src in ((gate, swg), (up, swu)):
                sp.dma_start(dst.rearrange("p (s n) -> p s n", s=NSH),
                             src.rearrange("s (p c) h -> p s (c h)", c=DC)).then_inc(ld_shared, 16)
            sp.dma_start(down, swd.rearrange("s (n p) d -> p (s n) d", p=P)).then_inc(ld_shared, 16)
            with sp.Fori(3, NT) as t:
                load_ctx(t)

            picks = [sp.alloc_register(f"expert{j}") for j in range(QB)]

            def load_tokens(g, k):
                if g_not_first(g):
                    done(sp, "q_xT_pe", g - QBUF)
                sp.dma_start(x_blk[k].rearrange("p (j d) -> p j d", j=QB),
                             xs.rearrange("(g j p) d -> g p j d", j=QB, p=P)[g]).then_inc(ld_tok[k], 16)

            def load_quad(g, k, _):
                if g_not_first(g):
                    done(sp, "q_down_pe", g - QBUF)
                elif g == QBUF - 1:
                    sp.wait_ge(route, GATE_STEPS)
                sp.load(picks, eid_i[0:1, bass.ds(QB * g, QB)])
                for j in range(QB):
                    e = sp.snap(picks[j], min_val=0, max_val=E - 1)
                    sp.dma_start(w_blk[:, k, j, :], w_exp[bass.ds(e, 1), :, :].rearrange("o p n -> p (o n)")).then_inc(ld_exp[k], 16)
                if not (isinstance(g, int) and g == NQ - 1):
                    if isinstance(g, int) and g == 0:
                        sp.wait_ge(scattered, 16 * TOPK * NT)
                        load_tokens(0, 0)
                    load_tokens(g + 1, (k + 1) % QBUF)
            sp.wait_ge(zero_done, 16 * ZEROS)
            sp.wait_ge(eid_ready, 1)
            run_quads(sp, load_quad)
            for t in range(NT):
                done(sp, "combined", TOPK * t + TOPK - 1)
                sp.dma_start(outr[:, t, :], x_sb[:, t, :]).then_inc(st_out, 16)
            sp.wait_ge(st_out, 16 * NT)

        @block.gpsimd
        def _(pool):
            g = nc.gpsimd
            g.memset(ident[:, :], 0.0).then_inc(zeroed, 1)
            g.memset(ones_f[:, :], 1.0).then_inc(zeroed, 1)
            g.memset(pick[:, :, :, :], 0.0).then_inc(zeroed, 1)
            g.memset(causal[:, :, :], 0.0).then_inc(zeroed, 1)
            g.memset(half_neg[:, :], -0.5).then_inc(zeroed, 1)
            g.memset(kv_nat[:, :, KVC:KVC + 1], 1.0).then_inc(consts, 1)
            g.memset(v_nat[:, :, :, :], 0.0).then_inc(consts, 1)
            g.iota(key_iota[:, :], pattern=[[1, LK]], base=0, channel_multiplier=0,
                   allow_small_or_imprecise_dtypes=True).then_inc(consts, 1)
            g.iota(e_iota[:, :], pattern=[[1, E]], base=0, channel_multiplier=0,
                   allow_small_or_imprecise_dtypes=True).then_inc(consts, 1)
            g.memset(ones_b[:, :], 1.0).then_inc(zeroed, 1)
            g.memset(taken[:, :], 0.0).then_inc(consts, 1)
            g.iota(block_1[:, :], pattern=[[0, 1]], base=CAP, channel_multiplier=CAP,
                   allow_small_or_imprecise_dtypes=True).then_inc(consts, 1)
            pool.wait_ge(consts, 6)
            g.tensor_scalar(e_scaled[:, :], e_iota[:, :], 1.0 / CAP, None, ALU.mult).then_inc(consts, 1)
            g.affine_select(out=tri[:, :], in_=ones_b[:, :], compare_op=ALU.is_ge, fill=0.0,
                            base=-1, pattern=[[1, P]], channel_multiplier=-1).then_inc(consts, 1)
            g.affine_select(out=ident[:, :], in_=ident[:, :], compare_op=ALU.not_equal, fill=1.0,
                            base=0, pattern=[[-1, P]], channel_multiplier=1).then_inc(consts, 1)
            for b in range(BT):
                g.affine_select(out=pick[:, b, :, :], in_=pick[:, b, :, :], compare_op=ALU.not_equal,
                                fill=1.0, base=-LQ * b, pattern=[[0, 2], [-1, LQ]],
                                channel_multiplier=1).then_inc(consts, 1)
            g.affine_select(out=causal[:, :, :], in_=causal[:, :, :], compare_op=ALU.is_ge,
                            fill=NEG, base=0, pattern=[[-LQ, BT], [-1, LQ]],
                            channel_multiplier=1).then_inc(consts, 1)
            g.affine_select(out=head_of[:, :], in_=ones_f[:, 0:P // SD], compare_op=ALU.is_ge,
                            fill=0.0, base=0, pattern=[[-SD, P // SD]],
                            channel_multiplier=1).then_inc(mask_step, 1)
            pool.wait_ge(mask_step, 1)
            g.affine_select(out=head_of[:, :], in_=head_of[:, :], compare_op=ALU.is_ge,
                            fill=0.0, base=SD - 1, pattern=[[SD, P // SD]],
                            channel_multiplier=-1).then_inc(consts, 1)

            def x_rstds(n):
                ts = slice(0, 1) if n == 0 else slice(1, NT)
                done(pool, "x_veps", n)
                g.tensor_tensor(x_rs[:, ts, 1], x_rs[:, ts, 0],
                                half_neg[:, :].to_broadcast([P, ts.stop - ts.start]), ALU.pow).then_inc(S["x_rstd"], 1)

            def a_rstd(t):
                done(pool, "a_veps", t)
                g.tensor_tensor(rstd[:, 1, 1:2], rstd[:, 1, 0:1], half_neg[:, :], ALU.pow).then_inc(S["a_rstd"], 1)

            def a_qbd(t):
                done(pool, "a_q", t)
                done(pool, "a_s_pe", t - 1)
                for b in range(BT):
                    for c in range(DC):
                        last = g.tensor_tensor(
                            qbd[:, b, c, :, :],
                            qT[:, c, b * LQ:(b + 1) * LQ].unsqueeze(1).to_broadcast([P, P // SD, LQ]),
                            head_of[:, :].unsqueeze(2).to_broadcast([P, P // SD, LQ]), ALU.mult)
                        last.then_inc(S["a_qbd"], 1)

            def a_resb(t):
                done(pool, "x_res", t)
                done(pool, "a_stat", t)
                done(pool, "a_norm", t)
                if isinstance(t, int) and t == 0:
                    pool.wait_ge(ld_late, 16 * LATE)
                g.tensor_tensor(x_sb[:, t, :], x_sb[:, t, :], bout_sb[:, :], ALU.add).then_inc(S["a_resb"], 1)

            def r_rstd(t):
                pool.wait_ge(S["r_pick"], PICKS * t + 3)
                g.tensor_tensor(rstd[:, 2, 1:2], rstd[:, 2, 0:1], half_neg[:, :], ALU.pow).then_inc(S["r_rstd"], 1)
                if is_last(t):
                    r_scatter(NT - 2)

            def r_scatter(t):
                pool.wait_ge(zero_done, 16 * ZEROS)
                pool.wait_ge(S["r_slot"], WAVES * t + WAVES)
                n = int(is_last(t))
                g.tensor_tensor(held_p[:, n:n + 1], half_neg[:, :], half_neg[:, :], ALU.mult)
                for j in range(TOPK):
                    g.indirect_dma_start(
                        out=xs, out_offset=bass.IndirectOffsetOnAxis(ap=slot_now[:, j:j + 1], axis=0),
                        in_=normed(t), in_offset=None).then_inc(scattered, 16)

            run_tiles(pool, {
                ("x", 1): lambda t: x_rstds(0) if isinstance(t, int) and t == 0 else None,
                "s": lambda n: x_rstds(1) if n == 1 else None,
                ("a", 0): a_rstd, ("a", 2): a_qbd, ("a", 3): a_resb, ("b", 3): r_rstd,
                ("b", 9): lambda t: None if isinstance(t, int) and t == NT - 2 else r_scatter(t)})

            def store_quad(gq, k, _):
                done(pool, "q_y", gq)
                pool.dma_start(ys.rearrange("(g j p) d -> g p j d", j=QB, p=P)[gq],
                               y_blk[k].rearrange("p (j d) -> p j d", j=QB)).then_inc(st_y[k], 16)
            run_quads(pool, store_quad)

            for k in range(QBUF):
                pool.wait_ge(st_y[k], 16 * (NQ // QBUF))
            for n in range(TOPK * NT):
                t, j = divmod(n, TOPK)
                done(pool, "combined", n - GB)
                g.indirect_dma_start(
                    out=y_got[:, n % GB, :], out_offset=None, in_=ys,
                    in_offset=bass.IndirectOffsetOnAxis(ap=slot_u[:, t, j:j + 1], axis=0)).then_inc(got[n % GB], 16)

        @block.vector
        def _(dve):
            v = nc.vector

            def turned_key_weights():
                dve.wait_ge(ld_w2, 48)
                v.tensor_scalar(w_kr_rot[:, 0:HALF], w_kr_sb[:, HALF:R], -1.0, None, ALU.mult).then_inc(masks, 1)
                v.tensor_copy(w_kr_rot[:, HALF:R], w_kr_sb[:, 0:HALF]).then_inc(masks, 1)

            def band_masks():
                dve.wait_ge(ld_small, 48)
                dve.wait_ge(consts, 13)
                for b in range(BT):
                    v.memset(v_nat[LQ * b:LQ * b + LQ, :, b, 2 * SD:2 * SD + 1], 1.0)
                v.tensor_copy(seg_f[:, :], seg_i[:, :]).then_inc(masks, 1)
                dve.wait_ge(masks, 3)
                dist = xp[:, 0, :, :].rearrange("p h k -> p (h k)").rearrange("p (t k) -> p t k", t=NT)
                dist2 = rt_b[:, :, :].rearrange("p h r -> p (h r)").rearrange("p (t k) -> p t k", t=NT)
                v.tensor_tensor(dist, key_iota[:, :].unsqueeze(1).to_broadcast([P, NT, LK]),
                                seg_f[:, :].unsqueeze(2).to_broadcast([P, NT, LK]), ALU.subtract).then_inc(masks, 1)
                dve.wait_ge(masks, 4)
                v.tensor_scalar(dist2, dist, 0.0, NEG, ALU.is_gt, ALU.mult).then_inc(masks, 1)
                v.tensor_scalar(dist, dist, float(-LOOKBACK), NEG, ALU.is_lt, ALU.mult).then_inc(masks, 1)
                dve.wait_ge(masks, 6)
                v.tensor_tensor(neg_mask[:, :, :], dist, dist2, ALU.add).then_inc(masks, 1)
                dve.wait_ge(masks, 7)

            def keep(n, formed):
                _, dst, src = formed
                dve.wait_ge(su_pe, n + 1)
                v.tensor_copy(dst, src).then_inc(su_ev, 1)

            def s_uvo(g):
                if g == 1:
                    x_stats_of(1)
                keep(4 + g, form_uvo(g))
                if g == 3:
                    v.memset(zeros, 0.0).then_inc(su_ev, 1)

            def norm_stats(t, k, pre, before):
                done(dve, before, t)
                v.memset(held[:, :], 0.0)
                v.bn_stats(stats[:, k, :], x_sb[:, t, :]).then_inc(S[pre + "_stat"], 1)
                done(dve, pre + "_stat", t)
                v.memset(held[:, :], 0.0)
                v.bn_aggr(mv[:, k, :], stats[:, k, :]).then_inc(S[pre + "_aggr"], 1)
                done(dve, pre + "_aggr", t)
                v.tensor_scalar(rstd[:, k, 0:1], mv[:, k, 1:2], EPS, None, ALU.add).then_inc(S[pre + "_veps"], 1)

            def norm_apply(t, k, pre, dst, reader):
                done(dve, pre + "_rstd", t)
                done(dve, reader, t - 1)
                v.tensor_scalar(dst[:, :], x_sb[:, t, :], mv[:, k, 0:1], rstd[:, k, 1:2],
                                ALU.subtract, ALU.mult).then_inc(S[pre + "_norm"], 1)

            def x_stats_of(n):
                tiles = [0] if n == 0 else list(range(1, NT))
                ts = slice(tiles[0], tiles[-1] + 1)
                dve.wait_ge(*((ld_x, 16) if n == 0 else (ld_late, 16 * LATE)))
                for t in tiles:
                    last = v.bn_stats(x_stats[:, t, :], x_sb[:, t, :])
                last.then_inc(S["x_stat"], 1)
                done(dve, "x_stat", n)
                v.memset(held[:, :], 0.0)
                for t in tiles:
                    last = v.bn_aggr(x_mv[:, t, :], x_stats[:, t, :])
                last.then_inc(S["x_aggr"], 1)
                done(dve, "x_aggr", n)
                v.tensor_scalar(x_rs[:, ts, 0], x_mv[:, ts, 1], EPS, None, ALU.add).then_inc(S["x_veps"], 1)

            def x_norm(t):
                if isinstance(t, int) and t == 0:
                    x_stats_of(0)
                dve.wait_ge(S["x_rstd"], 1 if isinstance(t, int) and t == 0 else 2)
                done(dve, "x_nT_pe", t - 1)
                v.tensor_scalar(xn[:, :], x_sb[:, t, :], x_mv[:, t, 0:1], x_rs[:, t, 1:2],
                                ALU.subtract, ALU.mult).then_inc(S["x_norm"], 1)
                if isinstance(t, int) and t == 0:
                    turned_key_weights()

            def x_nT(t):
                done(dve, "x_nT_pe", t)
                done(dve, "x_qcT_pe", t - 1)
                v.tensor_copy(xnT[:, :, :], bank(1)[:, 0:DC * P].rearrange("p (c n) -> p c n", c=DC)).then_inc(S["x_nT"], 1)

            def x_qcT(t):
                done(dve, "x_qcT_pe", t)
                done(dve, "x_qr1_pe", t - 1)
                v.tensor_copy(qcT[:, :], bank(3)[0:QC, 0:P]).then_inc(S["x_qcT"], 1)

            def x_kr(t):
                done(dve, "x_kr_pe", t)
                if isinstance(t, int) and t == 0:
                    dve.wait_ge(ld_small, 48)
                v.tensor_tensor(kr_a[KVC:P, :], bank(0)[KVC:P, 0:BT * LK], rope_k_sb[KVC:P, 0, :], ALU.mult)
                v.tensor_tensor(kr_b[KVC:P, :], bank(0)[KVC:P, BT * LK:2 * BT * LK], rope_k_sb[KVC:P, 1, :], ALU.mult).then_inc(S["x_krb"], 1)
                done(dve, "x_krb", t)
                done(dve, "x_s1_pe", t - 1)
                v.tensor_tensor(KK[KVC:P, :, :], kr_a[KVC:P, :].rearrange("p (b k) -> p b k", b=BT),
                                kr_b[KVC:P, :].rearrange("p (b k) -> p b k", b=BT), ALU.add).then_inc(S["x_kr"], 1)
                if isinstance(t, int) and t == 0:
                    for g in range(4):
                        keep(g, form_uqk(g))
                    band_masks()

            def x_rope(t, half):
                done(dve, f"x_qr{half}_pe", t)
                done(dve, "x_qt_pe3", t - 1)
                hh = H // 2
                for n, b in [(half, (4, 0)[half])]:
                    src = bank(b).rearrange("p (h r) -> p h r", h=hh)
                    hs = slice(hh * n, hh * n + hh)
                    cos = rope_q_sb[:, 0, :].unsqueeze(1).to_broadcast([P, hh, R])
                    v.tensor_tensor(QN[:, hs, KVC:], src, cos, ALU.mult)
                    done(dve, f"x_qn{n}", t - 1)
                    for lo, hi in ((0, HALF), (HALF, 0)):
                        sin = rope_q_sb[:, 1, lo:lo + HALF].unsqueeze(1).to_broadcast([P, hh, HALF])
                        last = v.tensor_tensor(rt_b[:, hs, lo:lo + HALF], src[:, :, hi:hi + HALF], sin, ALU.mult)
                    last.then_inc(S[f"x_sin{n}"], 1)
                    done(dve, f"x_sin{n}", t)
                    v.tensor_tensor(QN[:, hs, KVC:], QN[:, hs, KVC:], rt_b[:, hs, :], ALU.add).then_inc(S[f"x_qn{n}"], 1)

            def x_soft(t, b):
                s = ps[:, 2 * b:2 * b + 2, :].rearrange("p a (h k) -> p (a h) k", k=LK)
                done(dve, f"x_s{b}_pe", t)
                v.tensor_reduce(x_max[:, b, :], s, AX.X, ALU.max).then_inc(S[f"x_mx{b}"], 1)
                done(dve, f"x_mx{b}", t)
                done(dve, f"x_ph{b}_pe", t - 1)
                v.tensor_tensor(xp[:, b, :, :], s, x_max[:, b, :].unsqueeze(2).to_broadcast([P, HPAIR, LK]),
                                ALU.subtract).then_inc(S[f"x_sub{b}"], 1)

            def x_ph(t, b):
                done(dve, f"x_ph{b}_pe", t)
                done(dve, f"x_o{b}_pe", t - 1)
                v.tensor_copy(xpT[:, b, 4:8, :], bank((0, 3)[b]).rearrange("p (h n) -> p h n", h=4)).then_inc(S[f"x_ph{b}"], 1)

            def x_on(t, b):
                banks = ((1, 4), (0, 2))[b]
                done(dve, f"x_o{b}_pe", t)
                for n, k in enumerate(banks):
                    o = bank(k)[:, 0:4 * (KVC + 1)].rearrange("p (h c) -> p h c", h=4)
                    v.reciprocal(x_rec[:, b, 4 * n:4 * n + 4], o[:, :, KVC]).then_inc(S[f"x_rec{b}"], 1)
                dve.wait_ge(S[f"x_rec{b}"], 2 * t + 2)
                done(dve, f"x_ot{b}_pe", t - 1)
                for n, k in enumerate(banks):
                    o = bank(k)[:, 0:4 * (KVC + 1)].rearrange("p (h c) -> p h c", h=4)
                    last = v.tensor_tensor(ON[:, b, 4 * n:4 * n + 4, :], o[:, :, 0:KVC],
                                           x_rec[:, b, 4 * n:4 * n + 4].unsqueeze(2).to_broadcast([P, 4, KVC]), ALU.mult)
                last.then_inc(S[f"x_on{b}"], 1)

            def x_res(t):
                done(dve, "x_y_pe", t)
                done(dve, "x_norm", t)
                v.tensor_tensor(x_sb[:, t, :], x_sb[:, t, :], bank(4)[:, 0:D], ALU.add).then_inc(S["x_res"], 1)

            def a_stats(t):
                norm_stats(t, 1, "a", "x_res")

            def a_norm(t):
                norm_apply(t, 1, "a", an, "a_nT_pe")

            def a_nT(t):
                done(dve, "a_nT_pe", t)
                done(dve, "a_v_pe", t - 1)
                v.tensor_copy(anT[:, :, :], bank(5)[:, 0:DC * P].rearrange("p (c n) -> p c n", c=DC)).then_inc(S["a_nT"], 1)

            def a_v(t):
                done(dve, "a_v_pe", t)
                done(dve, "a_o_pe", t - 1)
                for b in range(BT):
                    rows = slice(LQ * b, LQ * b + LQ)
                    last = v.tensor_tensor(v_nat[rows, :, b, 0:2 * SD],
                                           bank(7)[rows, 0:D].rearrange("p (h d) -> p h d", h=HPAIR),
                                           bv_sb[rows, :].rearrange("p (h d) -> p h d", h=HPAIR), ALU.add)
                last.then_inc(S["a_v"], 1)

            def a_soft(t):
                s = ps[:, 5:7, :].rearrange("p b (h k) -> p b h k", k=LQ)
                done(dve, "a_s_pe", t)
                v.tensor_reduce(a_max[:, :, :], s, AX.X, ALU.max).then_inc(S["a_mx"], 1)

            def a_less_max(t):
                s = ps[:, 5:7, :].rearrange("p b (h k) -> p b h k", k=LQ)
                done(dve, "a_mx", t)
                done(dve, "a_ph_pe", t - 1)
                for b in range(BT):
                    last = v.tensor_tensor(ap[:, :, b, :], s[:, b, :, :],
                                           a_max[:, b, :].unsqueeze(2).to_broadcast([P, HPAIR, LQ]), ALU.subtract)
                last.then_inc(S["a_sub"], 1)

            def a_on(t):
                w = 2 * SD + 1
                o = ps[:, 6:8, :].rearrange("p a (h n) -> p (a h) n", n=P)[:, :, 0:BT * w].rearrange(
                    "p h (b d) -> p b h d", b=BT)
                done(dve, "a_o_pe", t)
                v.reciprocal(a_rec[:, :, :], o[:, :, :, 2 * SD]).then_inc(S["a_rec"], 1)
                done(dve, "a_rec", t)
                done(dve, "a_ot_pe", t - 1)
                for par in range(2):
                    rows = slice(LQ * par, LQ * par + LQ)
                    last = v.tensor_tensor(
                        aON[rows, :, :, :], o[rows, :, :, SD * par:SD * par + SD],
                        a_rec[rows, :, :].unsqueeze(3).to_broadcast([LQ, BT, HPAIR, SD]), ALU.mult)
                last.then_inc(S["a_on"], 1)

            def a_res(t):
                done(dve, "a_y_pe", t)
                done(dve, "a_resb", t)
                v.tensor_tensor(x_sb[:, t, :], x_sb[:, t, :], bank(6)[:, 0:D], ALU.add).then_inc(S["a_res"], 1)

            def r_norm(t):
                def step(n, ins):
                    ins.then_inc(S["r_pick"], 1)
                    dve.wait_ge(S["r_pick"], PICKS * t + n)
                done(dve, "a_res", t)
                v.memset(held[:, :], 0.0)
                step(1, v.bn_stats(stats[:, 2, :], x_sb[:, t, :]))
                v.memset(held[:, :], 0.0)
                step(2, v.bn_aggr(mv[:, 2, :], stats[:, 2, :]))
                step(3, v.tensor_scalar(rstd[:, 2, 0:1], mv[:, 2, 1:2], EPS, None, ALU.add))
                done(dve, "r_rstd", t)
                if not is_last(t):
                    done(dve, "r_T_pe", t - 1)
                    if not isinstance(t, int) or t > 0:
                        dve.wait_ge(scattered, 16 * TOPK * t)
                v.tensor_scalar(normed(t), x_sb[:, t, :], mv[:, 2, 0:1], rstd[:, 2, 1:2],
                                ALU.subtract, ALU.mult).then_inc(S["r_pick"], 1)

            def r_choose(t, part):
                def step(n, ins):
                    ins.then_inc(S["r_pick"], 1)
                    dve.wait_ge(S["r_pick"], PICKS * t + n)
                if part == 1:
                    choose_rest(t, step)
                    return
                done(dve, "r_l_pe", t)
                dve.wait_ge(ld_r, 32)
                dve.wait_ge(su_ev, SETUP)
                logits_t = bank(7)[:, D:D + E]
                v.tensor_copy(logit[:, t, :], logits_t).then_inc(S["r_pick"], 1)
                step(6, v.tensor_tensor(biased[:, :], logits_t, rb_sb[:, :], ALU.add))
                v.memset(held[:, :], 0.0)
                step(7, v.max(top_v[:, :], biased[:, :]))
                v.memset(held[:, :], 0.0)
                v.max_index(top_i[:, :], top_v[:, :], biased[:, :]).then_inc(S["r_pick"], 1)

            def choose_rest(t, step):
                dve.wait_ge(S["r_pick"], PICKS * t + 8)
                step(9, v.tensor_copy(top_f[:, :], top_i[:, :]))
                step(10, v.tensor_tensor(is_all[:, t, :, :], e_iota[:, :].unsqueeze(1).to_broadcast([P, TOPK, E]),
                                         top_f[:, 0:TOPK].unsqueeze(2).to_broadcast([P, TOPK, E]), ALU.is_equal))
                step(11, v.tensor_reduce(chosen[:, t, :], is_all[:, t, :, :].rearrange("p j e -> p e j"), AX.X,
                                         ALU.add))
                done(dve, "r_rank_pe", t - 1)
                v.memset(held[:, :], 0.0)
                v.tensor_copy(chosen_now[:, :], chosen[:, t, :]).then_inc(S["r_pick"], 1)

            def r_slots(t, part):
                def wave(n, *ins):
                    ins[-1].then_inc(S["r_slot"], 1)
                    dve.wait_ge(S["r_slot"], WAVES * t + n)
                local, add, cnt, rank, more, flag, ids, diff, over, slot, tmp = (wk[:, n, :] for n in range(11))
                if part == 0:
                    done(dve, "r_rank_pe", t)
                    wave(1, v.tensor_copy(wk[:, 0:2, :], bank(6)[:, 0:2 * E].rearrange("p (a e) -> p a e", a=2)))
                    wave(2, v.tensor_tensor(cnt, tokens_of, add, ALU.add),
                         v.tensor_tensor(rank, tokens_of, local, ALU.add))
                    wave(3, v.tensor_tensor(more, cnt, room_of, ALU.is_gt),
                         v.tensor_copy(tokens_of, cnt),
                         v.tensor_tensor(over, rank, room_of, ALU.is_ge),
                         v.tensor_tensor(slot, rank, last_of, ALU.add))
                    wave(4, v.tensor_scalar(flag, more, float(CAP), None, ALU.mult),
                         v.tensor_tensor(slot, slot, room_of, ALU.subtract))
                    wave(5, v.tensor_tensor(room_of, room_of, flag, ALU.add))
                    return
                v.memset(held[:, :], 0.0)
                wave(6, v.tensor_tensor(tmp, flag, e_scaled[:, :], ALU.mult),
                     v.tensor_tensor_scan(ids, ones_f[:, 0:E], flag, blocks_all, ALU.mult, ALU.add))
                wave(7, v.tensor_copy(blocks_all, ids[:, E - 1:E]),
                     v.tensor_tensor(diff, ids, last_of, ALU.subtract),
                     v.scalar_tensor_tensor(tmp, ids, block_1[:, 0:1], tmp, ALU.is_equal, ALU.mult))
                wave(8, v.scalar_tensor_tensor(over, diff, float(-CAP), over, ALU.add, ALU.mult),
                     v.scalar_tensor_tensor(flag, flag, 1.0 / CAP, diff, ALU.mult, ALU.mult),
                     v.tensor_reduce(sum_1[:, :], tmp, AX.X, ALU.add))
                wave(9, v.tensor_tensor(slot, slot, over, ALU.add),
                     v.tensor_tensor(last_of, last_of, flag, ALU.add),
                     v.tensor_tensor(eid_col, eid_col, sum_1[:, :], ALU.add))
                row_slots = picked[:, 0:TOPK, :]
                wave(10, v.tensor_tensor(row_slots, is_all[:, t, :, :],
                                         slot.unsqueeze(1).to_broadcast([P, TOPK, E]), ALU.mult))
                wave(11, v.tensor_reduce(slot_f[:, :], row_slots, AX.X, ALU.add))
                if is_last(t):
                    dve.wait_ge(scattered, 16 * TOPK * t)
                v.tensor_copy(slot_now[:, :], slot_f[:, :])
                v.tensor_copy(slot_u[:, t, :], slot_f[:, :]).then_inc(S["r_slot"], 1)

            def e_beat(u):
                shared_hidden(dve, v, u)
                if u >= 2:
                    shared_result(dve, v, u - 2)

            run_tiles(dve, {
                "s": s_uvo,
                ("x", 1): x_norm, ("x", 2): x_nT, ("a", 0): a_stats, ("x", 4): x_qcT, ("a", 0.5): a_norm, ("a", 1): a_nT,
                ("x", 6): x_kr, ("a", 3): a_v, ("x", 7.5): lambda t: x_rope(t, 0), ("x", 8): lambda t: x_rope(t, 1), ("a", 4.5): a_soft, ("a", 4.6): a_less_max,
                ("x", 10): lambda t: x_soft(t, 0), ("x", 11): lambda t: x_soft(t, 1),
                ("x", 12): lambda t: x_ph(t, 0), ("x", 14): lambda t: x_ph(t, 1),
                ("x", 13): lambda t: x_on(t, 0), ("a", 6): a_on,
                ("x", 15): lambda t: x_on(t, 1), ("b", 2): a_res, ("y", 18): x_res, ("b", 3): r_norm, ("b", 6): lambda t: r_choose(t, 0), ("b", 6.5): lambda t: r_choose(t, 1),
                ("b", 7.5): lambda t: r_slots(t, 0), ("b", 9): lambda t: r_slots(t, 1), "f": e_beat})

            steps = [0]

            def link(ins):
                steps[0] += 1
                ins.then_inc(route, 1)
                dve.wait_ge(route, steps[0])

            def over_e(a):
                return a.unsqueeze(2).to_broadcast([P, NT, E])

            for u in range(E_ROUND, E_EID):
                e_beat(u)
            dve.wait_ge(eid_pe, 1)
            v.tensor_copy(eid_i[:, :], bank(5)[0:1, 0:P]).then_inc(eid_ready, 1)
            link(v.tensor_reduce(row_s[:, 0, :], logit[:, :, :], AX.X, ALU.max))
            link(v.tensor_tensor(logit[:, :, :], logit[:, :, :], over_e(row_s[:, 0, :]), ALU.subtract))
            assert steps[0] == SUB_STEPS, steps
            for u in range(E_EID, E_PRE):
                e_beat(u)
            dve.wait_ge(route_ex, 1)
            link(v.tensor_tensor(comb[:, :, :], chosen[:, :, :], logit[:, :, :], ALU.mult))
            link(v.tensor_reduce(row_s[:, 1, :], comb[:, :, :], AX.X, ALU.add))
            link(v.reciprocal(row_s[:, 2, :], row_s[:, 1, :]))
            link(v.tensor_tensor(comb[:, :, :], comb[:, :, :], over_e(row_s[:, 2, :]), ALU.mult))
            for j in range(TOPK):
                link(v.tensor_tensor(picked[:, :, :], is_all[:, :, j, :], comb[:, :, :], ALU.mult))
                link(v.tensor_reduce(gate_j[:, j, :], picked[:, :, :], AX.X, ALU.add))
            assert steps[0] == GATE_STEPS, steps

            def quad(g, k, i):
                done(dve, "q_silu", g)
                done(dve, "q_hT_pe", g - 1)
                up = bank(2).rearrange("p (j w f) -> p j w f", j=QB, w=2)[:, :, 1, :]
                v.tensor_tensor(hid_q, sil_q.unsqueeze(2).to_broadcast([P, QB, 2, F]),
                                up.unsqueeze(2).to_broadcast([P, QB, 2, F]), ALU.mult).then_inc(S["q_hid"], 1)
                if not (isinstance(g, int) and g < 1):
                    y_copy(g - 1, (k - 1) % QBUF, i if k else i - 1)
                done(dve, "q_hT_pe", g)
                done(dve, "q_down_pe", g - 1)
                v.tensor_copy(hT_q, bank(3)).then_inc(S["q_hT"], 1)

            def y_copy(g, k, i):
                done(dve, "q_down_pe", g)
                if g_not_first(g):
                    dve.wait_ge(st_y[k], 16 * i)
                v.tensor_copy(y_blk[k].rearrange("p (j h n) -> p h j n", j=QB, h=2),
                              ps[:, 4:6, :].rearrange("p h (j n) -> p h j n", j=QB)).then_inc(S["q_y"], 1)
            run_quads(dve, quad)
            y_copy(NQ - 1, QBUF - 1, NQ // QBUF - 1)

            u = E_PRE
            for n in range(TOPK * NT):
                if n % 5 == 2 and u < NT:
                    e_beat(u)
                    u += 1
                elif n % 5 == 2 and u < NT + 2:
                    shared_result(dve, v, u - 2)
                    u += 1
                t, j = divmod(n, TOPK)
                if j == 0:
                    assert t <= u - 3, (t, u)
                dve.wait_ge(got[n % GB], 16 * (n // GB + 1))
                done(dve, "combined", n - 1)
                v.scalar_tensor_tensor(x_sb[:, t, :], y_got[:, n % GB, :], gate_j[:, j, t:t + 1], x_sb[:, t, :],
                                       ALU.mult, ALU.add).then_inc(S["combined"], 1)

        @block.scalar
        def _(act):
            s = nc.scalar
            for dst, src, s_ld in (
                    (x_sb[:, 0, :], xr[:, 0, :], ld_x),
                    (w_kvc_sb[:, :, :], w_kvc.rearrange("(c p) n -> p c n", p=P), ld_w2),
                    (w_dq_sb[:, :, :], w_dq.rearrange("(c p) n -> p c n", p=P), ld_w2),
                    (w_kr_sb[:, :], w_kr, ld_w2), (rope_k_sb[KVC:P, :, :], rope_k, ld_small),
                    (seg_i[:, :], seg, ld_small), (rope_q_sb[:, :, :], rope_q, ld_small)):
                act.dma_start(dst, src).then_inc(s_ld, 16)

            def x_ctxT(t):
                done(act, "x_ctxT_pe", t)
                done(act, "x_kvT_pe", t - 1)
                s.copy(ctxT[:, :, :, :], bank(0).rearrange("p (c b k) -> p c b k", c=DC, b=BT)).then_inc(S["x_ctxT"], 1)

            def x_kvT(t):
                done(act, "x_kvT_pe", t)
                done(act, "x_s1_pe", t - 1)
                s.copy(KK[0:KVC, :, :], bank(2)[0:KVC, 0:BT * LK].rearrange("p (b k) -> p b k", b=BT)).then_inc(S["x_kvT"], 1)

            def x_kvn(t):
                done(act, "x_kvn_pe", t)
                done(act, "x_o1_pe", t - 1)
                if isinstance(t, int) and t == 0:
                    act.wait_ge(consts, 13)
                s.copy(kv_nat[:, :, 0:KVC], bank(1)[:, 0:BT * KVC].rearrange("p (b c) -> p b c", b=BT)).then_inc(S["x_kvn"], 1)

            def x_q(t):
                done(act, "x_q_pe", t)
                done(act, "x_qt_pe3", t - 1)
                s.copy(QN[:, :, 0:KVC], ps[:, 2:4, :].rearrange("p a (h c) -> p (a h) c", c=KVC)).then_inc(S["x_q"], 1)

            def x_qt(t):
                for g in range(4):
                    done(act, f"x_qt_pe{g}", t)
                    if g == 0:
                        done(act, "x_s1_pe", t - 1)
                    s.copy(QT[:, :, 4 * g:4 * g + 4, :],
                           bank(1 + g).rearrange("p (h b q) -> p b h q", h=4, b=BT)).then_inc(S[f"x_qt{g}"], 1)

            def x_exp(t, b):
                done(act, f"x_sub{b}", t)
                s.activation(xp[:, b, :, :], xp[:, b, :, :], ACT.Exp, scale=XSCALE).then_inc(S[f"x_exp{b}"], 1)

            def x_pl(t, b):
                done(act, f"x_pl{b}_pe", t)
                done(act, f"x_o{b}_pe", t - 1)
                s.copy(xpT[:, b, 0:4, :], bank((4, 2)[b]).rearrange("p (h n) -> p h n", h=4)).then_inc(S[f"x_pl{b}"], 1)

            def x_ot(t, b):
                done(act, f"x_ot{b}_pe", t)
                done(act, "x_y_pe", t - 1)
                s.copy(OT[:, :, :, b, :], bank((1, 3)[b]).rearrange("p (k r q) -> p k r q", k=H // 4, r=2)).then_inc(S[f"x_ot{b}"], 1)

            def a_qk(t):
                done(act, "a_qk_pe", t)
                if not isinstance(t, int) or t > 0:
                    act.wait_ge(S["a_qbd"], 4 * t)
                q = bank(6).rearrange("p (c n) -> p c n", c=2 * DC)
                for c in range(DC):
                    last = s.activation(qT[:, c, :], q[:, c, :], ACT.Identity, bias=bqk_sb[:, c:c + 1])
                last.then_inc(S["a_q"], 1)
                done(act, "a_s_pe", t - 1)
                for c in range(DC):
                    last = s.activation(kT[:, c, :], q[:, DC + c, :], ACT.Identity, bias=bqk_sb[:, DC + c:DC + c + 1])
                last.then_inc(S["a_k"], 1)

            def a_exp(t):
                done(act, "a_sub", t)
                s.activation(ap[:, :, :, :], ap[:, :, :, :], ACT.Exp, scale=ASCALE).then_inc(S["a_exp"], 1)

            def a_pl(t):
                done(act, "a_pl_pe", t)
                done(act, "a_o_pe", t - 1)
                s.copy(apT[:, 0:4, :], bank(7).rearrange("p (h n) -> p h n", h=4)).then_inc(S["a_pl"], 1)
                done(act, "a_ph_pe", t)
                s.copy(apT[:, 4:8, :], bank(5).rearrange("p (h n) -> p h n", h=4)).then_inc(S["a_ph"], 1)

            def a_ot(t):
                done(act, "a_ot_pe", t)
                done(act, "a_y_pe", t - 1)
                s.copy(aOT[:, :, :, :], bank(5)[:, 0:2 * P].rearrange("p (b r q) -> p r b q", b=BT, r=2)).then_inc(S["a_ot"], 1)

            def r_T(t):
                done(act, "r_T_pe", t)
                done(act, "r_l_pe", t - 1)
                src = bank(7)[:, 0:D].rearrange("p (c n) -> p c n", c=DC)
                s.copy(rnT[:, :, :], src).then_inc(S["r_T"], 1)
                s.copy(xT[:, :, t, :], src).then_inc(S["r_T"], 1)

            def turned(u):
                done(act, "f_hT_pe", u)
                done(act, "f_y_pe", u - 2)
                s.copy(hidT[:, u % 2, :], bank(4)).then_inc(S["f_hT"], 1)

            def e_beat(u):
                done(act, "f_gu_pe", u)
                done(act, "f_hid", u - 2)
                s.activation(silu[:, u % 2, :], bank(u % 2), ACT.Silu).then_inc(S["f_silu"], 1)
                if u > 0:
                    turned(u - 1)

            run_tiles(act, {
                "f": e_beat,
                ("x", 1): x_ctxT, ("x", 3): x_kvT, ("a", 2): a_qk, ("x", 5): x_kvn, ("x", 7): x_q,
                ("x", 9): x_qt, ("a", 4.7): a_exp, ("x", 10): lambda t: x_exp(t, 0),
                ("x", 12.5): lambda t: x_exp(t, 1), ("a", 5): a_pl,
                ("x", 12): lambda t: x_pl(t, 0), ("x", 14): lambda t: x_pl(t, 1),
                ("b", 1): a_ot, ("b", 4): r_T, ("x", 16): lambda t: x_ot(t, 0), ("x", 17): lambda t: x_ot(t, 1)})

            for u in range(E_ROUND, E_EID):
                e_beat(u)
            act.wait_ge(route, SUB_STEPS)
            s.activation(logit[:, :, :], logit[:, :, :], ACT.Exp).then_inc(route_ex, 1)
            for u in range(E_EID, E_PRE):
                e_beat(u)

            def xT_copy(g):
                done(act, "q_xT_pe", g)
                done(act, "q_up_pe", g - 1)
                s.copy(xT_q.rearrange("p (a n) -> p a n", a=2), ps[:, 0:2, :]).then_inc(S["q_xT"], 1)

            def quad(g, k, i):
                done(act, "q_up_pe", g)
                done(act, "q_hid", g - 1)
                gate = bank(2).rearrange("p (j w f) -> p j w f", j=QB, w=2)[:, :, 0, :]
                s.activation(sil_q, gate, ACT.Silu).then_inc(S["q_silu"], 1)
                if not (isinstance(g, int) and g == NQ - 1):
                    xT_copy(g + 1)
            xT_copy(0)
            run_quads(act, quad)
            for u in range(E_PRE, NT):
                e_beat(u)
            turned(NT - 1)

        @block.tensor
        def _(pe):
            m = nc.tensor
            pe.wait_ge(consts, 13)
            def tr(dst, src):
                return m.transpose(dst, src, ident[0:src.shape[0], 0:src.shape[0]])

            def form(formed):
                for dst, a, b in formed[0]:
                    last = m.matmul(dst, a, b, start=True, stop=True)
                last.then_inc(su_pe, 1)

            def s_uvo(g):
                if g == 0:
                    pe.wait_ge(ld_late, 16 * LATE)
                    pe.wait_ge(su_ev, 4)
                if g == 3:
                    pe.wait_ge(su_ev, 5)
                form(form_uvo(g))

            def x_ctxT(t):
                pe.wait_ge(ld_ctx, 16 * t + 16)
                done(pe, "x_on1", t - 1)
                for c in range(DC):
                    for b in range(BT):
                        last = tr(bank(0)[:, (c * BT + b) * P:(c * BT + b + 1) * P], ctx_sb[:, b, c * P:(c + 1) * P])
                last.then_inc(S["x_ctxT_pe"], 1)

            def x_nT(t):
                done(pe, "x_norm", t)
                done(pe, "x_ot0", t - 1)
                for c in range(DC):
                    last = tr(bank(1)[:, c * P:(c + 1) * P], xn[:, c * P:(c + 1) * P])
                last.then_inc(S["x_nT_pe"], 1)

            def x_kvT(t):
                done(pe, "x_ctxT", t)
                if isinstance(t, int) and t == 0:
                    pe.wait_ge(ld_w2, 48)
                    pe.wait_ge(masks, 2)
                done(pe, "x_on1", t - 1)
                for c in range(DC):
                    last = m.matmul(bank(2)[0:KVC, 0:BT * LK], w_kvc_sb[:, c, :], ctxT[:, c, :, :],
                                    start=(c == 0), stop=(c == DC - 1))
                last.then_inc(S["x_kvT_pe"], 1)

            def x_qcT(t):
                done(pe, "x_nT", t)
                done(pe, "x_ot1", t - 1)
                for c in range(DC):
                    last = m.matmul(bank(3)[0:QC, 0:P], w_dq_sb[:, c, :], xnT[:, c, :],
                                    start=(c == 0), stop=(c == DC - 1))
                last.then_inc(S["x_qcT_pe"], 1)

            def x_kr(t):
                m.matmul(bank(0)[KVC:P, 0:BT * LK], w_kr_sb[:, :], KK[0:KVC, :, :], start=True, stop=True)
                m.matmul(bank(0)[KVC:P, BT * LK:2 * BT * LK], w_kr_rot[:, :], KK[0:KVC, :, :],
                         start=True, stop=True).then_inc(S["x_kr_pe"], 1)

            def x_kvn(t):
                done(pe, "x_kvT", t)
                for b in range(BT):
                    last = m.matmul(bank(1)[:, b * KVC:(b + 1) * KVC], KK[0:KVC, b, :], ident[0:KVC, 0:KVC],
                                    start=True, stop=True)
                last.then_inc(S["x_kvn_pe"], 1)

            def x_q(t):
                done(pe, "x_qcT", t)
                if isinstance(t, int) and t == 0:
                    for g in range(4):
                        if g == 3:
                            pe.wait_ge(su_ev, 1)
                        form(form_uqk(g))
                    pe.wait_ge(su_ev, 4)
                for n in range(2):
                    last = m.matmul(bank(2 + n), qcT[:, :], uqk_sb[:, 8 * n:8 * n + 8, :], start=True, stop=True)
                last.then_inc(S["x_q_pe"], 1)

            def x_qr(t, n):
                if n == 0:
                    if isinstance(t, int) and t == 0:
                        pe.wait_ge(ld_w1, 48)
                    done(pe, "x_qcT", t)
                    done(pe, "x_res", t - 1)
                else:
                    done(pe, "x_krb", t)
                m.matmul(bank((4, 0)[n]), qcT[:, :], w_qr_sb[:, 512 * n:512 * n + 512],
                         start=True, stop=True).then_inc(S[f"x_qr{n}_pe"], 1)

            def x_qt(t, half):
                if half == 0:
                    done(pe, "x_q", t)
                    done(pe, "x_kvn", t)
                done(pe, f"x_qn{half}", t)
                for g in (2 * half, 2 * half + 1):
                    for h in range(4):
                        last = tr(bank(1 + g)[:, h * P:(h + 1) * P], QN[:, 4 * g + h, :])
                    last.then_inc(S[f"x_qt_pe{g}"], 1)

            def x_s(t, b):
                if b == 0:
                    done(pe, "x_kr", t)
                    if isinstance(t, int) and t == 0:
                        pe.wait_ge(masks, 7)
                for a in range(2):
                    if b == 0:
                        done(pe, f"x_qt{2 * a}", t)
                        done(pe, f"x_qt{2 * a + 1}", t)
                    for h in range(4):
                        p = 4 * a + h
                        m.matmul(bank(2 * b + a)[:, h * LK:(h + 1) * LK],
                                 QT[:, b, 2 * p:2 * p + 2, :], KK[:, b, :], start=(h == 0), stop=False,
                                 skip_group_check=True)
                    last = m.matmul(bank(2 * b + a), pick[:, b, :, :],
                                    neg_mask[:, t, :].unsqueeze(1).to_broadcast([P, 4, LK]),
                                    start=False, stop=True, skip_group_check=True)
                last.then_inc(S[f"x_s{b}_pe"], 1)

            def x_p(t, b):
                done(pe, f"x_exp{b}", t)
                lo, hi = ((4, 0), (2, 3))[b]
                for name, k, p0 in ((f"x_pl{b}_pe", lo, 0), (f"x_ph{b}_pe", hi, 4)):
                    for h in range(4):
                        last = tr(bank(k)[:, h * P:(h + 1) * P], xp[:, b, p0 + h, :])
                    last.then_inc(S[name], 1)

            def x_o(t, b):
                done(pe, f"x_pl{b}", t)
                done(pe, f"x_ph{b}", t)
                w = KVC + 1
                for n, k in enumerate(((1, 4), (0, 2))[b]):
                    for h in range(4):
                        last = m.matmul(bank(k)[:, h * w:(h + 1) * w], xpT[:, b, 4 * n + h, :], kv_nat[:, b, :],
                                        start=True, stop=True)
                last.then_inc(S[f"x_o{b}_pe"], 1)

            def x_ot(t, b):
                done(pe, f"x_on{b}", t)
                for k in range(H // 4):
                    last = tr(bank((1, 3)[b])[:, k * P:(k + 1) * P], ON[:, b, 2 * k:2 * k + 2, :])
                last.then_inc(S[f"x_ot{b}_pe"], 1)

            def x_y(t):
                done(pe, "x_ot0", t)
                done(pe, "x_ot1", t)
                if isinstance(t, int) and t == 0:
                    pe.wait_ge(su_ev, SETUP)
                for n in range(H // 2):
                    k, par = n // 2, n % 2
                    last = m.matmul(bank(4)[:, 0:D], OT[:, k, par, :, :], uvo_sb[:, k, par, :],
                                    start=(n == 0), stop=(n == H // 2 - 1))
                last.then_inc(S["x_y_pe"], 1)

            def a_nT(t):
                done(pe, "a_norm", t)
                done(pe, "a_ot", t - 1)
                for c in range(DC):
                    last = tr(bank(5)[:, c * P:(c + 1) * P], an[:, c * P:(c + 1) * P])
                last.then_inc(S["a_nT_pe"], 1)

            def a_qk(t):
                done(pe, "a_nT", t)
                done(pe, "a_res", t - 1)
                for n in range(2 * DC):
                    for c in range(DC):
                        last = m.matmul(bank(6)[:, n * P:(n + 1) * P], w_qkvT[:, c, n * P:(n + 1) * P],
                                        anT[:, c, :], start=(c == 0), stop=(c == DC - 1))
                last.then_inc(S["a_qk_pe"], 1)

            def a_v(t):
                done(pe, "a_on", t - 1)
                for c in range(DC):
                    last = m.matmul(bank(7)[:, 0:D], anT[:, c, :], w_qkvT[:, c, 2 * D:3 * D],
                                    start=(c == 0), stop=(c == DC - 1))
                last.then_inc(S["a_v_pe"], 1)

            def a_s(t):
                pe.wait_ge(S["a_qbd"], 4 * t + 4)
                done(pe, "a_k", t)
                for b in range(BT):
                    for p in range(HPAIR):
                        c, h = divmod(2 * p, P // SD)
                        m.matmul(bank(5 + b)[:, p * LQ:(p + 1) * LQ], qbd[:, b, c, h:h + 2, :],
                                 kT[:, c, b * LQ:(b + 1) * LQ], start=(p == 0), stop=False,
                                 skip_group_check=True)
                    last = m.matmul(bank(5 + b), pick[:, b, :, :],
                                    causal[:, b, :].unsqueeze(1).to_broadcast([P, HPAIR, LQ]),
                                    start=False, stop=True, skip_group_check=True)
                last.then_inc(S["a_s_pe"], 1)

            def a_p(t):
                done(pe, "a_exp", t)
                done(pe, "a_v", t)
                if not isinstance(t, int) or t > 0:
                    pe.wait_ge(S["r_pick"], PICKS * (t - 1) + 6)
                for name, k, p0 in (("a_pl_pe", 7, 0), ("a_ph_pe", 5, 4)):
                    for h in range(4):
                        last = tr(bank(k)[:, h * P:(h + 1) * P], ap[:, p0 + h, :, :])
                    last.then_inc(S[name], 1)

            def a_o(t):
                done(pe, "a_pl", t)
                done(pe, "a_ph", t)
                if not isinstance(t, int) or t > 0:
                    pe.wait_ge(S["r_slot"], WAVES * (t - 1) + 1)
                w = BT * (2 * SD + 1)
                for p in range(HPAIR):
                    last = m.matmul(bank(6 + p // 4)[:, (p % 4) * P:(p % 4) * P + w], apT[:, p, :], v_nat[:, p, :, :],
                                    start=True, stop=True)
                last.then_inc(S["a_o_pe"], 1)

            def a_ot(t):
                done(pe, "a_on", t)
                for b in range(BT):
                    last = tr(bank(5)[:, b * P:(b + 1) * P], aON[:, b, :, :])
                last.then_inc(S["a_ot_pe"], 1)

            def a_y(t):
                done(pe, "a_ot", t)
                for par in range(2):
                    last = m.matmul(bank(6)[:, 0:D], aOT[:, par, :, :], w_outT[:, par, :],
                                    start=(par == 0), stop=(par == 1))
                last.then_inc(S["a_y_pe"], 1)

            def r_T(t):
                pe.wait_ge(S["r_pick"], PICKS * t + 4)
                done(pe, "a_v", t + 1) if not (isinstance(t, int) and t == NT - 1) else None
                pe.wait_ge(ld_r, 32)
                odd_even = normed(t).rearrange("p (n c) -> p c n", c=DC)
                for c in range(DC):
                    last = tr(bank(7)[:, c * P:(c + 1) * P], odd_even[:, c, :])
                last.then_inc(S["r_T_pe"], 1)

            def r_l(t):
                pe.wait_ge(S["r_T"], 2 * t + 2)
                for c in range(DC):
                    last = m.matmul(bank(7)[:, D:D + E], rnT[:, c, :], rw_sb[:, c, :],
                                    start=(c == 0), stop=(c == DC - 1))
                last.then_inc(S["r_l_pe"], 1)

            def up_products(u):
                k = u % 2
                if u == 0:
                    pe.wait_ge(ld_shared, 48)
                    done(pe, "x_res", NT - 1)
                pe.wait_ge(S["r_T"], 2 * u + 2)
                done(pe, "f_silu", u - 2)
                done(pe, "f_hid", u - 1)
                gate, up, _ = halves(shared)
                for w, b in ((gate, k), (up, 2)):
                    w = w.rearrange("p (s c n) -> p c s n", s=NSH, c=DC)
                    for c in range(DC):
                        last = m.matmul(bank(b), xT[:, c, u, :], w[:, c, :, :], start=(c == 0), stop=(c == DC - 1))
                last.then_inc(S["f_gu_pe"], 1)

            def down_products(u):
                done(pe, "f_hT", u)
                done(pe, "f_acc", u - 1)
                _, _, down = halves(shared)
                for n in range(4):
                    last = m.matmul(bank(3)[:, 0:D], hidT[:, u % 2, n * P:(n + 1) * P], down[:, n, :],
                                    start=(n == 0), stop=(n == 3))
                last.then_inc(S["f_y_pe"], 1)

            def turn_hidden(u):
                done(pe, "f_hid", u)
                done(pe, "f_hT", u - 1)
                for n in range(4):
                    last = tr(bank(4)[:, n * P:(n + 1) * P], hid[:, u % 2, n * P:(n + 1) * P])
                last.then_inc(S["f_hT_pe"], 1)

            def e_beat(u):
                up_products(u)
                if u >= 2:
                    down_products(u - 2)
                if u >= 1:
                    turn_hidden(u - 1)

            def r_rank(t):
                pe.wait_ge(S["r_pick"], PICKS * t + 12)
                done(pe, "a_res", t)
                m.matmul(bank(6)[:, 0:E], tri[:, :], chosen_now[:, :], start=True, stop=True)
                m.matmul(bank(6)[:, E:2 * E], ones_b[:, :], chosen_now[:, :],
                         start=True, stop=True).then_inc(S["r_rank_pe"], 1)

            run_tiles(pe, {
                "s": s_uvo, "e": e_beat, ("b", 7): r_rank,
                ("x", 1): x_ctxT, ("x", 2): x_nT, ("a", 1): a_nT, ("x", 3): x_kvT, ("x", 4): x_qcT,
                ("a", 2): a_qk, ("x", 5): x_kvn, ("x", 6): x_kr, ("x", 7): x_q, ("a", 3): a_v,
                ("x", 6.5): lambda t: x_qr(t, 0), ("x", 8): lambda t: x_qr(t, 1), ("a", 4): a_s, ("x", 9): lambda t: x_qt(t, 0), ("x", 9.5): lambda t: x_qt(t, 1),
                ("x", 10): lambda t: x_s(t, 0),
                ("a", 5): a_p, ("x", 11): lambda t: x_s(t, 1), ("a", 6): a_o,
                ("x", 12): lambda t: x_p(t, 0), ("b", 1): a_ot, ("x", 13): lambda t: x_o(t, 0),
                ("b", 2): a_y, ("b", 4): r_T, ("b", 5): r_l, ("x", 14): lambda t: x_p(t, 1), ("x", 15): lambda t: x_o(t, 1),
                ("x", 16): lambda t: x_ot(t, 0), ("x", 17): lambda t: x_ot(t, 1), ("y", 18): x_y})

            for u in range(E_ROUND, E_EID):
                e_beat(u)
            pe.wait_ge(S["r_slot"], WAVES * NT)
            m.matmul(bank(5)[0:1, 0:P], eid_col, ident[:, :], start=True, stop=True).then_inc(eid_pe, 1)
            for u in range(E_EID, E_PRE):
                e_beat(u)

            def turn_tokens(g, k, i):
                pe.wait_ge(ld_tok[k], 16 * (i + 1))
                done(pe, "q_xT", g - 1)
                for j in range(QB):
                    tokens = x_blk[k][:, j * D:(j + 1) * D].rearrange("p (n c) -> p c n", c=DC)
                    for c in range(DC):
                        n = DC * j + c
                        last = tr(bank(n // 4)[:, (n % 4) * P:(n % 4 + 1) * P], tokens[:, c, :])
                last.then_inc(S["q_xT_pe"], 1)

            def up_blocks(g, k, i):
                pe.wait_ge(ld_exp[k], 16 * QB * (i + 1))
                done(pe, "q_xT", g)
                done(pe, "q_hid", g - 1)
                for j in range(QB):
                    for c in range(DC):
                        last = m.matmul(bank(2)[:, j * P:(j + 1) * P], xT_q[:, (DC * j + c) * P:(DC * j + c + 1) * P],
                                        w_blk[:, k, j, c * P:(c + 1) * P], start=(c == 0), stop=(c == DC - 1))
                last.then_inc(S["q_up_pe"], 1)

            def down_blocks(g, k):
                done(pe, "q_hT", g)
                done(pe, "q_y", g - 1)
                for j in range(QB):
                    for h in range(2):
                        rows = slice(F * h, F * h + F)
                        last = m.matmul(bank(4 + h)[:, j * P:(j + 1) * P],
                                        hT_q[rows, j * P:(j + 1) * P], w_blk[rows, k, j, 2 * DC * F:],
                                        start=True, stop=True)
                last.then_inc(S["q_down_pe"], 1)

            def turn_block_hidden(g):
                done(pe, "q_hid", g)
                done(pe, "q_hT", g - 1)
                for j in range(QB):
                    last = tr(bank(3)[:, j * P:(j + 1) * P], hid_q[:, j, :, :])
                last.then_inc(S["q_hT_pe"], 1)

            def quad(g, k, i):
                up_blocks(g, k, i)
                if not (isinstance(g, int) and g == NQ - 1):
                    turn_tokens(g + 1, (k + 1) % QBUF, i if k < QBUF - 1 else i + 1)
                if not (isinstance(g, int) and g < 1):
                    down_blocks(g - 1, (k - 1) % QBUF)
                turn_block_hidden(g)
            done(pe, "f_silu", E_PRE - 1)
            done(pe, "f_hid", E_PRE - 1)
            done(pe, "f_acc", E_PRE - 3)
            done(pe, "f_hT", E_PRE - 2)
            pe.wait_ge(eid_ready, 1)
            turn_tokens(0, 0, 0)
            run_quads(pe, quad)
            down_blocks(NQ - 1, QBUF - 1)

            done(pe, "q_xT", NQ - 1)
            done(pe, "q_hid", NQ - 1)
            done(pe, "q_hT", NQ - 1)
            done(pe, "q_y", NQ - 1)
            for u in range(E_PRE, NT):
                e_beat(u)
            down_products(NT - 2)
            turn_hidden(NT - 1)
            down_products(NT - 1)


def rope_tables():
    import numpy as np
    inv = (1.0 / np.float32(10000.0) ** (np.arange(HALF, dtype=np.float32) / np.float32(HALF))).astype(np.float32)
    ang = np.arange(LK, dtype=np.float32)[:, None] * inv
    cos = np.concatenate([np.cos(ang)] * 2, axis=1).astype(np.float32)
    sin = np.concatenate([np.sin(ang)] * 2, axis=1).astype(np.float32)
    keys = np.stack([np.tile(cos.T, (1, BT)), np.tile(sin.T, (1, BT))], axis=1)
    signed = np.concatenate([-sin[:, :HALF], sin[:, HALF:]], axis=1)
    latents = np.stack([np.tile(cos[:LQ], (BT, 1)), np.tile(signed[:LQ], (BT, 1))], axis=1)
    return np.ascontiguousarray(keys), np.ascontiguousarray(latents)


def expert_rows(wg, wu, wd):
    import numpy as np
    ins = np.concatenate([wg.reshape(E, P, DC, F), wu.reshape(E, P, DC, F)], axis=3).reshape(E, P, 2 * DC * F)
    down = wd.reshape(E, F, 2, D // 2).transpose(0, 2, 1, 3).reshape(E, P, D // 2)
    return np.ascontiguousarray(np.concatenate([ins, down], axis=2))


def laid_out(inputs):
    import numpy as np
    a = {n.replace("L0_", ""): np.asarray(v) for n, v in inputs.items()}
    turned = lambda w, width: w.reshape(width, H, HD).transpose(2, 1, 0)
    b_qkv = a["attn_b_qkv"]
    rope_keys, rope_latents = rope_tables()
    return {
        "x": a["x"], "ctx": a["ctx_2048"], "seg": a["itok_BxS_0_1023"].reshape(NT, P).T,
        "w_kvc": a["xattn_W_kvc"], "w_dq": a["xattn_W_dq"], "w_uqT": turned(a["xattn_W_uq"], QC),
        "w_qr": a["xattn_W_qr"],
        "w_ukuvT": np.stack([turned(a["xattn_W_uk"], KVC), turned(a["xattn_W_uv"], KVC)], axis=1),
        "w_kr": a["xattn_W_kr"], "w_o": a["xattn_W_o"],
        "w_qkv_T": a["attn_W_qkv"].T.reshape(DC, P, 3 * D).transpose(1, 0, 2),
        "b_qk": b_qkv[:2 * D].reshape(2 * DC, P).T, "b_v": b_qkv[2 * D:],
        "w_out_T": a["attn_W_out"].T.reshape(HPAIR, 2, SD, D).transpose(0, 2, 1, 3).reshape(P, 2, D),
        "b_out": a["attn_b_out"], "router_w": a["ffn_router_w"], "router_b": a["ffn_router_bias"],
        "experts": expert_rows(a["ffn_wg"], a["ffn_wu"], a["ffn_wd"]),
        "swg": a["ffn_swg"], "swu": a["ffn_swu"], "swd": a["ffn_swd"],
        "rope_keys": rope_keys, "rope_latents": rope_latents}


def kernel(**inputs):
    import numpy as _np
    import concourse.bacc as _bacc
    from concourse import mybir as _mybir
    from concourse.bass_utils import run_bass_kernel_spmd as _run

    nc = _bacc.Bacc("TRN2", target_bir_lowering=False, num_devices=1)
    arrays, args = {}, []
    for name, a in laid_out(inputs).items():
        a = _np.ascontiguousarray(a)
        arrays[f"in_{name}_dram"] = a
        args.append(nc.dram_tensor(f"in_{name}_dram", a.shape, _mybir.dt.from_np(a.dtype), kind="ExternalInput").ap())
    out = nc.dram_tensor("out_0_dram", (NB, LQ, D), _mybir.dt.float32, kind="ExternalOutput").ap()
    rows = [nc.dram_tensor(name, (NBLK * CAP, D), _mybir.dt.float32, kind="Internal").ap()
            for name in ("expert_tokens", "expert_results")]
    build(nc, *args, out, *rows)
    r = _run(nc, [arrays], core_ids=[0])
    return r.results[0]["out_0_dram"]
```
